# Optimizing a Trainium2 kernel written in Bass

```python
import numpy as np
import jax
import jax.numpy as jnp

def _softmax(x, axis=-1):
    return jax.nn.softmax(x, axis=axis)

def _gelu(x):
    return jax.nn.gelu(x, approximate=True)

def _silu(x):
    return jax.nn.silu(x)

def _sigmoid(x):
    return jax.nn.sigmoid(x)

def _layernorm(x, axis=-1, eps=1e-05):
    m = jnp.mean(x, axis=axis, keepdims=True)
    v = jnp.var(x, axis=axis, keepdims=True)
    return (x - m) / jnp.sqrt(v + eps)

def _scatter_add(tgt, idx, src, axis=0):
    return tgt.at[idx].add(src)

def _segment_sum(src, seg, n):
    return jax.ops.segment_sum(src, seg, n)
kernel_name = 'mk_pixart_resid_d2_seqx_r4_ba710d'

def setup_inputs(seed: int=0):
    np.random.seed(seed)
    _w = jnp.asarray

    def _rec_inputs():
        import jax
        import jax.numpy as jnp
        _rk = jax.random.key(seed)
        x = -0.0002928 + 1 * jax.random.normal(jax.random.fold_in(_rk, 1), (8, 112, 256), jnp.float32)
        _lenS = 112 - jax.random.randint(jax.random.fold_in(_rk, 7), (8,), 0, max(1, 112 // 4) + 1, jnp.int32)
        _lenS2 = 375 - jax.random.randint(jax.random.fold_in(_rk, 8), (8,), 0, max(1, 375 // 4) + 1, jnp.int32)
        _ctx_1024P = jax.random.normal(jax.random.fold_in(_rk, 11), (8, 16, 256), jnp.float32)
        _ctx_1024c = jax.random.dirichlet(jax.random.fold_in(_rk, 511), 0.3 * jnp.ones((16,), jnp.float32), (8, 375))
        _ctx_1024t = jnp.einsum('bsk,bkd->bsd', _ctx_1024c, _ctx_1024P)
        _ctx_1024t = _ctx_1024t * jax.lax.rsqrt(jnp.mean(jnp.square(_ctx_1024t)) + 1e-12) * 0.953939
        ctx_1024 = -1.39393e-06 + 0.999914 * (_ctx_1024t + 0.3 * jax.random.normal(jax.random.fold_in(_rk, 611), (8, 375, 256), jnp.float32))
        condB_tau = jax.random.uniform(jax.random.fold_in(_rk, 12), (8,), jnp.float32, 0.0, 1.23395)
        fside_BxS2_0 = -0.00205293 + 0.99739 * jax.random.normal(jax.random.fold_in(_rk, 13), (8, 375), jnp.float32)
        condB_pt = jax.random.uniform(jax.random.fold_in(_rk, 15), (8,), jnp.float32, 0.0, 226.919)
        return (x, ctx_1024, condB_tau, fside_BxS2_0, condB_pt, _lenS2)
    x, ctx_1024, condB_tau, fside_BxS2_0, condB_pt, _lenS2 = _rec_inputs()

    def _L0_xcond_setup():
        import jax, jax.numpy as jnp
        import numpy as np
        B, S, D, H = (2, 512, 256, 16)
        DK = D // H

        def _split_heads(x):
            b, s, _ = x.shape
            return x.reshape(b, s, H, DK).transpose(0, 2, 1, 3)
        key = jax.random.key(seed)
        ks = jax.random.split(key, 14)
        inp = {'query': jax.random.normal(ks[0], (B, S, D), jnp.float32), 'key': jax.random.normal(ks[1], (B, S, D), jnp.float32), 'value': jax.random.normal(ks[2], (B, S, D), jnp.float32), 'tau': jax.random.uniform(ks[3], (B, 1), jnp.float32, 0.5, 1.5), 'delta': jax.random.normal(ks[4], (B, S), jnp.float32)}
        sc = 1.0 / np.sqrt(D)
        for i, name in enumerate(['q', 'k', 'v', 'o']):
            inp[f'W{name}'] = jax.random.normal(ks[5 + 2 * i], (D, D), jnp.float32) * sc
            inp[f'b{name}'] = jax.random.normal(ks[6 + 2 * i], (D,), jnp.float32) * 0.01
        return inp
    _L0_xcond_all = _L0_xcond_setup()
    _L0_xcond_in = {k: v for k, v in _L0_xcond_all.items() if k in ('Wq', 'bq', 'Wk', 'bk', 'Wv', 'bv', 'Wo', 'bo')}
    del _L0_xcond_all

    def _L0_ffn_setup():
        import jax, jax.numpy as jnp
        import numpy as np
        B, S, D_MODEL, D_HIDDEN = (4, 512, 256, 1024)

        def act_quant(x):
            scale = 127.0 / jnp.clip(jnp.max(jnp.abs(x), axis=-1, keepdims=True), 1e-05)
            return jnp.clip(jnp.round(x * scale), -128, 127) / scale

        def weight_quant(w):
            scale = 1.0 / jnp.clip(jnp.mean(jnp.abs(w)), 1e-05)
            return jnp.clip(jnp.round(w * scale), -1, 1) / scale

        def bit_linear(x, w):
            xq = x + jax.lax.stop_gradient(act_quant(x) - x)
            wq = w + jax.lax.stop_gradient(weight_quant(w) - w)
            return jnp.einsum('bsd,hd->bsh', xq, wq)

        def depthwise_conv1d(x_bcl, w, b):
            y = jax.lax.conv_general_dilated(x_bcl, w, window_strides=(1,), padding=[(1, 1)], dimension_numbers=('NCH', 'OIH', 'NCH'), feature_group_count=x_bcl.shape[1])
            return y + b[None, :, None]
        key = jax.random.key(seed)
        ks = jax.random.split(key, 5)
        lim1 = 1.0 / np.sqrt(D_MODEL)
        lim2 = 1.0 / np.sqrt(D_HIDDEN)
        limc = 1.0 / np.sqrt(3.0)
        return {'x': jax.random.normal(ks[0], (B, S, D_MODEL), dtype=jnp.float32), 'w1': jax.random.uniform(ks[1], (D_HIDDEN, D_MODEL), jnp.float32, -lim1, lim1), 'conv_w': jax.random.uniform(ks[2], (D_HIDDEN, 1, 3), jnp.float32, -limc, limc), 'conv_b': jax.random.uniform(ks[3], (D_HIDDEN,), jnp.float32, -limc, limc), 'w2': jax.random.uniform(ks[4], (D_MODEL, D_HIDDEN), jnp.float32, -lim2, lim2)}
    _L0_ffn_all = _L0_ffn_setup()
    _L0_ffn_in = {k: v for k, v in _L0_ffn_all.items() if k in ('w1', 'conv_w', 'conv_b', 'w2')}
    del _L0_ffn_all

    def _L1_xcond_setup():
        import jax, jax.numpy as jnp
        import numpy as np
        N, L, H, Q = (64, 258, 256, 64)
        WINDOW = 16.0
        DEV_POW = 128.0
        key = jax.random.key(seed)
        k1, k2, k3, k4, k5, k6 = jax.random.split(key, 6)
        encoder_outputs = jax.random.normal(k1, (N, L, H), dtype=jnp.float32)
        decoder_h_t = jax.random.normal(k2, (N, Q, H), dtype=jnp.float32)
        src_len = jax.random.randint(k3, (N,), 32, L + 1).astype(jnp.int32)
        p_t = jax.random.uniform(k4, (N,), dtype=jnp.float32) * (src_len.astype(jnp.float32) - 1.0)
        W_a = jax.random.normal(k5, (H, H), dtype=jnp.float32) * (1.0 / np.sqrt(H))
        W_c = jax.random.normal(k6, (H, 2 * H), dtype=jnp.float32) * (1.0 / np.sqrt(2 * H))
        return {'encoder_outputs': encoder_outputs, 'decoder_h_t': decoder_h_t, 'src_len': src_len, 'p_t': p_t, 'W_a': W_a, 'W_c': W_c}
    _L1_xcond_all = _L1_xcond_setup()
    _L1_xcond_in = {k: v for k, v in _L1_xcond_all.items() if k in ('W_a', 'W_c')}
    del _L1_xcond_all

    def _L1_ffn_setup():
        import jax, jax.numpy as jnp
        import numpy as np
        B, S, D, F, E = (4, 512, 256, 1024, 8)
        key = jax.random.key(seed)
        ks = jax.random.split(key, 7)
        s1 = 1.0 / np.sqrt(D)
        s2 = 1.0 / np.sqrt(F)
        x = jax.random.normal(ks[0], (B, S, D), dtype=jnp.float32)
        W1 = jax.random.uniform(ks[1], (E, D, F), jnp.float32, -s1, s1)
        b1 = jax.random.uniform(ks[2], (E, F), jnp.float32, -s1, s1)
        W2 = jax.random.uniform(ks[3], (E, F, D), jnp.float32, -s2, s2)
        b2 = jax.random.uniform(ks[4], (E, D), jnp.float32, -s2, s2)
        Wr = jax.random.uniform(ks[5], (D, E), jnp.float32, -s1, s1)
        br = jax.random.uniform(ks[6], (E,), jnp.float32, -s1, s1)
        return {'x': x, 'W1': W1, 'b1': b1, 'W2': W2, 'b2': b2, 'Wr': Wr, 'br': br}
    _L1_ffn_all = _L1_ffn_setup()
    _L1_ffn_in = {k: v for k, v in _L1_ffn_all.items() if k in ('W1', 'b1', 'W2', 'b2', 'Wr', 'br')}
    del _L1_ffn_all
    return {'x': x, 'ctx_1024': ctx_1024, 'condB_tau': condB_tau, 'fside_BxS2_0': fside_BxS2_0, 'condB_pt': condB_pt, '_lenS2': _lenS2, 'L0_xcond_Wq': _L0_xcond_in['Wq'], 'L0_xcond_bq': _L0_xcond_in['bq'], 'L0_xcond_Wk': _L0_xcond_in['Wk'], 'L0_xcond_bk': _L0_xcond_in['bk'], 'L0_xcond_Wv': _L0_xcond_in['Wv'], 'L0_xcond_bv': _L0_xcond_in['bv'], 'L0_xcond_Wo': _L0_xcond_in['Wo'], 'L0_xcond_bo': _L0_xcond_in['bo'], 'L0_ffn_w1': _L0_ffn_in['w1'], 'L0_ffn_conv_w': _L0_ffn_in['conv_w'], 'L0_ffn_conv_b': _L0_ffn_in['conv_b'], 'L0_ffn_w2': _L0_ffn_in['w2'], 'L1_xcond_W_a': _L1_xcond_in['W_a'], 'L1_xcond_W_c': _L1_xcond_in['W_c'], 'L1_ffn_W1': _L1_ffn_in['W1'], 'L1_ffn_b1': _L1_ffn_in['b1'], 'L1_ffn_W2': _L1_ffn_in['W2'], 'L1_ffn_b2': _L1_ffn_in['b2'], 'L1_ffn_Wr': _L1_ffn_in['Wr'], 'L1_ffn_br': _L1_ffn_in['br']}

def reference(x, ctx_1024, condB_tau, fside_BxS2_0, condB_pt, _lenS2, L0_xcond_Wq, L0_xcond_bq, L0_xcond_Wk, L0_xcond_bk, L0_xcond_Wv, L0_xcond_bv, L0_xcond_Wo, L0_xcond_bo, L0_ffn_w1, L0_ffn_conv_w, L0_ffn_conv_b, L0_ffn_w2, L1_xcond_W_a, L1_xcond_W_c, L1_ffn_W1, L1_ffn_b1, L1_ffn_W2, L1_ffn_b2, L1_ffn_Wr, L1_ffn_br):
    import jax
    import jax.numpy as jnp

    def _L0_xcond_ref(query, key, value, tau, delta, Wq, bq, Wk, bk, Wv, bv, Wo, bo):
        import jax, jax.numpy as jnp
        import numpy as np
        B, S, D, H = (2, 512, 256, 16)
        DK = D // H

        def _split_heads(x):
            b, s, _ = x.shape
            return x.reshape(b, s, H, DK).transpose(0, 2, 1, 3)
        q = _split_heads(query @ Wq.T + bq)
        k = _split_heads(key @ Wk.T + bk)
        v = _split_heads(value @ Wv.T + bv)
        scores = jnp.einsum('bhqd,bhkd->bhqk', q, k)
        scores = scores * tau[:, :, None, None] + delta[:, None, None, :]
        scores = scores / jnp.sqrt(jnp.asarray(DK, scores.dtype))
        p_attn = jax.nn.softmax(scores, axis=-1)
        x = jnp.einsum('bhqk,bhkd->bhqd', p_attn, v)
        x = x.transpose(0, 2, 1, 3).reshape(query.shape[0], -1, H * DK)
        return x @ Wo.T + bo

    def _L0_ffn_ref(x, w1, conv_w, conv_b, w2):
        import jax, jax.numpy as jnp
        import numpy as np
        B, S, D_MODEL, D_HIDDEN = (4, 512, 256, 1024)

        def act_quant(x):
            scale = 127.0 / jnp.clip(jnp.max(jnp.abs(x), axis=-1, keepdims=True), 1e-05)
            return jnp.clip(jnp.round(x * scale), -128, 127) / scale

        def weight_quant(w):
            scale = 1.0 / jnp.clip(jnp.mean(jnp.abs(w)), 1e-05)
            return jnp.clip(jnp.round(w * scale), -1, 1) / scale

        def bit_linear(x, w):
            xq = x + jax.lax.stop_gradient(act_quant(x) - x)
            wq = w + jax.lax.stop_gradient(weight_quant(w) - w)
            return jnp.einsum('bsd,hd->bsh', xq, wq)

        def depthwise_conv1d(x_bcl, w, b):
            y = jax.lax.conv_general_dilated(x_bcl, w, window_strides=(1,), padding=[(1, 1)], dimension_numbers=('NCH', 'OIH', 'NCH'), feature_group_count=x_bcl.shape[1])
            return y + b[None, :, None]
        h = bit_linear(x, w1)
        h = depthwise_conv1d(h.transpose(0, 2, 1), conv_w, conv_b)
        h = h.transpose(0, 2, 1)
        h = jax.nn.silu(h)
        return bit_linear(h, w2)

    def _L1_xcond_ref(encoder_outputs, decoder_h_t, src_len, p_t, W_a, W_c):
        import jax, jax.numpy as jnp
        import numpy as np
        N, L, H, Q = (64, 258, 256, 64)
        WINDOW = 16.0
        DEV_POW = 128.0
        n, l, h = encoder_outputs.shape
        idx = jnp.arange(l, dtype=jnp.float32)
        src_end = src_len.astype(jnp.float32)
        attn_start = jnp.maximum(p_t - WINDOW, 0.0)
        attn_end = jnp.minimum(p_t + WINDOW, src_end)
        mask = (idx[None, :] < attn_start[:, None]) | (idx[None, :] > attn_end[:, None])
        score = jnp.einsum('nqh,hk,nlk->nql', decoder_h_t, W_a, encoder_outputs)
        score = jnp.where(mask[:, None, :], -1000000000.0, score)
        align = jax.nn.softmax(score, axis=2)
        gauss = jnp.exp(-(idx[None, :] - p_t[:, None]) ** 2 / DEV_POW)
        align = align * gauss[:, None, :]
        context = jnp.einsum('nql,nlh->nqh', align, encoder_outputs)
        cat = jnp.concatenate([context, decoder_h_t], axis=2)
        return jnp.tanh(cat @ W_c.T)

    def _L1_ffn_ref(x, W1, b1, W2, b2, Wr, br):
        import jax, jax.numpy as jnp
        import numpy as np
        B, S, D, F, E = (4, 512, 256, 1024, 8)
        b, s, d = x.shape
        e = Wr.shape[1]
        logits = x @ Wr + br
        idx = jnp.argmax(logits, axis=-1)
        probs = jax.nn.softmax(logits, axis=-1)
        gates = jnp.take_along_axis(probs, idx[..., None], axis=-1)[..., 0]
        xf = x.reshape(-1, d)
        idxf = idx.reshape(-1)
        gf = gates.reshape(-1)
        out = jnp.zeros_like(xf)
        for ei in range(e):
            h = jax.nn.gelu(xf @ W1[ei] + b1[ei], approximate=False)
            y = h @ W2[ei] + b2[ei]
            mask = (idxf == ei).astype(xf.dtype)
            out = out + y * (gf * mask)[:, None]
        return out.reshape(b, s, d)
    x = x + _L0_xcond_ref(_layernorm(x, axis=-1), ctx_1024, ctx_1024, condB_tau[:, None], fside_BxS2_0, L0_xcond_Wq, L0_xcond_bq, L0_xcond_Wk, L0_xcond_bk, L0_xcond_Wv, L0_xcond_bv, L0_xcond_Wo, L0_xcond_bo)
    x = x + _L0_ffn_ref(_layernorm(x, axis=-1), L0_ffn_w1, L0_ffn_conv_w, L0_ffn_conv_b, L0_ffn_w2)
    x = x + _L1_xcond_ref(ctx_1024, _layernorm(x, axis=-1), _lenS2, condB_pt, L1_xcond_W_a, L1_xcond_W_c)
    x = x + _L1_ffn_ref(_layernorm(x, axis=-1), L1_ffn_W1, L1_ffn_b1, L1_ffn_W2, L1_ffn_b2, L1_ffn_Wr, L1_ffn_br)
    return x

_drawn_inputs = setup_inputs


def setup_inputs(seed=0):
    import zlib

    import numpy as np

    out = dict(_drawn_inputs(seed))
    spreads = {}
    factors = {'fside_BxS2_0': 3.684,
     'L0_xcond_bq': 34.533,
     'L0_xcond_bk': 64.0,
     'L0_xcond_bv': 4.482,
     'L0_xcond_bo': 5.6,
     'L1_ffn_b1': 8.0,
     'L1_ffn_b2': 8.0,
     'L1_ffn_br': 6.466}
    for name, (base, spread) in spreads.items():
        noise = np.random.default_rng([zlib.crc32(name.encode()), seed]).standard_normal(out[name].shape)
        drawn = base * np.exp(spread * noise) if base else spread * noise
        out[name] = jnp.asarray(drawn.astype(out[name].dtype))
    for name, factor in factors.items():
        out[name] = (out[name] * factor).astype(out[name].dtype)
    return out
```

```python
import concourse.bass as bass
from concourse import mybir
from contextlib import ExitStack


def pixart_block(nc, A, out):
    fp32 = mybir.dt.float32
    bf16 = mybir.dt.bfloat16
    i32 = mybir.dt.int32
    ALU = mybir.AluOpType
    ACT = mybir.ActivationFunctionType
    X = mybir.AxisListType.X

    B, T, D = A["x"].shape
    L = A["ctx_1024"].shape[1]
    NH, DK = 16, 16
    KT = 3
    LT = L // KT
    DC = D // 128
    HM = NH // DC
    HG = 4
    NG = NH // HG
    F0 = A["L0_ffn_w1"].shape[0]
    M0 = F0 // 128
    NE, _, F1 = A["L1_ffn_W1"].shape
    M1 = F1 // 128
    FB = F1 + D
    NT = B * T
    NB = NT // 128 + NE - 1
    TERMS = [(0, 0), (0, 1), (0, 2), (1, 0), (1, 1), (2, 0)]
    KS = 16 * len(TERMS)
    KD = KS + 3
    KX = KD + 3
    MAGIC = 12582912.0
    EPS = 1e-5
    QMAX = 127.0

    ctx = ExitStack()
    with ctx:
        def sb(name, shape, dt=fp32):
            return ctx.enter_context(nc.sbuf_tensor(name, shape, dt))

        def sem(name):
            return ctx.enter_context(nc.semaphore(name))

        def dram(name, shape, dt=fp32):
            return nc.dram_tensor(name, shape, dt).ap()

        d_k = [dram(f"d_k{i}", [DC, 3, 128, L], bf16) for i in range(2)]
        d_q = [dram(f"d_q{i}", [DC, 3, 128, T], bf16) for i in range(2)]
        d_nm = [dram(f"d_nm{i}", [3 * NH, T], bf16) for i in range(2)]
        d_delta = dram("d_delta", [B, 3, L], bf16)
        d_mask = dram("d_mask", [B, 3 * L])
        d_x3 = dram("d_x3", [B, T, D])
        d_xn3 = dram("d_xn3", [B, T, D])
        d_lg = dram("d_lg", [B, T, NE])
        d_eb = dram("d_eb", [3, NE, FB], bf16)
        d_xs = dram("d_xs", [NB * 128, D])
        d_ys = dram("d_ys", [NB * 128, D])

        EW = DC * F1 + M1 * D
        W = sb("W", [128, NE, EW])
        late = W[:, :, :].rearrange("p e n -> p (e n)")
        LATE0 = 3 * EW
        taken = [LATE0]

        def carve(words):
            a = taken[0]
            taken[0] += words
            assert taken[0] <= (NE - 1) * EW
            return late[:, a:a + words]

        kst = [carve(NH * L // 2).bitcast(bf16).rearrange("p (h l) -> p h l", h=NH) for _ in range(2)]
        qst = [carve(NH * T // 2).bitcast(bf16).rearrange("p (h t) -> p h t", h=NH) for _ in range(2)]
        pexp = [carve(KT * HG * T).rearrange("p (k n) -> p k n", k=KT) for _ in range(2)]
        vaug = [carve(KT * NH * 32).rearrange("p (k h c) -> p k h c", k=KT, h=NH) for _ in range(2)]
        kf = carve(DC * L).rearrange("p (m l) -> p m l", m=DC)
        kr = carve(DC * L).rearrange("p (m l) -> p m l", m=DC)
        kt3 = carve(3 * DC * L // 2).bitcast(bf16).rearrange("p (m t l) -> p m t l", t=3, m=DC)

        st3 = W[:, NE - 1, :]
        nat_qkv = st3[:, 0:3 * 512].rearrange("p (w m d) -> p w m d", w=3, m=DC)
        nat_o = st3[:, 1536:2048].rearrange("p (m d) -> p m d", m=DC)
        nat_c = st3[:, 2048:3072].rearrange("p (m d) -> p m d", m=DC)
        nat_op = st3[:, 3072:4096].rearrange("p (m h c) -> p m h c", m=DC, h=NH)
        nat_f = [W[:, 2, i * 2048:(i + 1) * 2048] for i in range(2)]
        qw_a = [W[:, 1, i * 2048:(i + 1) * 2048] for i in range(2)]
        qw_b = [W[:, 0, i * 1024:(i + 1) * 1024].bitcast(bf16) for i in range(2)]
        eb3 = W[0:NE, 0, 2048:2048 + 3 * FB // 2].bitcast(bf16).rearrange("e (t f) -> e t f", t=3)

        WqT = sb("WqT", [128, DC, DC, 128])
        WkT = sb("WkT", [128, DC, DC, 128])
        WvT = sb("WvT", [128, DC, D])
        WoT = sb("WoT", [128, NG, D])
        WcT = sb("WcT", [128, 2 * DC, D])
        Wa = sb("Wa", [128, DC, D])
        Wr = sb("Wr", [128, DC, NE])
        w1T = sb("w1T", [128, DC, F0], bf16)
        w2T = sb("w2T", [128, M0, D], bf16)
        bq = sb("bq", [128, DC])
        bk = sb("bk", [128, DC])
        bv_b = sb("bv_b", [128, D])
        bo_b = sb("bo_b", [T, D])
        br_b = sb("br_b", [T, NE])
        cw = sb("cw", [128, M0, 3])
        cb = sb("cb", [128, M0])
        idf = sb("idf", [128, 128])
        idb = sb("idb", [128, 128], bf16)
        onesf = sb("onesf", [128, 128])
        onesb = sb("onesb", [128, 128], bf16)
        swap = sb("swap", [128, 128])
        expo = sb("expo", [128, 1])
        wsum = sb("wsum", [128, 2])
        wscl = sb("wscl", [128, 2, 2])
        spare = kst[1][0:B].rearrange("p h l -> p (h l)")
        prep8 = spare[:, 0:12 * L].bitcast(fp32).rearrange("p (k l) -> p k l", k=6)
        prepb = spare[:, 12 * L:15 * L].rearrange("p (k l) -> p k l", k=3)
        ebn = pexp[0][0:NE].rearrange("p k n -> p (k n)")[:, 0:FB]
        ebr = pexp[1][0:NE].rearrange("p k n -> p (k n)")[:, 0:FB]
        prepi = sb("prepi", [B, 1], i32)
        prepc = sb("prepc", [B, 5])

        HOLD = 12752
        hold = sb("hold", [128, HOLD])
        used = [0]

        def hb(rows, *dims, dt=fp32):
            n = 1
            for d in dims:
                n *= d
            words = n if dt == fp32 else (n + 1) // 2
            a = used[0]
            used[0] += words
            assert used[0] <= HOLD, used[0]
            v = hold[0:rows, a:a + words]
            if dt != fp32:
                v = v.bitcast(dt)
            if len(dims) == 2:
                v = v.rearrange("p (a b) -> p a b", a=dims[0])
            if len(dims) == 3:
                v = v.rearrange("p (a b c) -> p a b c", a=dims[0], b=dims[1])
            return v

        cx = hb(LT, KT, D)
        cxT = [hb(128, DC, L) for i in range(2)]
        cx_t = hb(LT, KT, D)
        cxT_t = hb(128, DC, L)
        x0 = [hb(T, D) for i in range(2)]
        x0b = [hb(T, D) for i in range(2)]
        xn0 = hb(T, D)
        xn0T = hb(128, DC, T)
        qf = hb(128, DC, T)
        qr = hb(128, DC, T)
        qt3 = hb(128, DC, 3, T, dt=bf16)
        osb = hb(128, HG * T)
        rsm = hb(128, HG * T)
        on = hb(128, NG, T)
        x1 = hb(T, D)
        x2 = hb(T, D)
        x3 = hb(T, D)
        xn = hb(T, D)
        xq = hb(T, D, dt=bf16)
        xqT = hb(128, DC, T, dt=bf16)
        dg = hb(T, T)
        stB = hb(128, T)
        amc = hb(128, T)
        msk = hb(T, 3, L)
        al = hb(T, L)
        alT = hb(LT, KT, T)
        xn2T = hb(128, DC, T)
        tT = hb(128, DC, T)
        cT = hb(128, DC, T)
        thx = hb(T, D)
        zero = rsm[:, 0:D]
        big = W[:, NE - 1, :]
        hs = big[:, 0:M0 * (T + 2)].rearrange("p (m t) -> p m t", m=M0)
        yc = big[:, 1024:1024 + M0 * T].rearrange("p (m t) -> p m t", m=M0)
        th = big[:, 2048:2048 + M0 * T].rearrange("p (m t) -> p m t", m=M0)
        hq = big[:, 3072:3072 + M0 * T // 2].bitcast(bf16).rearrange("p (m t) -> p m t", m=M0)
        scr = big[0:T, 3520:3520 + L]
        used[0] = 0
        xnall = hb(T, B, D)
        yg = xnall
        x3all = hb(T, B, D)
        hx = hb(128, 2, F1)
        hxT = hb(128, 2, M1, 128)
        xsb = hb(128, 4, D)
        xsT = hb(128, 2, DC, 128)
        ysb = hb(128, 2, D)
        selx = hb(3 * NE, NB, 128, dt=bf16)
        lgall, oh, m_d3, m_e3, w8, base = (hb(T, B, NE) for _ in range(6))
        ohb = hb(T, B * NE, dt=bf16)
        cnt = hb(128, B, NE)
        pre = hb(128, B + 1, NE)
        thr, cmp1 = (hb(128, NE, NB - NE + 1) for _ in range(2))
        jix, cmp2 = (hb(128, NB, NE - 1) for _ in range(2))
        nblk, bs = (hb(128, NE) for _ in range(2))
        ebj = hb(128, NB)
        ebi = hb(1, NB).bitcast(i32)
        ecol, ecol2, ecol3 = (hb(3 * NE, 1) for _ in range(3))
        sel = hb(3 * NE, NB)
        ebt = hb(3 * NE, FB, dt=bf16)
        tau = [sb(f"tau{i}", [128, 1]) for i in range(2)]
        mx = sb("mx", [T, NH])
        nr = sb("nr", [T, NH])
        nm = sb("nm", [T, 3, NH], bf16)
        nmT = sb("nmT", [3 * NH, T], bf16)
        lg = sb("lg", [T, NE])
        bst = sb("bst", [T, 4, 6])
        mv = sb("mv", [T, 4, 2])
        ve = sb("ve", [T, 4])
        rstd = sb("rstd", [T, 4])
        tiny = sb("tiny", [T, 16])
        brow = kf[0:1].rearrange("o m l -> o (m l)")[:, 0:2 * D].rearrange("o (w d) -> o w d", w=2)
        bperm = kr[0:1].rearrange("o m l -> o (m l)")[:, 0:2 * D].rearrange("o (w d) -> o w d", w=2)
        mi = sb("mi", [T, B], i32)
        m_g = sb("m_g", [T, 8, B])

        tri = sb("tri", [T, T], bf16)[:, :]

        ps = ctx.enter_context(nc.psum_tensor("ps", [128, 8, 512], fp32))
        pS = [ps[:, i, :] for i in range(2)]
        pT = [ps[:, 2 + i, :] for i in range(2)]
        pO = ps[:, 4, :]
        pAB = ps[:, 5:7, :]
        pC = ps[:, 7, :]
        pCb = pC.bitcast(bf16)
        pOb = pO.bitcast(bf16)

        alT_ps = sem("alT_ps")
        alT_sb = sem("alT_sb")
        al_ready = sem("al_ready")
        amcT_ps = sem("amcT_ps")
        amc_ready = sem("amc_ready")
        bias_loaded = sem("bias_loaded")
        bperm_made = sem("bperm_made")
        c_ps = sem("c_ps")
        c_sb = sem("c_sb")
        cnt_ps = sem("cnt_ps")
        const_loaded = sem("const_loaded")
        cxT_copied = sem("cxT_copied")
        cxT_ps = sem("cxT_ps")
        cxT_sb = sem("cxT_sb")
        cx_loaded = sem("cx_loaded")
        cxt_loaded = sem("cxt_loaded")
        dg2_ps = sem("dg2_ps")
        dg2_ready = sem("dg2_ready")
        dve_step = sem("dve_step")
        e_ready = sem("e_ready")
        eb_loaded = sem("eb_loaded")
        eb_made = sem("eb_made")
        eb_written = sem("eb_written")
        ebt_loaded = sem("ebt_loaded")
        exp_done = sem("exp_done")
        f_ps = sem("f_ps")
        g_made = sem("g_made")
        gauss_made = sem("gauss_made")
        gelu_done = sem("gelu_done")
        h1_ps = sem("h1_ps")
        hT_ps = sem("hT_ps")
        hT_sb = sem("hT_sb")
        h_evac = sem("h_evac")
        h_ps = sem("h_ps")
        hq_ready = sem("hq_ready")
        idents = sem("idents")
        iota_made = sem("iota_made")
        k_evac = sem("k_evac")
        k_ps = sem("k_ps")
        k_written = sem("k_written")
        kh_made = sem("kh_made")
        km_made = sem("km_made")
        kr_made = sem("kr_made")
        kst_loaded = sem("kst_loaded")
        kt3_ready = sem("kt3_ready")
        lg_ready = sem("lg_ready")
        lg_stored = sem("lg_stored")
        m_d = sem("m_d")
        m_e = sem("m_e")
        m_iota = sem("m_iota")
        m_loaded = sem("m_loaded")
        m_oh = sem("m_oh")
        m_slots = sem("m_slots")
        msk_loaded = sem("msk_loaded")
        mx_done = sem("mx_done")
        mx_loaded = sem("mx_loaded")
        nat_loaded = sem("nat_loaded")
        nmT_ps = sem("nmT_ps")
        nmT_sb = sem("nmT_sb")
        nm_loaded = sem("nm_loaded")
        nm_ready = sem("nm_ready")
        nm_written = sem("nm_written")
        o_evac = sem("o_evac")
        on_ready = sem("on_ready")
        ones_made = sem("ones_made")
        op_made = sem("op_made")
        oproj_ps = sem("oproj_ps")
        out_ready = sem("out_ready")
        out_stored = sem("out_stored")
        pads_made = sem("pads_made")
        prep_loaded = sem("prep_loaded")
        prep_made = sem("prep_made")
        pv_ps = sem("pv_ps")
        q_evac = sem("q_evac")
        q_ps = sem("q_ps")
        q_written = sem("q_written")
        qst_loaded = sem("qst_loaded")
        qt3_ready = sem("qt3_ready")
        quant = sem("quant")
        r_ps = sem("r_ps")
        recip_done = sem("recip_done")
        s_ps = sem("s_ps")
        sc_done = sem("sc_done")
        sc_ps = sem("sc_ps")
        scattered = sem("scattered")
        scr_written = sem("scr_written")
        sel_ready = sem("sel_ready")
        st_ps = sem("st_ps")
        sums_ps = sem("sums_ps")
        swap_made = sem("swap_made")
        t_ps = sem("t_ps")
        t_sb = sem("t_sb")
        tau_loaded = sem("tau_loaded")
        th_ready = sem("th_ready")
        thx_ready = sem("thx_ready")
        tr_c = sem("tr_c")
        tr_f = sem("tr_f")
        tr_o = sem("tr_o")
        tr_qkv = sem("tr_qkv")
        tri_made = sem("tri_made")
        v_evac = sem("v_evac")
        v_ps = sem("v_ps")
        vpads_made = sem("vpads_made")
        w_evac = sem("w_evac")
        w_loaded = sem("w_loaded")
        wc_ps = sem("wc_ps")
        wsum_made = sem("wsum_made")
        wsum_ps = sem("wsum_ps")
        x0b_ready = sem("x0b_ready")
        x1_done = sem("x1_done")
        x3_ready = sem("x3_ready")
        x3_stored = sem("x3_stored")
        xT_ps = sem("xT_ps")
        xT_sb = sem("xT_sb")
        x_loaded = sem("x_loaded")
        xn0T_ps = sem("xn0T_ps")
        xn0T_sb = sem("xn0T_sb")
        xn0_ready = sem("xn0_ready")
        xn2T_ps = sem("xn2T_ps")
        xn2T_sb = sem("xn2T_sb")
        xn2_ready = sem("xn2_ready")
        xn3T_ps = sem("xn3T_ps")
        xn3T_sb = sem("xn3T_sb")
        xn3_ready = sem("xn3_ready")
        xn3_stored = sem("xn3_stored")
        xqT_ps = sem("xqT_ps")
        xqT_sb = sem("xqT_sb")
        xq_ready = sem("xq_ready")
        y_ps = sem("y_ps")
        y_ready = sem("y_ready")
        y_sb = sem("y_sb")
        yc_done = sem("yc_done")
        zero_made = sem("zero_made")
        zeroed = sem("zeroed")
        y_stored = [sem(f"y_stored{i}") for i in range(2)]
        xs_loaded = [sem(f"xs_loaded{i}") for i in range(4)]
        gathered = [sem(f"gathered{i}") for i in range(B)]
        ln_in = [sem(f"ln_in{i}") for i in range(4)]
        ln_rstd = [sem(f"ln_rstd{i}") for i in range(4)]

        block = ctx.enter_context(nc.Block())

        @block.sync
        def _(sp):
            def load_rows(b):
                if b >= 1:
                    sp.wait_ge(cxT_ps, b)
                sp.dma_start(cx[:, :, :], A["ctx_1024"][b].rearrange("(k p) d -> p k d", p=LT)).then_inc(cx_loaded, 16)
                if b >= 2:
                    sp.wait_ge(x0b_ready, b - 1)
                if b >= 2:
                    sp.wait_ge(xn0_ready, b - 1)
                sp.dma_start(x0[b % 2][:, :], A["x"][b]).then_inc(x_loaded, 16)
                if b >= 2:
                    sp.wait_ge(q_evac, b - 1)
                sp.dma_start(tau[b % 2][:, :], A["condB_tau"][b:b + 1].partition_broadcast(128)).then_inc(tau_loaded, 16)

            def stack_k(b):
                sp.wait_ge(kt3_ready, b + 1)
                sp.dma_start(d_k[b % 2].rearrange("m t p l -> p (m t) l"), kt3.rearrange("p m t l -> p (m t) l")).then_inc(k_written, 16)
                sp.wait_ge(k_written, 16 * (b + 1))
                if b >= 2:
                    sp.wait_ge(st_ps, 12 * (b - 1))
                src = d_k[b % 2].rearrange("m t (d h) l -> (t d) m (h l)", h=HM)
                for lo, n in ((0, 3), (48, 2), (80, 1)):
                    sp.dma_start(kst[b % 2][lo:lo + 16 * n].rearrange("p (m h) l -> p m (h l)", m=DC), src[0:16 * n]).then_inc(kst_loaded, 16)
                sp.dma_start(kst[b % 2][KS:KD], d_delta[b].unsqueeze(1).to_broadcast([3, NH, L])).then_inc(kst_loaded, 16)

            def stack_q(b):
                sp.wait_ge(qt3_ready, b + 1)
                sp.dma_start(d_q[b % 2].rearrange("m t p l -> p (m t) l"), qt3.rearrange("p m t l -> p (m t) l")).then_inc(q_written, 16)
                sp.wait_ge(q_written, 16 * (b + 1))
                src = d_q[b % 2].rearrange("m t (d h) l -> (t d) m (h l)", h=HM)
                for r, (tq, _) in enumerate(TERMS):
                    sp.dma_start(qst[b % 2][16 * r:16 * r + 16].rearrange("p (m h) l -> p m (h l)", m=DC),
                         src[16 * tq:16 * tq + 16]).then_inc(qst_loaded, 16)

            def stack_max(b):
                sp.wait_ge(nmT_sb, b + 1)
                sp.dma_start(d_nm[b % 2], nmT[:, :]).then_inc(nm_written, 16)
                sp.wait_ge(nm_written, 16 * (b + 1))
                sp.dma_start(qst[b % 2][KD:KX].rearrange("p h t -> p (h t)"), d_nm[b % 2].rearrange("(t h) n -> t (h n)", t=3)).then_inc(nm_loaded, 16)

            def load_tail(b):
                if b >= 1:
                    sp.wait_ge(c_ps, b)
                sp.dma_start(cx_t[:, :, :], A["ctx_1024"][b].rearrange("(k p) d -> p k d", p=LT)).then_inc(cxt_loaded, 16)
                if b >= 1:
                    sp.wait_ge(al_ready, b)
                sp.dma_start(msk[:, :, :], d_mask[b].partition_broadcast(T).rearrange("t (k l) -> t k l", k=3)).then_inc(msk_loaded, 16)

            def store(b):
                sp.wait_ge(x3_ready, b + 1)
                sp.dma_start(d_x3[b], x3[:, :]).then_inc(x3_stored, 16)
                sp.wait_ge(xn3_ready, b + 1)
                sp.dma_start(d_xn3[b], xn[:, :]).then_inc(xn3_stored, 16)
                sp.wait_ge(lg_ready, b + 1)
                sp.dma_start(d_lg[b], lg[:, :]).then_inc(lg_stored, 16)

            for i, n in enumerate(("Wq", "Wk", "Wv")):
                sp.dma_start(nat_qkv[:, i], A[f"L0_xcond_{n}"].rearrange("(m p) d -> p m d", p=128)).then_inc(nat_loaded, 16)
            load_rows(0)
            sp.dma_start(nat_o, A["L0_xcond_Wo"].rearrange("(m p) d -> p m d", p=128)).then_inc(nat_loaded, 16)
            sp.dma_start(nat_c, A["L1_xcond_W_c"].rearrange("(m p) d -> p m d", p=128)).then_inc(nat_loaded, 16)
            sp.dma_start(nat_f[0].rearrange("p (m d) -> p m d", m=M0), A["L0_ffn_w1"].rearrange("(m p) d -> p m d", p=128)).then_inc(nat_loaded, 16)
            sp.dma_start(nat_f[1].rearrange("p (m d) -> p m d", m=DC), A["L0_ffn_w2"].rearrange("(m p) d -> p m d", p=128)).then_inc(nat_loaded, 16)
            sp.dma_start(brow[0:1, 0], A["L0_xcond_bq"].unsqueeze(0)).then_inc(bias_loaded, 16)
            sp.dma_start(brow[0:1, 1], A["L0_xcond_bk"].unsqueeze(0)).then_inc(bias_loaded, 16)
            sp.dma_start(bv_b[:, :], A["L0_xcond_bv"].partition_broadcast(128)).then_inc(const_loaded, 16)
            sp.dma_start(bo_b[:, :], A["L0_xcond_bo"].partition_broadcast(T)).then_inc(const_loaded, 16)
            sp.dma_start(br_b[:, :], A["L1_ffn_br"].partition_broadcast(T)).then_inc(const_loaded, 16)
            sp.dma_start(cw[:, :, :], A["L0_ffn_conv_w"].rearrange("(m p) o j -> p m (o j)", p=128)).then_inc(const_loaded, 16)
            sp.dma_start(cb[:, :], A["L0_ffn_conv_b"].rearrange("(m p) -> p m", p=128),
                         allow_slow_non_contiguous=True).then_inc(const_loaded, 16)
            sp.dma_start(Wa[:, :, :], A["L1_xcond_W_a"].rearrange("(m p) d -> p m d", p=128)).then_inc(const_loaded, 16)
            sp.dma_start(Wr[:, :, :], A["L1_ffn_Wr"].rearrange("(m p) d -> p m d", p=128)).then_inc(const_loaded, 16)
            sp.dma_start(prep8[:, 0, :], A["fside_BxS2_0"]).then_inc(prep_loaded, 16)
            sp.dma_start(prepc[:, 0:1], A["condB_pt"].unsqueeze(1)).then_inc(prep_loaded, 16)
            sp.dma_start(prepi[:, :], A["_lenS2"].unsqueeze(1)).then_inc(prep_loaded, 16)
            sp.dma_start(ebn[:, 0:F1], A["L1_ffn_b1"]).then_inc(eb_loaded, 16)
            sp.dma_start(ebn[:, F1:FB], A["L1_ffn_b2"]).then_inc(eb_loaded, 16)
            sp.wait_ge(prep_made, 1)
            sp.dma_start(d_delta, prepb[:, :, :]).then_inc(scr_written, 16)
            sp.wait_ge(gauss_made, 1)
            sp.dma_start(d_mask, prep8[:, 3:6, :].rearrange("b k l -> b (k l)")).then_inc(scr_written, 16)
            sp.wait_ge(eb_made, 1)
            sp.dma_start(d_eb.rearrange("t e f -> e t f"), eb3).then_inc(eb_written, 16)
            sp.wait_ge(zero_made, 1)
            for j in range(NB):
                sp.dma_start(d_xs[128 * j:128 * j + 128, :], zero).then_inc(zeroed, 16)
            sp.wait_ge(scr_written, 32)
            sp.wait_ge(pads_made, 1)

            for i in range(-1, B + 1):
                proj, att, tail = i + 1, i, i - 1
                if proj < B and proj > 0:
                    load_rows(proj)
                if 0 <= tail:
                    load_tail(tail)
                if 0 <= att < B:
                    stack_max(att)
                if proj < B:
                    stack_k(proj)
                    stack_q(proj)
                if 0 <= tail:
                    store(tail)

            sp.wait_ge(x3_stored, 16 * B)
            sp.wait_ge(xn3_stored, 16 * B)
            sp.wait_ge(lg_stored, 16 * B)
            sp.wait_ge(eb_written, 16)
            sp.dma_start(ebt, d_eb.rearrange("t e f -> (t e) f")).then_inc(ebt_loaded, 16)
            sp.dma_start(lgall, d_lg.rearrange("b t e -> t b e")).then_inc(m_loaded, 16)
            sp.dma_start(xnall, d_xn3.rearrange("b t d -> t b d")).then_inc(mx_loaded, 16)
            sp.dma_start(x3all, d_x3.rearrange("b t d -> t b d")).then_inc(mx_loaded, 16)
            sp.wait_ge(scattered, 16 * B)
            for j in range(NB):
                if j >= 4:
                    sp.wait_ge(xT_ps, j - 3)
                sp.dma_start(xsb[:, j % 4, :], d_xs[128 * j:128 * j + 128, :]).then_inc(xs_loaded[j % 4], 16)
                if j >= 2:
                    if j >= 2:
                        sp.wait_ge(y_sb, j - 1)
                    sp.dma_start(d_ys[128 * (j - 2):128 * (j - 1), :], ysb[:, j % 2, :]).then_inc(y_stored[j % 2], 16)
            for j in range(NB - 2, NB):
                sp.wait_ge(y_sb, j + 1)
                sp.dma_start(d_ys[128 * j:128 * (j + 1), :], ysb[:, j % 2, :]).then_inc(y_stored[j % 2], 16)
            for b in range(B):
                sp.wait_ge(out_ready, b + 1)
                sp.dma_start(out[b], yg[:, b, :]).then_inc(out_stored, 16)
            sp.wait_ge(out_stored, 16 * B)

        @block.tensor
        def _(pe):
            def mm(o, l, r, start, stop):
                return pe.matmul(o, lhsT=l, rhs=r, start=start, stop=stop, skip_group_check=True)

            def tr(o, i, ident):
                n = i.shape[0]
                return pe.transpose(o, i, ident[0:n, 0:n])

            pe.wait_ge(idents, 1)
            pe.wait_ge(nat_loaded, 16 * 7)
            for w in range(3):
                for m in range(DC):
                    for k in range(DC):
                        a = (k * DC + m) * 128
                        last = tr(ps[:, w, a:a + 128], nat_qkv[:, w, m, k * 128:k * 128 + 128], idf)
            last.then_inc(tr_qkv, 1)
            for m in range(DC):
                for k in range(2 * DC):
                    last = tr(ps[:, 3 + k // 2, (k % 2) * D + m * 128:(k % 2) * D + m * 128 + 128],
                              nat_c[:, m, k * 128:k * 128 + 128], idf)
            last.then_inc(tr_c, 1)
            pe.wait_ge(op_made, 1)
            for m in range(DC):
                for g in range(NG):
                    last = tr(ps[:, 5 + g // 2, (g % 2) * D + m * 128:(g % 2) * D + m * 128 + 128],
                              nat_op[:, m, HG * g:HG * g + HG, :].rearrange("p h c -> p (h c)"), idf)
            last.then_inc(tr_o, 1)
            pe.wait_ge(bperm_made, 1)
            for w in range(2):
                for m in range(DC):
                    last = mm(pC[:, 2 * w + m:2 * w + m + 1], bperm[0:1, w, 128 * m:128 * m + 128], onesf[0:1, 0:1],
                              True, True)
            pe.wait_ge(wsum_made, 1)
            mm(pC[:, 8:10], onesf[:, :], wsum[:, :], True, True).then_inc(wsum_ps, 1)
            pe.wait_ge(w_evac, 3)
            pe.wait_ge(quant, 1)
            psb = ps[:, :, :].bitcast(bf16)
            for t in range(M0):
                for k in range(DC):
                    last = tr(psb[:, k, t * 128:t * 128 + 128], qw_b[0][:, t * D + k * 128:t * D + k * 128 + 128], idb)
            last.then_inc(tr_f, 1)
            pe.wait_ge(quant, 2)
            for m in range(DC):
                for t in range(M0):
                    last = tr(psb[:, 2 + t // 4, (t % 4) * D + m * 128:(t % 4) * D + m * 128 + 128],
                              qw_b[1][:, m * F0 + t * 128:m * F0 + t * 128 + 128], idb)
            last.then_inc(tr_f, 1)

            def p_cxT(b):
                if b == 0:
                    pe.wait_ge(w_evac, 5)
                pe.wait_ge(cx_loaded, 16 * (b + 1))
                if b >= 1:
                    pe.wait_ge(q_evac, b)
                if b >= 1:
                    pe.wait_ge(v_evac, b)
                for k in range(DC):
                    for t in range(KT):
                        last = tr(pAB[:, k, LT * t:LT * t + LT], cx[:, t, 128 * k:128 * k + 128], idf)
                last.then_inc(cxT_ps, 1)
                pe.wait_ge(xn0_ready, b + 1)
                for k in range(DC):
                    last = tr(pAB[:, k, 384:384 + T], xn0[:, 128 * k:128 * k + 128], idf)
                last.then_inc(xn0T_ps, 1)

            def p_k(b):
                pe.wait_ge(cxT_sb, b + 1)
                pe.wait_ge(xn0T_sb, b + 1)
                for m in range(DC):
                    for k in range(DC):
                        last = mm(pAB[:, m, 0:L], WkT[:, k, m, :], cxT[b % 2][:, k, :], k == 0, k == DC - 1)
                last.then_inc(k_ps, 1)

            def p_vq(b):
                pe.wait_ge(k_evac, b + 1)
                for t in range(KT):
                    for k in range(DC):
                        last = mm(pAB[0:LT, t // 2, (t % 2) * D:(t % 2) * D + D], cxT[b % 2][:, k, LT * t:LT * t + LT],
                                  WvT[:, k, :], k == 0, k == DC - 1)
                last.then_inc(v_ps, 1)
                for m in range(DC):
                    for k in range(DC):
                        last = mm(pAB[:, 1, D + T * m:D + T * m + T], WqT[:, k, m, :], xn0T[:, k, :], k == 0, k == DC - 1)
                last.then_inc(q_ps, 1)

            def a_scores(b, h):
                if h == 0:
                    pe.wait_ge(kst_loaded, 64 * (b + 1))
                    pe.wait_ge(qst_loaded, 96 * (b + 1))
                if b >= 1 or h >= 2:
                    pe.wait_ge(mx_done, NH * b + h - 1)
                mm(pS[h % 2][0:T, 0:L], qst[b % 2][0:KD, h, :], kst[b % 2][0:KD, h, :], True, True).then_inc(s_ps, 1)

            def a_max(b):
                pe.wait_ge(nm_ready, b + 1)
                if b >= 1:
                    pe.wait_ge(o_evac, b)
                tr(pOb[0:3 * NH, 0:T], nm[:, :, :].rearrange("p t h -> p (t h)"), idb).then_inc(nmT_ps, 1)

            def a_scoresT(b, g):
                if g == 0:
                    pe.wait_ge(nm_loaded, 16 * (b + 1))
                for t in range(KT):
                    n = KT * g + t
                    if b >= 1 or n >= 2:
                        pe.wait_ge(exp_done, KT * NG * b + n - 1)
                    for j in range(HG):
                        last = mm(pT[n % 2][0:LT, T * j:T * j + T], kst[b % 2][0:KX, HG * g + j, LT * t:LT * t + LT],
                                  qst[b % 2][0:KX, HG * g + j, :], True, True)
                    last.then_inc(st_ps, 1)

            def a_pv(b, g):
                if g == 0:
                    pe.wait_ge(v_evac, b + 1)
                    pe.wait_ge(nmT_sb, b + 1)
                pe.wait_ge(exp_done, KT * NG * b + KT * (g + 1))
                for t in range(KT):
                    for j in range(HG):
                        last = mm(pO[32 * j:32 * j + 32, T * g:T * g + T], vaug[b % 2][0:LT, t, HG * g + j, :],
                                  pexp[g % 2][0:LT, t, T * j:T * j + T], t == 0, t == KT - 1)
                last.then_inc(pv_ps, 1)

            def t_sums(b):
                pe.wait_ge(swap_made, 1)
                pe.wait_ge(o_evac, b + 1)
                if b >= 1:
                    pe.wait_ge(lg_ready, b)
                mm(pC[:, 0:HG * T], swap[:, :], osb[:, :], True, True).then_inc(sums_ps, 1)

            def t_oproj(b):
                pe.wait_ge(on_ready, b + 1)
                for g in range(NG):
                    last = mm(pC[0:T, 0:D], on[:, g, :], WoT[:, g, :], g == 0, g == NG - 1)
                last.then_inc(oproj_ps, 1)

            def t_xqT(b):
                pe.wait_ge(xq_ready, b + 1)
                for k in range(DC):
                    tr(pCb[:, T * k:T * k + T], xq[:, 128 * k:128 * k + 128], idb)
                mm(pC[:, 128:128 + T], onesf[0:T, :], dg[:, :], True, True).then_inc(xqT_ps, 1)

            def t_h(b, half):
                pe.wait_ge(xqT_sb, b + 1)
                if b >= 1 or half:
                    pe.wait_ge(h_evac, 2 * b + half)
                for m in range(M0 // 2):
                    for k in range(DC):
                        f = (half * M0 // 2 + m) * 128
                        last = mm(pC[:, T * m:T * m + T], w1T[:, k, f:f + 128], xqT[:, k, :], k == 0, k == DC - 1)
                last.then_inc(h_ps, 1)

            def t_amcT(b):
                pe.wait_ge(amc_ready, b + 1)
                tr(pC[0:T, 0:128], amc[:, :], idf).then_inc(amcT_ps, 1)

            def t_dg2(b):
                pe.wait_ge(dg2_ready, b + 1)
                mm(pC[:, 128:128 + T], onesf[0:T, :], dg[:, :], True, True).then_inc(dg2_ps, 1)

            def t_down(b):
                pe.wait_ge(hq_ready, b + 1)
                for m in range(M0):
                    last = mm(pC[0:T, 0:D], hq[:, m, :], w2T[:, m, :], m == 0, m == M0 - 1)
                last.then_inc(f_ps, 1)

            def t_xn2T(b):
                pe.wait_ge(xn2_ready, b + 1)
                for k in range(DC):
                    last = tr(pC[:, T * k:T * k + T], xn[:, 128 * k:128 * k + 128], idf)
                last.then_inc(xn2T_ps, 1)

            def t_t(b):
                pe.wait_ge(xn2T_sb, b + 1)
                for m in range(DC):
                    for k in range(DC):
                        last = mm(pC[:, T * m:T * m + T], Wa[:, k, 128 * m:128 * m + 128], xn2T[:, k, :], k == 0, k == DC - 1)
                last.then_inc(t_ps, 1)

            def t_sc(b):
                pe.wait_ge(t_sb, b + 1)
                pe.wait_ge(cxT_copied, b + 1)
                for k in range(DC):
                    last = mm(pC[0:T, 0:L], tT[:, k, :], cxT_t[:, k, :], k == 0, k == DC - 1)
                last.then_inc(sc_ps, 1)

            def t_alT(b):
                pe.wait_ge(al_ready, b + 1)
                for t in range(KT):
                    last = tr(pC[0:LT, T * t:T * t + T], al[:, LT * t:LT * t + LT], idf)
                last.then_inc(alT_ps, 1)

            def t_c(b):
                pe.wait_ge(alT_sb, b + 1)
                pe.wait_ge(cxt_loaded, 16 * (b + 1))
                for m in range(DC):
                    for t in range(KT):
                        last = mm(pC[:, T * m:T * m + T], cx_t[:, t, 128 * m:128 * m + 128], alT[:, t, :], t == 0, t == KT - 1)
                last.then_inc(c_ps, 1)

            def t_wc(b):
                pe.wait_ge(c_sb, b + 1)
                for k in range(2 * DC):
                    last = mm(pC[0:T, 0:D], cT[:, k, :] if k < DC else xn2T[:, k - DC, :], WcT[:, k, :],
                              k == 0, k == 2 * DC - 1)
                last.then_inc(wc_ps, 1)

            def t_router(b):
                pe.wait_ge(xn3_ready, b + 1)
                pe.wait_ge(thx_ready, b + 1)
                for k in range(DC):
                    last = tr(pC[:, T * k:T * k + T], xn[:, 128 * k:128 * k + 128], idf)
                last.then_inc(xn3T_ps, 1)
                pe.wait_ge(xn3T_sb, b + 1)
                for k in range(DC):
                    last = mm(pC[0:T, 256:256 + NE], cT[:, k, :], Wr[:, k, :], k == 0, k == DC - 1)
                last.then_inc(r_ps, 1)

            for i in range(-1, B + 1):
                p, a, t = i + 1, i, i - 1
                P, AT, TL = p < B, 0 <= a < B, t >= 0
                if TL: t_sums(t)
                if AT: [a_scores(a, h) for h in range(0, 4)]
                if TL: t_oproj(t)
                if AT: [a_scores(a, h) for h in range(4, 8)]
                if AT: [a_scores(a, h) for h in range(8, 12)]
                if TL: t_xqT(t)
                if AT: [a_scores(a, h) for h in range(12, 16)]
                if TL: t_h(t, 0)
                if AT: a_max(a)
                if TL: t_h(t, 1)
                if P: p_cxT(p)
                if AT: a_scoresT(a, 0)
                if TL: t_amcT(t)
                if P: p_k(p)
                if TL: t_dg2(t)
                if AT: a_scoresT(a, 1)
                if AT: a_pv(a, 0)
                if TL: t_down(t)
                if P: p_vq(p)
                if AT: a_scoresT(a, 2)
                if TL: t_xn2T(t)
                if AT: a_pv(a, 1)
                if TL: t_t(t)
                if AT: a_scoresT(a, 3)
                if TL: t_sc(t)
                if AT: a_pv(a, 2)
                if AT: a_pv(a, 3)
                if TL: t_alT(t)
                if TL: t_c(t)
                if TL: t_wc(t)
                if TL: t_router(t)

            pe.wait_ge(tri_made, 1)
            pe.wait_ge(m_oh, 1)
            pe.wait_ge(lg_ready, B)
            mm(pC[:, 0:64], onesb[0:T, :], ohb, True, True)
            mm(pC[0:T, 64:128], tri[0:T, 0:T], ohb, True, True).then_inc(cnt_ps, 1)
            pe.wait_ge(sel_ready, 1)
            pe.wait_ge(m_slots, 1)
            pe.wait_ge(ebt_loaded, 16)

            def e_xT(j):
                pe.wait_ge(xs_loaded[j % 4], 16 * (j // 4 + 1))
                if j >= 1:
                    pe.wait_ge(xT_sb, j)
                for k in range(DC):
                    last = tr(pC[:, 128 * k:128 * k + 128], xsb[:, j % 4, 128 * k:128 * k + 128], idf)
                last.then_inc(xT_ps, 1)

            def e_up(j, e):
                pe.wait_ge(xT_sb, j + 1)
                if j >= 2:
                    pe.wait_ge(gelu_done, 2 * (j - 1))
                for n in range(F1 // 512):
                    o = ps[:, 2 * (j % 2) + n, :]
                    mm(o, selx[:, j, :], ebt[:, 512 * n:512 * n + 512], True, False)
                    for k in range(DC):
                        last = mm(o, xsT[:, j % 2, k, :], late[:, bass.ds(e * EW + k * F1 + 512 * n, 512)], False, k == DC - 1)
                    last.then_inc(h1_ps, 1)

            def e_hT(j):
                for n in range(2):
                    pe.wait_ge(gelu_done, 2 * j + n + 1)
                    if j >= 1:
                        pe.wait_ge(hT_sb, 2 * (j - 1) + n + 1)
                    for f in range(M1 // 2):
                        g = n * M1 // 2 + f
                        last = tr(pAB[:, n, 128 * f:128 * f + 128], hx[:, j % 2, 128 * g:128 * g + 128], idf)
                    last.then_inc(hT_ps, 1)

            def e_down(j, e):
                if j >= 1:
                    pe.wait_ge(y_sb, j)
                mm(pO[:, 0:D], selx[:, j, :], ebt[:, F1:FB], True, False)
                for f in range(M1):
                    if f % 4 == 0:
                        pe.wait_ge(hT_sb, 2 * j + f // 4 + 1)
                    last = mm(pO[:, 0:D], hxT[:, j % 2, f, :], late[:, bass.ds(e * EW + DC * F1 + f * D, D)], False, f == M1 - 1)
                last.then_inc(y_ps, 1)

            def expert(j):
                return pe.value_load(ebi[0:1, j:j + 1], min_val=0, max_val=NE - 1)

            pe.wait_ge(w_loaded, 16 * 2 * NE)
            e_xT(0)
            cur = expert(0)
            e_up(0, cur)
            for j in range(NB):
                if j + 1 < NB:
                    e_xT(j + 1)
                    nxt = expert(j + 1)
                    e_up(j + 1, nxt)
                e_hT(j)
                e_down(j, cur)
                cur = nxt

        @block.scalar
        def _(act):
            def copy(dst, src):
                return act.activation(dst, src, ACT.Copy)

            def load_expert(e):
                act.dma_start(W[:, e, 0:DC * F1].rearrange("p (k f) -> p k f", k=DC),
                              A["L1_ffn_W1"][e].rearrange("(k p) f -> p k f", p=128)).then_inc(w_loaded, 16)
                act.dma_start(W[:, e, DC * F1:EW].rearrange("p (m d) -> p m d", m=M1),
                              A["L1_ffn_W2"][e].rearrange("(m p) d -> p m d", p=128)).then_inc(w_loaded, 16)

            act.wait_ge(prep_made, 1)
            act.activation(prep8[:, 5, :], prep8[:, 2, :], ACT.Exp, scale=-1.0 / 128.0).then_inc(gauss_made, 1)
            act.wait_ge(tr_qkv, 1)
            for w, dst in ((0, WqT), (1, WkT)):
                for k in range(DC):
                    for m in range(DC):
                        a = (k * DC + m) * 128
                        copy(dst[:, k, m, :].rearrange("p (d h) -> p d h", h=HM),
                             ps[:, w, a:a + 128].rearrange("p (h d) -> p d h", h=HM))
            copy(WvT[:, :, :].rearrange("p k d -> p (k d)"), ps[:, 2, :]).then_inc(w_evac, 1)
            act.wait_ge(tr_c, 1)
            copy(WcT[:, :, :].rearrange("p (a k) d -> p a (k d)", a=2), ps[:, 3:5, :]).then_inc(w_evac, 1)
            act.wait_ge(tr_o, 1)
            copy(WoT[:, :, :].rearrange("p (a k) d -> p a (k d)", a=2), ps[:, 5:7, :]).then_inc(w_evac, 1)
            psb = ps[:, :, :].bitcast(bf16)
            act.wait_ge(tr_f, 1)
            copy(w1T[:, :, :], psb[:, 0:2, :]).then_inc(w_evac, 1)
            act.wait_ge(tr_f, 2)
            copy(w2T[:, :, :].rearrange("p (a m) d -> p a (m d)", a=2), psb[:, 2:4, :]).then_inc(w_evac, 1)

            def p_cxT(b):
                act.wait_ge(xn0T_ps, b + 1)
                if b >= 2:
                    act.wait_ge(v_ps, b - 1)
                if b >= 2:
                    act.wait_ge(cxT_copied, b - 1)
                copy(cxT[b % 2][:, :, :], pAB[:, :, 0:L]).then_inc(cxT_sb, 1)
                if b >= 1:
                    act.wait_ge(q_ps, b)
                copy(xn0T[:, :, :], pAB[:, :, 384:384 + T]).then_inc(xn0T_sb, 1)

            def a_exp(b, g):
                for t in range(KT):
                    n = KT * g + t
                    act.wait_ge(st_ps, KT * NG * b + n + 1)
                    if b >= 1 or g >= 2:
                        act.wait_ge(pv_ps, NG * b + g - 1)
                    act.activation(pexp[g % 2][0:LT, t, :], pT[n % 2][0:LT, 0:HG * T], ACT.Exp).then_inc(exp_done, 1)

            def t_osb(b):
                act.wait_ge(pv_ps, NG * (b + 1))
                if b >= 1:
                    act.wait_ge(on_ready, b)
                copy(osb[:, :], pO[:, 0:HG * T]).then_inc(o_evac, 1)

            def t_xqT(b):
                act.wait_ge(xqT_ps, b + 1)
                if b >= 1:
                    act.wait_ge(h_ps, 2 * b)
                if b >= 1:
                    act.wait_ge(h_evac, 2 * b)
                copy(xqT[:, :, :], pCb[:, 0:DC * T].rearrange("p (k t) -> p k t", k=DC))
                copy(stB[:, :], pC[:, 128:128 + T]).then_inc(xqT_sb, 1)

            def t_tanh(b):
                act.wait_ge(y_ready, b + 1)
                if b >= 1:
                    act.wait_ge(hq_ready, b)
                act.activation(th, yc, ACT.Tanh, scale=0.5).then_inc(th_ready, 1)

            def t_xn2T(b):
                act.wait_ge(xn2T_ps, b + 1)
                if b >= 1:
                    act.wait_ge(wc_ps, b)
                copy(xn2T[:, :, :], pC[:, 0:DC * T].rearrange("p (k t) -> p k t", k=DC)).then_inc(xn2T_sb, 1)

            def t_t(b):
                act.wait_ge(t_ps, b + 1)
                if b >= 1:
                    act.wait_ge(sc_ps, b)
                copy(tT[:, :, :], pC[:, 0:DC * T].rearrange("p (k t) -> p k t", k=DC)).then_inc(t_sb, 1)

            def t_e(b):
                act.wait_ge(sc_done, b + 1)
                if b >= 1:
                    act.wait_ge(al_ready, b)
                act.activation(al[:, :], scr, ACT.Exp, bias=tiny[:, 8:9], accum_out=tiny[:, 9:10]).then_inc(e_ready, 1)

            def t_alT(b):
                act.wait_ge(alT_ps, b + 1)
                if b >= 1:
                    act.wait_ge(c_ps, b)
                copy(alT[:, :, :], pC[0:LT, 0:KT * T].rearrange("p (k t) -> p k t", k=KT)).then_inc(alT_sb, 1)

            def t_c(b):
                act.wait_ge(c_ps, b + 1)
                if b >= 1:
                    act.wait_ge(r_ps, b)
                copy(cT[:, :, :], pC[:, 0:DC * T].rearrange("p (k t) -> p k t", k=DC)).then_inc(c_sb, 1)

            def t_thx(b):
                act.wait_ge(wc_ps, b + 1)
                if b >= 1:
                    act.wait_ge(x3_ready, b)
                act.activation(thx[:, :], pC[0:T, 0:D], ACT.Tanh).then_inc(thx_ready, 1)

            def t_router(b):
                act.wait_ge(xn3T_ps, b + 1)
                copy(cT[:, :, :], pC[:, 0:DC * T].rearrange("p (k t) -> p k t", k=DC)).then_inc(xn3T_sb, 1)

            for i in range(-1, B + 1):
                p, a, t = i + 1, i, i - 1
                P, AT, TL = p < B, 0 <= a < B, t >= 0
                if TL: t_osb(t)
                if TL: t_xqT(t)
                if 1 <= i <= 3:
                    if i == 1:
                        act.wait_ge(w_evac, 5)
                        act.wait_ge(eb_written, 16)
                    load_expert(i - 1)
                if P: p_cxT(p)
                if AT: a_exp(a, 0)
                if TL: t_tanh(t)
                if AT: a_exp(a, 1)
                if AT: a_exp(a, 2)
                if TL: t_xn2T(t)
                if TL: t_t(t)
                if AT: a_exp(a, 3)
                if TL: t_e(t)
                if i == B:
                    act.wait_ge(pv_ps, NG * B)
                    act.wait_ge(nm_loaded, 16 * B)
                    for e in range(3, NE - 1):
                        load_expert(e)
                if TL: t_alT(t)
                if TL: t_c(t)
                if TL: t_thx(t)
                if TL: t_router(t)

            act.wait_ge(lg_ready, B)
            load_expert(NE - 1)
            act.wait_ge(m_d, 1)
            act.activation(m_e3, m_d3, ACT.Exp).then_inc(m_e, 1)
            for j in range(NB):
                for n in range(2):
                    act.wait_ge(h1_ps, 2 * j + n + 1)
                    if j >= 2:
                        act.wait_ge(hT_ps, 2 * (j - 2) + n + 1)
                    act.activation(hx[:, j % 2, 512 * n:512 * n + 512], ps[:, 2 * (j % 2) + n, :], ACT.Gelu)\
                       .then_inc(gelu_done, 1)

        @block.gpsimd
        def _(pool):
            pool.memset(idf[:, :], 0.0)
            pool.memset(idb[:, :], 0.0)
            pool.memset(onesf[:, :], 1.0)
            pool.memset(onesb[:, :], 1.0)
            pool.memset(swap[:, :], 0.0)
            pool.memset(tri, 1.0)
            pool.memset(expo[:, :], -0.5).then_inc(ones_made, 1)
            pool.wait_ge(ones_made, 1)
            for m in (idf, idb):
                last = pool.affine_select(out=m[:, :], in_=m[:, :], compare_op=ALU.not_equal, fill=1.0, base=0,
                                          pattern=[[-1, 128]], channel_multiplier=1)
            last.then_inc(idents, 1)
            v = swap[:, :].rearrange("p (j c) -> p j c", c=32)
            pool.affine_select(out=v, in_=v, compare_op=ALU.not_equal, fill=1.0, base=-16,
                               pattern=[[-32, 4], [0, 32]], channel_multiplier=1).then_inc(swap_made, 1)
            pool.affine_select(out=tri, in_=tri, compare_op=ALU.is_gt, fill=0.0, base=0,
                               pattern=[[1, T]], channel_multiplier=-1).then_inc(tri_made, 1)
            pool.iota(prep8[:, 1, :], [[1, L]], base=0, channel_multiplier=0, allow_small_or_imprecise_dtypes=True)\
                .then_inc(iota_made, 1)
            for n in range(2):
                last = pool.memset(vaug[n][:, :, :, :], 1.0)
            last.then_inc(vpads_made, 1)
            pool.memset(zero, 0.0).then_inc(zero_made, 1)

            def rstd_of(b, which):
                pool.wait_ge(ln_in[which], b + 1)
                pool.tensor_tensor(rstd[:, which:which + 1], ve[:, which:which + 1], expo[0:T, :], ALU.pow)\
                    .then_inc(ln_rstd[which], 1)

            def p_x0b(b):
                pool.wait_ge(x_loaded, 16 * (b + 1))
                if b >= 2:
                    pool.wait_ge(x1_done, b - 1)
                pool.tensor_tensor(x0b[b % 2][:, :], x0[b % 2][:, :], bo_b[:, :], ALU.add).then_inc(x0b_ready, 1)

            def p_k(b):
                pool.wait_ge(k_evac, b + 1)
                if b >= 1:
                    pool.wait_ge(k_written, 16 * b)
                pool.tensor_copy(kt3[:, :, 0, :], kf).then_inc(kh_made, 1)
                pool.wait_ge(kr_made, b + 1)
                pool.tensor_copy(kt3[:, :, 1, :], kr).then_inc(km_made, 1)

            def t_center(b):
                for half in range(2):
                    pool.wait_ge(h_evac, 2 * b + half + 1)
                    if b >= 1:
                        pool.wait_ge(th_ready, b)
                    if b >= 1:
                        pool.wait_ge(g_made, b)
                    for m in range(half * M0 // 2, (half + 1) * M0 // 2):
                        last = pool.tensor_scalar(yc[:, m, :], hs[:, m, 1:1 + T], cw[:, m, 1:2], cb[:, m:m + 1],
                                                  ALU.mult, ALU.add)
                    last.then_inc(yc_done, 1)

            def t_cxT(b):
                pool.wait_ge(cxT_sb, b + 1)
                if b >= 1:
                    pool.wait_ge(sc_ps, b)
                pool.tensor_copy(cxT_t[:, :, :], cxT[b % 2][:, :, :]).then_inc(cxT_copied, 1)

            def t_x3(b):
                pool.wait_ge(thx_ready, b + 1)
                if b >= 1:
                    pool.wait_ge(x3_stored, 16 * b)
                pool.tensor_tensor(x3[:, :], x2[:, :], thx[:, :], ALU.add).then_inc(x3_ready, 1)

            for i in range(-1, B + 1):
                p, a, t = i + 1, i, i - 1
                P, AT, TL = p < B, 0 <= a < B, t >= 0
                if i == -1:
                    pool.wait_ge(const_loaded, 16 * 7)
                if TL: t_cxT(t)
                if TL: rstd_of(t, 1)
                if P: rstd_of(p, 0)
                if P: p_x0b(p)
                if TL: t_center(t)
                if P: p_k(p)
                if TL: rstd_of(t, 2)
                if TL: t_x3(t)
                if TL: rstd_of(t, 3)

            pool.wait_ge(lg_ready, B)
            pool.wait_ge(x3_stored, 16 * B)
            pool.wait_ge(xn3_stored, 16 * B)
            pool.iota(w8, [[0, B], [-1, NE]], base=NE, channel_multiplier=0, allow_small_or_imprecise_dtypes=True)
            pool.iota(thr, [[0, NE], [128, NB - NE + 1]], base=0, channel_multiplier=0, allow_small_or_imprecise_dtypes=True)
            pool.iota(jix, [[1, NB], [0, NE - 1]], base=0, channel_multiplier=0, allow_small_or_imprecise_dtypes=True)
            pool.iota(ecol, [[0, 1]], base=0, channel_multiplier=1, allow_small_or_imprecise_dtypes=True)\
                .then_inc(m_iota, 1)
            pool.wait_ge(m_slots, 1)
            pool.wait_ge(mx_loaded, 32)
            pool.wait_ge(zeroed, 16 * NB)
            for b in range(B):
                pool.indirect_dma_start(d_xs, bass.IndirectOffsetOnAxis(ap=mi[:, b:b + 1], axis=0), xnall[:, b, :], None)\
                    .then_inc(scattered, 16)
            for n in range(2):
                pool.wait_ge(y_stored[n], 16 * (NB // 2))
            for b in range(B):
                pool.indirect_dma_start(yg[:, b, :], None, d_ys, bass.IndirectOffsetOnAxis(ap=mi[:, b:b + 1], axis=0))\
                    .then_inc(gathered[b], 16)

        @block.vector
        def _(dve):
            steps = [0]

            def step(ins):
                steps[0] += 1
                ins.then_inc(dve_step, 1)
                dve.wait_ge(dve_step, steps[0])

            def tt(o, a, b, op):
                return dve.tensor_tensor(o, a, b, op)

            def ts(o, a, s1, s2, op0, op1):
                return dve.tensor_scalar(o, a, s1, s2, op0, op1)

            for n in range(2):
                dve.memset(kst[n][96:128, :, :], 1.0)
                last = dve.memset(qst[n][96:128, :, :], 1.0)
            last.then_inc(pads_made, 1)
            dve.wait_ge(nat_loaded, 16 * 7)
            step(dve.memset(nat_op, 0.0))
            dve.tensor_copy(nat_op[:, :, :, 0:DK], nat_o.rearrange("p m (h c) -> p m h c", c=DK)).then_inc(op_made, 1)
            for i in range(2):
                step(dve.tensor_reduce(wsum[:, i:i + 1], nat_f[i], X, ALU.add, apply_absolute_value=True))
            dve.sem_inc(wsum_made, 1)
            dve.wait_ge(bias_loaded, 32)
            dve.tensor_copy(bperm[0:1, :, :].rearrange("o w (m d h) -> o (w m) d h", m=DC, h=HM),
                            brow[0:1, :, :].rearrange("o w (m h d) -> o (w m) d h", m=DC, h=HM)).then_inc(bperm_made, 1)
            dve.wait_ge(wsum_ps, 1)
            dve.tensor_copy(bq[:, :], pC[:, 0:2])
            dve.tensor_copy(bk[:, :], pC[:, 2:4])
            step(ts(wscl[:, 0, :], pC[:, 8:10], 1.0 / (F0 * D), 1e-5, ALU.mult, ALU.max))
            step(dve.reciprocal(wscl[:, 1, :], wscl[:, 0, :]))
            for i in range(2):
                step(ts(qw_a[i], nat_f[i], wscl[:, 1, i:i + 1], MAGIC, ALU.mult, ALU.add))
                step(ts(qw_a[i], qw_a[i], MAGIC, 1.0, ALU.subtract, ALU.min))
                ts(qw_b[i], qw_a[i], -1.0, None, ALU.max, ALU.bypass).then_inc(quant, 1)
            dve.wait_ge(prep_loaded, 48)
            dve.wait_ge(iota_made, 1)
            step(ts(prep8[:, 2, :], prep8[:, 0, :], 0.25, None, ALU.mult, ALU.bypass))
            step(dve.tensor_copy(prepb[:, 0, :], prep8[:, 2, :]))
            step(tt(prep8[:, 2, :], prep8[:, 2, :], prepb[:, 0, :], ALU.subtract))
            step(dve.tensor_copy(prepb[:, 1, :], prep8[:, 2, :]))
            step(tt(prepb[:, 2, :], prep8[:, 2, :], prepb[:, 1, :], ALU.subtract))
            step(dve.tensor_copy(prepc[:, 1:2], prepi[:, :]))
            step(ts(prepc[:, 2:3], prepc[:, 0:1], 16.0, 0.0, ALU.subtract, ALU.max))
            step(ts(prepc[:, 3:4], prepc[:, 0:1], 16.0, prepc[:, 1:2], ALU.add, ALU.min))
            step(ts(prep8[:, 3, :], prep8[:, 1, :], prepc[:, 2:3], None, ALU.is_ge, ALU.bypass))
            step(dve.scalar_tensor_tensor(prep8[:, 3, :], prep8[:, 1, :], prepc[:, 3:4], prep8[:, 3, :], ALU.is_le, ALU.mult))
            step(ts(prep8[:, 4, :], prep8[:, 3, :], 1.0, 1e9, ALU.subtract, ALU.mult))
            step(ts(prep8[:, 2, :], prep8[:, 1, :], prepc[:, 0:1], None, ALU.subtract, ALU.bypass))
            step(tt(prep8[:, 2, :], prep8[:, 2, :], prep8[:, 2, :], ALU.mult))
            dve.sem_inc(prep_made, 1)
            dve.wait_ge(eb_loaded, 32)
            step(dve.tensor_copy(eb3[:, 0, :], ebn))
            step(tt(ebr, ebn, eb3[:, 0, :], ALU.subtract))
            step(dve.tensor_copy(eb3[:, 1, :], ebr))
            step(tt(eb3[:, 2, :], ebr, eb3[:, 1, :], ALU.subtract))
            dve.sem_inc(eb_made, 1)

            def ln(x, which, b, o):
                step(dve.bn_stats(bst[:, which, :], x))
                step(dve.bn_aggr(mv[:, which, :], bst[:, which, :]))
                ts(ve[:, which:which + 1], mv[:, which, 1:2], EPS, None, ALU.add, ALU.bypass).then_inc(ln_in[which], 1)
                dve.wait_ge(ln_rstd[which], b + 1)
                return ts(o, x, mv[:, which, 0:1], rstd[:, which:which + 1], ALU.subtract, ALU.mult)

            def p_ln(b):
                dve.wait_ge(x_loaded, 16 * (b + 1))
                if b >= 1:
                    dve.wait_ge(xn0T_ps, b)
                ln(x0[b % 2][:, :], 0, b, xn0[:, :]).then_inc(xn0_ready, 1)

            def p_k(b):
                dve.wait_ge(k_ps, b + 1)
                if b >= 1:
                    dve.wait_ge(km_made, b)
                for m in range(DC):
                    last = ts(kf[:, m, :], pAB[:, m, 0:L], bk[:, m:m + 1], 0.25, ALU.add, ALU.mult)
                last.then_inc(k_evac, 1)
                dve.wait_ge(kh_made, b + 1)
                tt(kr, kf, kt3[:, :, 0, :], ALU.subtract).then_inc(kr_made, 1)
                dve.wait_ge(km_made, b + 1)
                tt(kt3[:, :, 2, :], kr, kt3[:, :, 1, :], ALU.subtract).then_inc(kt3_ready, 1)

            def p_vq(b):
                dve.wait_ge(q_ps, b + 1)
                if b == 0:
                    dve.wait_ge(vpads_made, 1)
                if b >= 2:
                    dve.wait_ge(pv_ps, NG * (b - 1))
                for t in range(KT):
                    last = tt(vaug[b % 2][0:LT, t, :, 0:DK],
                              pAB[0:LT, t // 2, (t % 2) * D:(t % 2) * D + D].rearrange("p (h c) -> p h c", c=DK),
                              bv_b[0:LT, :].rearrange("p (h c) -> p h c", c=DK), ALU.add)
                last.then_inc(v_evac, 1)
                dve.wait_ge(tau_loaded, 16 * (b + 1))
                if b >= 1:
                    dve.wait_ge(q_written, 16 * b)
                for m in range(DC):
                    last = ts(qf[:, m, :], pAB[:, 1, D + T * m:D + T * m + T], bq[:, m:m + 1], tau[b % 2][:, 0:1],
                              ALU.add, ALU.mult)
                last.then_inc(q_evac, 1)
                dve.wait_ge(q_evac, b + 1)
                step(dve.tensor_copy(qt3[:, :, 0, :], qf[:, :, :]))
                step(tt(qr[:, :, :], qf[:, :, :], qt3[:, :, 0, :], ALU.subtract))
                step(dve.tensor_copy(qt3[:, :, 1, :], qr[:, :, :]))
                tt(qt3[:, :, 2, :], qr[:, :, :], qt3[:, :, 1, :], ALU.subtract).then_inc(qt3_ready, 1)

            def a_max(b, h):
                dve.wait_ge(s_ps, NH * b + h + 1)
                dve.tensor_reduce(mx[:, h:h + 1], pS[h % 2][0:T, 0:L], X, ALU.max).then_inc(mx_done, 1)

            def a_neg(b):
                dve.wait_ge(mx_done, NH * (b + 1))
                if b >= 1:
                    dve.wait_ge(nmT_ps, b)
                step(ts(nm[:, 0, :], mx[:, :], -1.0, None, ALU.mult, ALU.bypass))
                step(dve.scalar_tensor_tensor(nr[:, :], mx[:, :], -1.0, nm[:, 0, :], ALU.mult, ALU.subtract))
                step(dve.tensor_copy(nm[:, 1, :], nr[:, :]))
                tt(nm[:, 2, :], nr[:, :], nm[:, 1, :], ALU.subtract).then_inc(nm_ready, 1)

            def a_nmT(b):
                dve.wait_ge(nmT_ps, b + 1)
                if b >= 1:
                    dve.wait_ge(nm_written, 16 * b)
                dve.tensor_copy(nmT[:, :], pOb[0:3 * NH, 0:T]).then_inc(nmT_sb, 1)

            def t_norm(b):
                dve.wait_ge(sums_ps, b + 1)
                dve.reciprocal(rsm[:, :], pC[:, 0:HG * T]).then_inc(recip_done, 1)
                dve.wait_ge(recip_done, b + 1)
                if b >= 1:
                    dve.wait_ge(oproj_ps, b)
                tt(on[:, :, :].rearrange("p g t -> p (g t)"), osb[:, :], rsm[:, :], ALU.mult).then_inc(on_ready, 1)

            def quant_scale(am, c0, half, w, b):
                step(ts(tiny[:, c0 + 2:c0 + 3], am, half, 1e-5, ALU.mult, ALU.max))
                step(dve.reciprocal(tiny[:, c0 + 3:c0 + 4], tiny[:, c0 + 2:c0 + 3]))
                ts(tiny[:, c0:c0 + 1], tiny[:, c0 + 3:c0 + 4], QMAX * half, None, ALU.mult, ALU.bypass)
                step(ts(tiny[:, c0 + 1:c0 + 2], tiny[:, c0 + 2:c0 + 3], 1.0 / QMAX, wscl[0:T, 0, w:w + 1], ALU.mult, ALU.mult))

            def t_x1(b):
                dve.wait_ge(oproj_ps, b + 1)
                dve.wait_ge(x0b_ready, b + 1)
                tt(x1[:, :], pC[0:T, 0:D], x0b[b % 2][:, :], ALU.add).then_inc(x1_done, 1)
                dve.wait_ge(x1_done, b + 1)
                if b >= 1:
                    dve.wait_ge(xn3T_ps, b)
                if b >= 1:
                    dve.wait_ge(xn3_stored, 16 * b)
                step(ln(x1[:, :], 1, b, xn[:, :]))
                step(dve.tensor_reduce(tiny[:, 4:5], xn[:, :], X, ALU.max, apply_absolute_value=True))
                quant_scale(tiny[:, 4:5], 0, 1.0, 0, b)
                step(ts(xn[:, :], xn[:, :], tiny[:, 0:1], MAGIC, ALU.mult, ALU.add))
                ts(xq[:, :], xn[:, :], MAGIC, QMAX, ALU.subtract, ALU.min)
                ts(dg[:, :], idf[0:T, 0:T], tiny[:, 1:2], None, ALU.mult, ALU.bypass).then_inc(xq_ready, 1)

            def t_h(b, half):
                dve.wait_ge(xqT_sb, b + 1)
                dve.wait_ge(h_ps, 2 * b + half + 1)
                if b >= 1:
                    dve.wait_ge(yc_done, 2 * b)
                m0 = half * M0 // 2
                tt(hs[:, m0:m0 + M0 // 2, 1:1 + T], pC[:, 0:M0 // 2 * T].rearrange("p (m t) -> p m t", t=T),
                   stB[:, :].unsqueeze(1).to_broadcast([128, M0 // 2, T]), ALU.mult).then_inc(h_evac, 1)

            def t_conv(b):
                dve.wait_ge(h_evac, 2 * b + 2)
                for half in range(2):
                    dve.wait_ge(yc_done, 2 * b + half + 1)
                    for m in range(half * M0 // 2, (half + 1) * M0 // 2):
                        last = dve.scalar_tensor_tensor(yc[:, m, :], hs[:, m, 0:T], cw[:, m, 0:1], yc[:, m, :],
                                                        ALU.mult, ALU.add)
                step(last)
                for m in range(M0):
                    last = dve.scalar_tensor_tensor(yc[:, m, :], hs[:, m, 2:2 + T], cw[:, m, 2:3], yc[:, m, :],
                                                    ALU.mult, ALU.add)
                last.then_inc(y_ready, 1)

            def t_silu(b):
                dve.wait_ge(th_ready, b + 1)
                dve.scalar_tensor_tensor(th, th, 1.0, yc, ALU.add, ALU.mult).then_inc(g_made, 1)
                dve.wait_ge(g_made, b + 1)
                if b >= 1:
                    dve.wait_ge(amcT_ps, b)
                dve.tensor_reduce(amc[:, :], th.rearrange("p m t -> p t m"), X, ALU.max, apply_absolute_value=True)\
                   .then_inc(amc_ready, 1)

            def t_q2(b):
                dve.wait_ge(amcT_ps, b + 1)
                step(dve.tensor_reduce(tiny[:, 5:6], pC[0:T, 0:128], X, ALU.max))
                quant_scale(tiny[:, 5:6], 10, 0.5, 1, b)
                ts(dg[:, :], idf[0:T, 0:T], tiny[:, 10:11], None, ALU.mult, ALU.bypass).then_inc(dg2_ready, 1)
                dve.wait_ge(dg2_ps, b + 1)
                if b >= 1:
                    dve.wait_ge(f_ps, b)
                step(tt(th, th, pC[:, 128:128 + T].unsqueeze(1).to_broadcast([128, M0, T]), ALU.mult))
                ts(hq, th, MAGIC, MAGIC, ALU.add, ALU.subtract).then_inc(hq_ready, 1)

            def t_x2(b):
                dve.wait_ge(f_ps, b + 1)
                if b >= 1:
                    dve.wait_ge(x3_ready, b)
                step(dve.scalar_tensor_tensor(x2[:, :], pC[0:T, 0:D], tiny[:, 11:12], x1[:, :], ALU.mult, ALU.add))
                ln(x2[:, :], 2, b, xn[:, :]).then_inc(xn2_ready, 1)

            def t_sc(b):
                dve.wait_ge(sc_ps, b + 1)
                dve.wait_ge(msk_loaded, 16 * (b + 1))
                if b >= 1:
                    dve.wait_ge(e_ready, b)
                step(tt(scr, pC[0:T, 0:L], msk[:, 0, :], ALU.mult))
                step(tt(scr, scr, msk[:, 1, :], ALU.add))
                step(dve.tensor_reduce(tiny[:, 6:7], scr, X, ALU.max))
                ts(tiny[:, 8:9], tiny[:, 6:7], -1.0, None, ALU.mult, ALU.bypass).then_inc(sc_done, 1)
                dve.wait_ge(e_ready, b + 1)
                step(dve.reciprocal(tiny[:, 7:8], tiny[:, 9:10]))
                if b >= 1:
                    dve.wait_ge(alT_ps, b)
                dve.scalar_tensor_tensor(al[:, :], al[:, :], tiny[:, 7:8], msk[:, 2, :], ALU.mult, ALU.mult)\
                   .then_inc(al_ready, 1)

            def t_x3(b):
                dve.wait_ge(x3_ready, b + 1)
                ln(x3[:, :], 3, b, xn[:, :]).then_inc(xn3_ready, 1)
                dve.wait_ge(r_ps, b + 1)
                if b >= 1:
                    dve.wait_ge(lg_stored, 16 * b)
                tt(lg[:, :], pC[0:T, 256:256 + NE], br_b[:, :], ALU.add).then_inc(lg_ready, 1)

            for i in range(-1, B + 1):
                p, a, t = i + 1, i, i - 1
                P, AT, TL = p < B, 0 <= a < B, t >= 0
                if i == 1:
                    dve.wait_ge(zeroed, 16 * NB)
                if TL: t_norm(t)
                if AT: [a_max(a, h) for h in range(0, 4)]
                if TL: t_x1(t)
                if AT: [a_max(a, h) for h in range(4, 16)]
                if AT: a_neg(a)
                if i == 1:
                    dve.wait_ge(w_evac, 5)
                    dve.memset(hs[:, :, 0:1], 0.0)
                    step(dve.memset(hs[:, :, T + 1:T + 2], 0.0))
                if TL: t_h(t, 0)
                if AT: a_nmT(a)
                if TL: t_h(t, 1)
                if P: p_ln(p)
                if TL: t_conv(t)
                if TL: t_silu(t)
                if P: p_k(p)
                if TL: t_q2(t)
                if TL: t_x2(t)
                if P: p_vq(p)
                if TL: t_sc(t)
                if TL: t_x3(t)

            dve.wait_ge(m_loaded, 16)
            dve.wait_ge(m_iota, 1)

            def bc(x):
                return x.unsqueeze(2).to_broadcast([T, B, NE])

            step(dve.tensor_reduce(m_g[:, 0, :], lgall, X, ALU.max))
            tt(m_d3, lgall, bc(m_g[:, 0, :]), ALU.subtract).then_inc(m_d, 1)
            step(tt(oh, lgall, bc(m_g[:, 0, :]), ALU.is_equal))
            step(tt(oh, oh, w8, ALU.mult))
            step(dve.tensor_reduce(m_g[:, 1, :], oh, X, ALU.max))
            step(tt(oh, oh, bc(m_g[:, 1, :]), ALU.is_equal))
            dve.tensor_copy(ohb, oh.rearrange("p b e -> p (b e)")).then_inc(m_oh, 1)
            dve.wait_ge(m_e, 1)
            step(dve.tensor_reduce(m_g[:, 2, :], m_e3, X, ALU.add))
            step(dve.reciprocal(m_g[:, 3, :], m_g[:, 2, :]))
            dve.wait_ge(cnt_ps, 1)
            step(dve.tensor_copy(cnt, pC[:, 0:64].rearrange("p (b e) -> p b e", e=NE)))
            step(dve.memset(pre[:, 0, :], 0.0))
            for b in range(B):
                step(tt(pre[:, b + 1, :], pre[:, b, :], cnt[:, b, :], ALU.add))
            step(tt(cmp1, pre[:, B, :].unsqueeze(2).to_broadcast([128, NE, NB - NE + 1]), thr, ALU.is_gt))
            step(dve.tensor_reduce(nblk, cmp1, X, ALU.add))
            step(dve.memset(bs[:, 0:1], 0.0))
            for e in range(NE - 1):
                step(tt(bs[:, e + 1:e + 2], bs[:, e:e + 1], nblk[:, e:e + 1], ALU.add))
            step(tt(cmp2, jix, bs[:, 1:NE].unsqueeze(1).to_broadcast([128, NB, NE - 1]), ALU.is_ge))
            step(dve.tensor_reduce(ebj, cmp2, X, ALU.add))
            dve.tensor_copy(ebi[:, :], ebj[0:1, :])
            step(ts(ecol2, ecol, float(NE), float(NE), ALU.is_ge, ALU.mult))
            step(ts(ecol3, ecol, 2.0 * NE, float(NE), ALU.is_ge, ALU.mult))
            step(tt(ecol2, ecol2, ecol3, ALU.add))
            step(tt(ecol2, ecol, ecol2, ALU.subtract))
            step(ts(sel, ebj[0:3 * NE, :], ecol2, None, ALU.is_equal, ALU.bypass))
            dve.tensor_copy(selx[:, :, :], sel.unsqueeze(2).to_broadcast([3 * NE, NB, 128])).then_inc(sel_ready, 1)
            step(dve.scalar_tensor_tensor(base, bs[0:T, :].unsqueeze(1).to_broadcast([T, B, NE]), 128.0, pre[0:T, 0:B, :],
                                          ALU.mult, ALU.add))
            step(tt(base, pC[0:T, 64:128].rearrange("p (b e) -> p b e", e=NE), base, ALU.add))
            step(tt(base, base, oh, ALU.mult))
            step(dve.tensor_reduce(m_g[:, 4, :], base, X, ALU.add))
            dve.tensor_copy(mi[:, :], m_g[:, 4, :]).then_inc(m_slots, 1)

            for j in range(NB):
                if j == 0:
                    dve.wait_ge(xT_ps, 1)
                    dve.tensor_copy(xsT[:, 0], pC[:, 0:D].rearrange("p (k t) -> p k t", k=DC)).then_inc(xT_sb, 1)
                if j + 1 < NB:
                    dve.wait_ge(xT_ps, j + 2)
                    if j >= 1:
                        dve.wait_ge(h1_ps, 2 * j)
                    dve.tensor_copy(xsT[:, (j + 1) % 2], pC[:, 0:D].rearrange("p (k t) -> p k t", k=DC))\
                       .then_inc(xT_sb, 1)
                for n in range(2):
                    dve.wait_ge(hT_ps, 2 * j + n + 1)
                    if j >= 2:
                        dve.wait_ge(y_ps, j - 1)
                    dve.tensor_copy(hxT[:, j % 2, 4 * n:4 * n + 4, :].rearrange("p f t -> p (f t)"), pAB[:, n, :])\
                       .then_inc(hT_sb, 1)
                dve.wait_ge(y_ps, j + 1)
                if j >= 2:
                    dve.wait_ge(y_stored[j % 2], 16 * (j // 2))
                dve.tensor_copy(ysb[:, j % 2, :], pO[:, 0:D]).then_inc(y_sb, 1)
            for b in range(B):
                dve.wait_ge(gathered[b], 16)
                dve.scalar_tensor_tensor(yg[:, b, :], yg[:, b, :], m_g[:, 3, b:b + 1], x3all[:, b, :], ALU.mult, ALU.add)\
                   .then_inc(out_ready, 1)


_INS = ['x', 'ctx_1024', 'condB_tau', 'fside_BxS2_0', 'condB_pt', '_lenS2', 'L0_xcond_Wq', 'L0_xcond_bq', 'L0_xcond_Wk',
        'L0_xcond_bk', 'L0_xcond_Wv', 'L0_xcond_bv', 'L0_xcond_Wo', 'L0_xcond_bo', 'L0_ffn_w1', 'L0_ffn_conv_w',
        'L0_ffn_conv_b', 'L0_ffn_w2', 'L1_xcond_W_a', 'L1_xcond_W_c', 'L1_ffn_W1', 'L1_ffn_b1', 'L1_ffn_W2', 'L1_ffn_b2',
        'L1_ffn_Wr', 'L1_ffn_br']


def kernel(**inputs):
    import numpy as _np
    import concourse.bacc as _bacc
    from concourse import mybir as _mybir
    from concourse.bass_utils import run_bass_kernel_spmd as _run

    nc = _bacc.Bacc("TRN2", target_bir_lowering=False, num_devices=1)
    arrays, aps = {}, {}
    for name in _INS:
        a = _np.ascontiguousarray(inputs[name])
        arrays[f"in_{name}"] = a
        aps[name] = nc.dram_tensor(f"in_{name}", a.shape, _mybir.dt.from_np(a.dtype), kind="ExternalInput").ap()
    out = nc.dram_tensor("out_x", inputs["x"].shape, _mybir.dt.float32, kind="ExternalOutput").ap()
    pixart_block(nc, aps, out)
    r = _run(nc, [arrays], core_ids=[0])
    return r.results[0]["out_x"]
```

```python
import concourse.bass as bass
from concourse import mybir
from contextlib import ExitStack


def pixart_block(nc, A, out):
    fp32 = mybir.dt.float32
    bf16 = mybir.dt.bfloat16
    i32 = mybir.dt.int32
    ALU = mybir.AluOpType
    ACT = mybir.ActivationFunctionType
    X = mybir.AxisListType.X

    B, T, D = A["x"].shape
    L = A["ctx_1024"].shape[1]
    NH, DK = 16, 16
    KT = 3
    LT = L // KT
    DC = D // 128
    HM = NH // DC
    HG = 4
    NG = NH // HG
    F0 = A["L0_ffn_w1"].shape[0]
    M0 = F0 // 128
    NE, _, F1 = A["L1_ffn_W1"].shape
    M1 = F1 // 128
    FB = F1 + D
    NT = B * T
    NB = NT // 128 + NE - 1
    TERMS = [(0, 0), (0, 1), (0, 2), (1, 0), (1, 1), (2, 0)]
    KS = 16 * len(TERMS)
    KD = KS + 3
    KX = KD + 3
    MAGIC = 12582912.0
    EPS = 1e-5
    QMAX = 127.0

    ctx = ExitStack()
    with ctx:
        def sb(name, shape, dt=fp32):
            return ctx.enter_context(nc.sbuf_tensor(name, shape, dt))

        def sem(name):
            return ctx.enter_context(nc.semaphore(name))

        def dram(name, shape, dt=fp32):
            return nc.dram_tensor(name, shape, dt).ap()

        d_k = [dram(f"d_k{i}", [DC, 3, 128, L], bf16) for i in range(2)]
        d_q = [dram(f"d_q{i}", [DC, 3, 128, T], bf16) for i in range(2)]
        d_nm = [dram(f"d_nm{i}", [3 * NH, T], bf16) for i in range(2)]
        d_delta = dram("d_delta", [B, 3, L], bf16)
        d_mask = dram("d_mask", [B, 3 * L])
        d_x3 = dram("d_x3", [B, T, D])
        d_xn3 = dram("d_xn3", [B, T, D])
        d_lg = dram("d_lg", [B, T, NE])
        d_eb = dram("d_eb", [3, NE, FB], bf16)
        d_xs = dram("d_xs", [NB * 128, D])
        d_ys = dram("d_ys", [NB * 128, D])

        EW = DC * F1 + M1 * D
        W = sb("W", [128, NE, EW])
        late = W[:, :, :].rearrange("p e n -> p (e n)")
        LATE0 = 3 * EW
        taken = [LATE0]

        def carve(words):
            a = taken[0]
            taken[0] += words
            assert taken[0] <= (NE - 1) * EW
            return late[:, a:a + words]

        kst = [carve(NH * L // 2).bitcast(bf16).rearrange("p (h l) -> p h l", h=NH) for _ in range(2)]
        qst = [carve(NH * T // 2).bitcast(bf16).rearrange("p (h t) -> p h t", h=NH) for _ in range(2)]
        pexp = [carve(KT * HG * T).rearrange("p (k n) -> p k n", k=KT) for _ in range(2)]
        vaug = [carve(KT * NH * 32).rearrange("p (k h c) -> p k h c", k=KT, h=NH) for _ in range(2)]
        kf = carve(DC * L).rearrange("p (m l) -> p m l", m=DC)
        kr = carve(DC * L).rearrange("p (m l) -> p m l", m=DC)
        kt3 = carve(3 * DC * L // 2).bitcast(bf16).rearrange("p (m t l) -> p m t l", t=3, m=DC)

        st3 = W[:, NE - 1, :]
        nat_qkv = st3[:, 0:3 * 512].rearrange("p (w m d) -> p w m d", w=3, m=DC)
        nat_o = st3[:, 1536:2048].rearrange("p (m d) -> p m d", m=DC)
        nat_c = st3[:, 2048:3072].rearrange("p (m d) -> p m d", m=DC)
        nat_f = [W[:, 2, i * 2048:(i + 1) * 2048] for i in range(2)]
        qw_a = [W[:, 1, i * 2048:(i + 1) * 2048] for i in range(2)]
        qw_b = [W[:, 0, i * 1024:(i + 1) * 1024].bitcast(bf16) for i in range(2)]
        eb3 = W[0:NE, 0, 2048:2048 + 3 * FB // 2].bitcast(bf16).rearrange("e (t f) -> e t f", t=3)

        WqT = sb("WqT", [128, DC, DC, 128])
        WkT = sb("WkT", [128, DC, DC, 128])
        WvT = sb("WvT", [128, DC, D])
        WoT = sb("WoT", [128, DC, D])
        WcT = sb("WcT", [128, 2 * DC, D])
        Wa = sb("Wa", [128, DC, D])
        Wr = sb("Wr", [128, DC, NE])
        w1T = sb("w1T", [128, DC, F0], bf16)
        w2T = sb("w2T", [128, M0, D], bf16)
        bq = sb("bq", [128, DC])
        bk4 = sb("bk4", [128, DC])
        bv_b = sb("bv_b", [128, D])
        bo_b = sb("bo_b", [T, D])
        br_b = sb("br_b", [T, NE])
        cw = sb("cw", [128, M0, 3])
        cb = sb("cb", [128, M0])
        idf = sb("idf", [128, 128])
        idb = sb("idb", [128, 128], bf16)
        onesf = sb("onesf", [128, 128])
        onesb = sb("onesb", [128, 128], bf16)
        expo = sb("expo", [128, 1])
        wsum = sb("wsum", [128, 2])
        wscl = sb("wscl", [128, 2, 2])
        spare = kst[1][0:B].rearrange("p h l -> p (h l)")
        prep8 = spare[:, 0:12 * L].bitcast(fp32).rearrange("p (k l) -> p k l", k=6)
        prepb = spare[:, 12 * L:15 * L].rearrange("p (k l) -> p k l", k=3)
        ebn = pexp[0][0:NE].rearrange("p k n -> p (k n)")[:, 0:FB]
        ebr = pexp[1][0:NE].rearrange("p k n -> p (k n)")[:, 0:FB]
        prepi = sb("prepi", [B, 1], i32)
        prepc = sb("prepc", [B, 5])

        HOLD = 12752
        hold = sb("hold", [128, HOLD])
        used = [0]

        def hb(rows, *dims, dt=fp32):
            n = 1
            for d in dims:
                n *= d
            words = n if dt == fp32 else (n + 1) // 2
            a = used[0]
            used[0] += words
            assert used[0] <= HOLD, used[0]
            v = hold[0:rows, a:a + words]
            if dt != fp32:
                v = v.bitcast(dt)
            if len(dims) == 2:
                v = v.rearrange("p (a b) -> p a b", a=dims[0])
            if len(dims) == 3:
                v = v.rearrange("p (a b c) -> p a b c", a=dims[0], b=dims[1])
            return v

        cx = hb(LT, KT, D)
        cxT = [hb(128, DC, L) for i in range(3)]
        cx_t = hb(LT, KT, D)
        x0 = [hb(T, D) for i in range(2)]
        x0b = [hb(T, D) for i in range(2)]
        xn0 = hb(T, D)
        xn0T = hb(128, DC, T)
        qf = hb(128, DC, T)
        qr = hb(128, DC, T)
        qt3 = hb(128, DC, 3, T, dt=bf16)
        osb = hb(128, HG * T)
        on = hb(T, D)
        onT = hb(128, DC, T)
        x1 = hb(T, D)
        x2 = hb(T, D)
        zero = hb(128, D)
        x3 = zero[0:T, :]
        xn = hb(T, D)
        xm = hb(T, D)
        xq = hb(T, D, dt=bf16)
        xqT = hb(128, DC, T, dt=bf16)
        amc = hb(128, T)
        msk = hb(T, 3, L)
        al = hb(T, L)
        alT = hb(LT, KT, T)
        xn2T = hb(128, DC, T)
        tT = hb(128, DC, T)
        cT = hb(128, DC, T)
        thx = hb(T, D)
        big = W[:, NE - 1, :]
        hs = big[:, 0:M0 * (T + 2)].rearrange("p (m t) -> p m t", m=M0)
        yc = big[:, 1024:1024 + M0 * T].rearrange("p (m t) -> p m t", m=M0)
        th = big[:, 2048:2048 + M0 * T].rearrange("p (m t) -> p m t", m=M0)
        hq = big[:, 3072:3072 + M0 * T // 2].bitcast(bf16).rearrange("p (m t) -> p m t", m=M0)
        scr = big[0:T, 3520:3520 + L]
        stB = big[:, 1920:1920 + T]
        dg = big[0:T, 2944:2944 + T]
        used[0] = 0
        xnall = hb(T, B, D)
        yg = xnall
        x3all = hb(T, B, D)
        hx = hb(128, 2, F1)
        hxT = hb(128, 2, M1, 128)
        xsb = hb(128, 4, D)
        xsT = hb(128, 2, DC, 128)
        ysb = hb(128, 2, D)
        selx = hb(3 * NE, NB, 128, dt=bf16)
        lgall, oh, m_d3, m_e3, w8, base = (hb(T, B, NE) for _ in range(6))
        ohb = hb(T, B * NE, dt=bf16)
        cnt = hb(128, B, NE)
        pre = hb(128, B + 1, NE)
        thr, cmp1 = (hb(128, NE, NB - NE + 1) for _ in range(2))
        jix, cmp2 = (hb(128, NB, NE - 1) for _ in range(2))
        nblk, bs = (hb(128, NE) for _ in range(2))
        ebj = hb(128, NB)
        ebi = hb(1, NB).bitcast(i32)
        ecol, ecol2, ecol3 = (hb(3 * NE, 1) for _ in range(3))
        sel = hb(3 * NE, NB)
        ebt = hb(3 * NE, FB, dt=bf16)
        tau = [sb(f"tau{i}", [128, 1]) for i in range(2)]
        mx = sb("mx", [T, NH])
        rs = sb("rs", [T, NH])
        nr = sb("nr", [T, NH])
        nm = sb("nm", [T, 3, NH], bf16)
        nmT = sb("nmT", [3 * NH, T], bf16)
        lg = sb("lg", [T, NE])
        bst = sb("bst", [T, 4, 6])
        mv = sb("mv", [T, 4, 2])
        ve = sb("ve", [T, 4])
        rstd = sb("rstd", [T, 4])
        tiny = sb("tiny", [T, 16])
        brow = kf[0:1].rearrange("o m l -> o (m l)")[:, 0:2 * D].rearrange("o (w d) -> o w d", w=2)
        bperm = kr[0:1].rearrange("o m l -> o (m l)")[:, 0:2 * D].rearrange("o (w d) -> o w d", w=2)
        mi = sb("mi", [T, B], i32)
        m_g = sb("m_g", [T, 8, B])

        tri = sb("tri", [T, T], bf16)[:, :]

        ps = ctx.enter_context(nc.psum_tensor("ps", [128, 8, 512], fp32))
        pS = [ps[:, i, :] for i in range(3)]
        pU = ps[:, 3, :]
        pO = ps[:, 4, :]
        pAB = ps[:, 5:7, :]
        pC = ps[:, 7, :]
        pCb = pC.bitcast(bf16)
        pOb = pO.bitcast(bf16)

        alT_ps = sem("alT_ps")
        alT_sb = sem("alT_sb")
        al_ready = sem("al_ready")
        amcT_ps = sem("amcT_ps")
        amc_ready = sem("amc_ready")
        bias_loaded = sem("bias_loaded")
        bk4_made = sem("bk4_made")
        bperm_made = sem("bperm_made")
        c_ps = sem("c_ps")
        c_sb = sem("c_sb")
        cnt_ps = sem("cnt_ps")
        const_loaded = sem("const_loaded")
        cxT_ps = sem("cxT_ps")
        cxT_sb = sem("cxT_sb")
        cx_loaded = sem("cx_loaded")
        cxt_loaded = sem("cxt_loaded")
        dg2_ps = sem("dg2_ps")
        dg2_ready = sem("dg2_ready")
        dve_step = sem("dve_step")
        e_ready = sem("e_ready")
        eb_loaded = sem("eb_loaded")
        eb_made = sem("eb_made")
        eb_written = sem("eb_written")
        ebt_loaded = sem("ebt_loaded")
        exp_done = sem("exp_done")
        f_ps = sem("f_ps")
        g_made = sem("g_made")
        gauss_made = sem("gauss_made")
        gelu_done = sem("gelu_done")
        h1_ps = sem("h1_ps")
        hT_ps = sem("hT_ps")
        hT_sb = sem("hT_sb")
        h_evac = sem("h_evac")
        h_ps = sem("h_ps")
        hq_ready = sem("hq_ready")
        idents = sem("idents")
        iota_made = sem("iota_made")
        k_evac = sem("k_evac")
        k_ps = sem("k_ps")
        k_written = sem("k_written")
        kh_made = sem("kh_made")
        km_made = sem("km_made")
        kr_made = sem("kr_made")
        kst_loaded = sem("kst_loaded")
        kt3_ready = sem("kt3_ready")
        lg_ready = sem("lg_ready")
        lg_stored = sem("lg_stored")
        m_d = sem("m_d")
        m_e = sem("m_e")
        m_iota = sem("m_iota")
        m_loaded = sem("m_loaded")
        m_oh = sem("m_oh")
        m_slots = sem("m_slots")
        msk_loaded = sem("msk_loaded")
        mx_done = sem("mx_done")
        mx_loaded = sem("mx_loaded")
        nat_loaded = sem("nat_loaded")
        nmT_ps = sem("nmT_ps")
        nmT_sb = sem("nmT_sb")
        nm_loaded = sem("nm_loaded")
        nm_ready = sem("nm_ready")
        nm_written = sem("nm_written")
        o_evac = sem("o_evac")
        on_ready = sem("on_ready")
        ones_made = sem("ones_made")
        oT_ps = sem("oT_ps")
        onT_ps = sem("onT_ps")
        onT_sb = sem("onT_sb")
        oproj_ps = sem("oproj_ps")
        recip_done = sem("recip_done")
        out_ready = sem("out_ready")
        out_stored = sem("out_stored")
        pads_made = sem("pads_made")
        prep_loaded = sem("prep_loaded")
        prep_made = sem("prep_made")
        pv_ps = sem("pv_ps")
        q_evac = sem("q_evac")
        q_ps = sem("q_ps")
        q_written = sem("q_written")
        qst_loaded = sem("qst_loaded")
        qt3_ready = sem("qt3_ready")
        quant = sem("quant")
        r_ps = sem("r_ps")
        s_ps = sem("s_ps")
        sc_done = sem("sc_done")
        sc_ps = sem("sc_ps")
        scattered = sem("scattered")
        scr_written = sem("scr_written")
        sel_ready = sem("sel_ready")
        st_ps = sem("st_ps")
        t_ps = sem("t_ps")
        t_sb = sem("t_sb")
        tau_loaded = sem("tau_loaded")
        th_ready = sem("th_ready")
        thx_ready = sem("thx_ready")
        tr_c = sem("tr_c")
        tr_f = sem("tr_f")
        tr_o = sem("tr_o")
        tr_qkv = sem("tr_qkv")
        tri_made = sem("tri_made")
        v_evac = sem("v_evac")
        v_ps = sem("v_ps")
        vpads_made = sem("vpads_made")
        w_evac = sem("w_evac")
        w_loaded = sem("w_loaded")
        wc_ps = sem("wc_ps")
        wsum_made = sem("wsum_made")
        wsum_ps = sem("wsum_ps")
        x0b_ready = sem("x0b_ready")
        x1_done = sem("x1_done")
        x2_ready = sem("x2_ready")
        x3_ready = sem("x3_ready")
        x3_stored = sem("x3_stored")
        xT_ps = sem("xT_ps")
        xT_sb = sem("xT_sb")
        x_loaded = sem("x_loaded")
        xn0T_ps = sem("xn0T_ps")
        xn0T_sb = sem("xn0T_sb")
        xn0_ready = sem("xn0_ready")
        xn2T_ps = sem("xn2T_ps")
        xn2T_sb = sem("xn2T_sb")
        xn2_ready = sem("xn2_ready")
        xn3T_ps = sem("xn3T_ps")
        xn3T_sb = sem("xn3T_sb")
        xn3_ready = sem("xn3_ready")
        xn3_stored = sem("xn3_stored")
        xqT_ps = sem("xqT_ps")
        xqT_sb = sem("xqT_sb")
        xq_ready = sem("xq_ready")
        y_ps = sem("y_ps")
        y_ready = sem("y_ready")
        y_sb = sem("y_sb")
        yc_done = sem("yc_done")
        zero_made = sem("zero_made")
        zeroed = sem("zeroed")
        y_stored = [sem(f"y_stored{i}") for i in range(2)]
        xs_loaded = [sem(f"xs_loaded{i}") for i in range(4)]
        gathered = [sem(f"gathered{i}") for i in range(B)]
        ln_in = [sem(f"ln_in{i}") for i in range(4)]
        ln_rstd = [sem(f"ln_rstd{i}") for i in range(4)]

        block = ctx.enter_context(nc.Block())

        def batch(f):
            def stage(b, *part):
                if 0 <= b < B:
                    f(b, *part)
            return stage


        @block.sync
        def _(sp):
            @batch
            def p_rows(b):
                if b >= 1:
                    sp.wait_ge(cxT_ps, b)
                sp.dma_start(cx[:, :, :], A["ctx_1024"][b].rearrange("(k p) d -> p k d", p=LT)).then_inc(cx_loaded, 16)
                if b >= 2:
                    sp.wait_ge(x0b_ready, b - 1)
                if b >= 2:
                    sp.wait_ge(xn0_ready, b - 1)
                sp.dma_start(x0[b % 2][:, :], A["x"][b]).then_inc(x_loaded, 16)
                if b >= 2:
                    sp.wait_ge(q_evac, b - 1)
                sp.dma_start(tau[b % 2][:, :], A["condB_tau"][b:b + 1].partition_broadcast(128)).then_inc(tau_loaded, 16)

            @batch
            def p_stackk(b):
                sp.wait_ge(kt3_ready, b + 1)
                sp.dma_start(d_k[b % 2].rearrange("m t p l -> p (m t) l"), kt3.rearrange("p m t l -> p (m t) l")).then_inc(k_written, 16)
                sp.wait_ge(k_written, 16 * (b + 1))
                if b >= 2:
                    sp.wait_ge(st_ps, 12 * (b - 1))
                src = d_k[b % 2].rearrange("m t (d h) l -> (t d) m (h l)", h=HM)
                for lo, n in ((0, 3), (48, 2), (80, 1)):
                    sp.dma_start(kst[b % 2][lo:lo + 16 * n].rearrange("p (m h) l -> p m (h l)", m=DC), src[0:16 * n]).then_inc(kst_loaded, 16)
                sp.dma_start(kst[b % 2][KS:KD], d_delta[b].unsqueeze(1).to_broadcast([3, NH, L])).then_inc(kst_loaded, 16)

            @batch
            def p_stackq(b):
                sp.wait_ge(qt3_ready, b + 1)
                sp.dma_start(d_q[b % 2].rearrange("m t p l -> p (m t) l"), qt3.rearrange("p m t l -> p (m t) l")).then_inc(q_written, 16)
                sp.wait_ge(q_written, 16 * (b + 1))
                src = d_q[b % 2].rearrange("m t (d h) l -> (t d) m (h l)", h=HM)
                for r, (tq, _) in enumerate(TERMS):
                    sp.dma_start(qst[b % 2][16 * r:16 * r + 16].rearrange("p (m h) l -> p m (h l)", m=DC),
                         src[16 * tq:16 * tq + 16]).then_inc(qst_loaded, 16)

            @batch
            def a_stack(b):
                sp.wait_ge(nmT_sb, b + 1)
                sp.dma_start(d_nm[b % 2], nmT[:, :]).then_inc(nm_written, 16)
                sp.wait_ge(nm_written, 16 * (b + 1))
                sp.dma_start(qst[b % 2][KD:KX].rearrange("p h t -> p (h t)"), d_nm[b % 2].rearrange("(t h) n -> t (h n)", t=3)).then_inc(nm_loaded, 16)

            @batch
            def u_cx(b):
                if b >= 1:
                    sp.wait_ge(c_ps, b)
                sp.dma_start(cx_t[:, :, :], A["ctx_1024"][b].rearrange("(k p) d -> p k d", p=LT)).then_inc(cxt_loaded, 16)

            @batch
            def u_mask(b):
                if b >= 1:
                    sp.wait_ge(al_ready, b)
                sp.dma_start(msk[:, :, :], d_mask[b].partition_broadcast(T).rearrange("t (k l) -> t k l", k=3)).then_inc(msk_loaded, 16)

            @batch
            def u_store(b):
                sp.wait_ge(x3_ready, b + 1)
                sp.dma_start(d_x3[b], x3).then_inc(x3_stored, 16)
                sp.wait_ge(xn3_ready, b + 1)
                sp.dma_start(d_xn3[b], xm[:, :]).then_inc(xn3_stored, 16)
                sp.wait_ge(lg_ready, b + 1)
                sp.dma_start(d_lg[b], lg[:, :]).then_inc(lg_stored, 16)

            for i, n in enumerate(("Wq", "Wk", "Wv")):
                sp.dma_start(nat_qkv[:, i], A[f"L0_xcond_{n}"].rearrange("(m p) d -> p m d", p=128)).then_inc(nat_loaded, 16)
            p_rows(0)
            sp.dma_start(nat_o, A["L0_xcond_Wo"].rearrange("(m p) d -> p m d", p=128)).then_inc(nat_loaded, 16)
            sp.dma_start(nat_c, A["L1_xcond_W_c"].rearrange("(m p) d -> p m d", p=128)).then_inc(nat_loaded, 16)
            sp.dma_start(nat_f[0].rearrange("p (m d) -> p m d", m=M0), A["L0_ffn_w1"].rearrange("(m p) d -> p m d", p=128)).then_inc(nat_loaded, 16)
            sp.dma_start(nat_f[1].rearrange("p (m d) -> p m d", m=DC), A["L0_ffn_w2"].rearrange("(m p) d -> p m d", p=128)).then_inc(nat_loaded, 16)
            sp.dma_start(brow[0:1, 0], A["L0_xcond_bq"].unsqueeze(0)).then_inc(bias_loaded, 16)
            sp.dma_start(brow[0:1, 1], A["L0_xcond_bk"].unsqueeze(0)).then_inc(bias_loaded, 16)
            sp.dma_start(bv_b[:, :], A["L0_xcond_bv"].partition_broadcast(128)).then_inc(const_loaded, 16)
            sp.dma_start(bo_b[:, :], A["L0_xcond_bo"].partition_broadcast(T)).then_inc(const_loaded, 16)
            sp.dma_start(br_b[:, :], A["L1_ffn_br"].partition_broadcast(T)).then_inc(const_loaded, 16)
            sp.dma_start(cw[:, :, :], A["L0_ffn_conv_w"].rearrange("(m p) o j -> p m (o j)", p=128)).then_inc(const_loaded, 16)
            sp.dma_start(cb[:, :], A["L0_ffn_conv_b"].rearrange("(m p) -> p m", p=128),
                         allow_slow_non_contiguous=True).then_inc(const_loaded, 16)
            sp.dma_start(Wa[:, :, :], A["L1_xcond_W_a"].rearrange("(m p) d -> p m d", p=128)).then_inc(const_loaded, 16)
            sp.dma_start(Wr[:, :, :], A["L1_ffn_Wr"].rearrange("(m p) d -> p m d", p=128)).then_inc(const_loaded, 16)
            sp.dma_start(prep8[:, 0, :], A["fside_BxS2_0"]).then_inc(prep_loaded, 16)
            sp.dma_start(prepc[:, 0:1], A["condB_pt"].unsqueeze(1)).then_inc(prep_loaded, 16)
            sp.dma_start(prepi[:, :], A["_lenS2"].unsqueeze(1)).then_inc(prep_loaded, 16)
            sp.dma_start(ebn[:, 0:F1], A["L1_ffn_b1"]).then_inc(eb_loaded, 16)
            sp.dma_start(ebn[:, F1:FB], A["L1_ffn_b2"]).then_inc(eb_loaded, 16)
            sp.wait_ge(prep_made, 1)
            sp.dma_start(d_delta, prepb[:, :, :]).then_inc(scr_written, 16)
            sp.wait_ge(gauss_made, 1)
            sp.dma_start(d_mask, prep8[:, 3:6, :].rearrange("b k l -> b (k l)")).then_inc(scr_written, 16)
            sp.wait_ge(eb_made, 1)
            sp.dma_start(d_eb.rearrange("t e f -> e t f"), eb3).then_inc(eb_written, 16)
            sp.wait_ge(zero_made, 1)
            for j in range(NB):
                sp.dma_start(d_xs[128 * j:128 * j + 128, :], zero).then_inc(zeroed, 16)
            sp.wait_ge(scr_written, 32)
            sp.wait_ge(pads_made, 1)

            for i in range(-1, B + 2):
                u_cx(i - 2)
                u_mask(i - 2)
                a_stack(i)
                p_rows(i + 2)
                p_stackk(i + 1)
                p_stackq(i + 1)
                u_store(i - 2)
            sp.wait_ge(x3_stored, 16 * B)
            sp.wait_ge(xn3_stored, 16 * B)
            sp.wait_ge(lg_stored, 16 * B)
            sp.wait_ge(eb_written, 16)
            sp.dma_start(ebt, d_eb.rearrange("t e f -> (t e) f")).then_inc(ebt_loaded, 16)
            sp.dma_start(lgall, d_lg.rearrange("b t e -> t b e")).then_inc(m_loaded, 16)
            sp.dma_start(xnall, d_xn3.rearrange("b t d -> t b d")).then_inc(mx_loaded, 16)
            sp.dma_start(x3all, d_x3.rearrange("b t d -> t b d")).then_inc(mx_loaded, 16)
            sp.wait_ge(scattered, 16 * B)
            for j in range(NB):
                if j >= 4:
                    sp.wait_ge(xT_ps, j - 3)
                sp.dma_start(xsb[:, j % 4, :], d_xs[128 * j:128 * j + 128, :]).then_inc(xs_loaded[j % 4], 16)
                if j >= 2:
                    if j >= 2:
                        sp.wait_ge(y_sb, j - 1)
                    sp.dma_start(d_ys[128 * (j - 2):128 * (j - 1), :], ysb[:, j % 2, :]).then_inc(y_stored[j % 2], 16)
            for j in range(NB - 2, NB):
                sp.wait_ge(y_sb, j + 1)
                sp.dma_start(d_ys[128 * j:128 * (j + 1), :], ysb[:, j % 2, :]).then_inc(y_stored[j % 2], 16)
            for b in range(B):
                sp.wait_ge(out_ready, b + 1)
                sp.dma_start(out[b], yg[:, b, :]).then_inc(out_stored, 16)
            sp.wait_ge(out_stored, 16 * B)

        @block.tensor
        def _(pe):
            def mm(o, l, r, start, stop):
                return pe.matmul(o, lhsT=l, rhs=r, start=start, stop=stop, skip_group_check=True)

            def tr(o, i, ident):
                n = i.shape[0]
                return pe.transpose(o, i, ident[0:n, 0:n])

            pe.wait_ge(idents, 1)
            pe.wait_ge(nat_loaded, 16 * 7)
            for w in range(3):
                for m in range(DC):
                    for k in range(DC):
                        a = (k * DC + m) * 128
                        last = tr(ps[:, w, a:a + 128], nat_qkv[:, w, m, k * 128:k * 128 + 128], idf)
            last.then_inc(tr_qkv, 1)
            for m in range(DC):
                for k in range(2 * DC):
                    last = tr(ps[:, 3 + k // 2, (k % 2) * D + m * 128:(k % 2) * D + m * 128 + 128],
                              nat_c[:, m, k * 128:k * 128 + 128], idf)
            last.then_inc(tr_c, 1)
            for m in range(DC):
                for k in range(DC):
                    last = tr(ps[:, 5, k * D + m * 128:k * D + m * 128 + 128], nat_o[:, m, k * 128:k * 128 + 128], idf)
            last.then_inc(tr_o, 1)
            pe.wait_ge(bperm_made, 1)
            for w in range(2):
                for m in range(DC):
                    last = mm(pC[:, 2 * w + m:2 * w + m + 1], bperm[0:1, w, 128 * m:128 * m + 128], onesf[0:1, 0:1],
                              True, True)
            pe.wait_ge(wsum_made, 1)
            mm(pC[:, 8:10], onesf[:, :], wsum[:, :], True, True).then_inc(wsum_ps, 1)
            pe.wait_ge(w_evac, 3)
            pe.wait_ge(quant, 1)
            psb = ps[:, :, :].bitcast(bf16)
            for t in range(M0):
                for k in range(DC):
                    last = tr(psb[:, k, t * 128:t * 128 + 128], qw_b[0][:, t * D + k * 128:t * D + k * 128 + 128], idb)
            last.then_inc(tr_f, 1)
            pe.wait_ge(quant, 2)
            for m in range(DC):
                for t in range(M0):
                    last = tr(psb[:, 2 + t // 4, (t % 4) * D + m * 128:(t % 4) * D + m * 128 + 128],
                              qw_b[1][:, m * F0 + t * 128:m * F0 + t * 128 + 128], idb)
            last.then_inc(tr_f, 1)

            @batch
            def p_cxT(b):
                if b == 0:
                    pe.wait_ge(w_evac, 5)
                pe.wait_ge(cx_loaded, 16 * (b + 1))
                if b >= 1:
                    pe.wait_ge(q_evac, b)
                if b >= 1:
                    pe.wait_ge(v_evac, b)
                for k in range(DC):
                    for t in range(KT):
                        last = tr(pAB[:, k, LT * t:LT * t + LT], cx[:, t, 128 * k:128 * k + 128], idf)
                last.then_inc(cxT_ps, 1)
                pe.wait_ge(xn0_ready, b + 1)
                for k in range(DC):
                    last = tr(pAB[:, k, 384:384 + T], xn0[:, 128 * k:128 * k + 128], idf)
                last.then_inc(xn0T_ps, 1)

            @batch
            def p_k(b):
                pe.wait_ge(cxT_sb, b + 1)
                pe.wait_ge(xn0T_sb, b + 1)
                for m in range(DC):
                    for k in range(DC):
                        last = mm(pAB[:, m, 0:L], WkT[:, k, m, :], cxT[b % 3][:, k, :], k == 0, k == DC - 1)
                last.then_inc(k_ps, 1)

            @batch
            def p_vq(b):
                pe.wait_ge(k_evac, b + 1)
                for t in range(KT):
                    for k in range(DC):
                        last = mm(pAB[0:LT, t // 2, (t % 2) * D:(t % 2) * D + D], cxT[b % 3][:, k, LT * t:LT * t + LT],
                                  WvT[:, k, :], k == 0, k == DC - 1)
                last.then_inc(v_ps, 1)
                for m in range(DC):
                    for k in range(DC):
                        last = mm(pAB[:, 1, D + T * m:D + T * m + T], WqT[:, k, m, :], xn0T[:, k, :], k == 0, k == DC - 1)
                last.then_inc(q_ps, 1)

            @batch
            def a_scores(b, h):
                if h == 0:
                    pe.wait_ge(kst_loaded, 64 * (b + 1))
                    pe.wait_ge(qst_loaded, 96 * (b + 1))
                if b >= 1 and h < 3:
                    pe.wait_ge(exp_done, KT * NG * b - 2 + h)
                if h >= 3:
                    pe.wait_ge(mx_done, NH * b + h - 2)
                mm(pS[h % 3][0:T, 0:L], qst[b % 2][0:KD, h, :], kst[b % 2][0:KD, h, :], True, True).then_inc(s_ps, 1)

            @batch
            def a_max(b):
                pe.wait_ge(nm_ready, b + 1)
                if b >= 1:
                    pe.wait_ge(o_evac, b)
                tr(pOb[0:3 * NH, 0:T], nm[:, :, :].rearrange("p t h -> p (t h)"), idb).then_inc(nmT_ps, 1)

            @batch
            def a_scoresT(b, g):
                if g == 0:
                    pe.wait_ge(nm_loaded, 16 * (b + 1))
                for t in range(KT):
                    n = KT * g + t
                    if n >= 3:
                        pe.wait_ge(exp_done, KT * NG * b + n - 2)
                    for j in range(HG):
                        last = mm(pS[n % 3][0:LT, T * j:T * j + T], kst[b % 2][0:KX, HG * g + j, LT * t:LT * t + LT],
                                  qst[b % 2][0:KX, HG * g + j, :], True, True)
                    last.then_inc(st_ps, 1)

            @batch
            def a_pv(b, g):
                if g == 0:
                    pe.wait_ge(v_evac, b + 1)
                    pe.wait_ge(nmT_sb, b + 1)
                pe.wait_ge(exp_done, KT * NG * b + KT * (g + 1))
                for t in range(KT):
                    for j in range(HG):
                        last = mm(pO[32 * j:32 * j + 32, T * g:T * g + T], vaug[b % 2][0:LT, t, HG * g + j, :],
                                  pexp[g % 2][0:LT, t, T * j:T * j + T], t == 0, t == KT - 1)
                last.then_inc(pv_ps, 1)

            @batch
            def t_oT(b):
                pe.wait_ge(o_evac, b + 1)
                if b >= 1:
                    pe.wait_ge(x2_ready, b)
                for g in range(NG):
                    last = tr(pC[0:T, 128 * g:128 * g + 128], osb[:, T * g:T * g + T], idf)
                last.then_inc(oT_ps, 1)

            @batch
            def t_onT(b):
                pe.wait_ge(on_ready, b + 1)
                for k in range(DC):
                    last = tr(pC[:, T * k:T * k + T], on[:, 128 * k:128 * k + 128], idf)
                last.then_inc(onT_ps, 1)

            @batch
            def t_oproj(b):
                pe.wait_ge(onT_sb, b + 1)
                for k in range(DC):
                    last = mm(pC[0:T, 0:D], onT[:, k, :], WoT[:, k, :], k == 0, k == DC - 1)
                last.then_inc(oproj_ps, 1)

            @batch
            def t_xqT(b):
                pe.wait_ge(xq_ready, b + 1)
                for k in range(DC):
                    tr(pCb[:, T * k:T * k + T], xq[:, 128 * k:128 * k + 128], idb)
                mm(pC[:, 128:128 + T], onesf[0:T, :], dg[:, :], True, True).then_inc(xqT_ps, 1)

            @batch
            def t_h(b, half):
                pe.wait_ge(xqT_sb, b + 1)
                if b >= 1 or half:
                    pe.wait_ge(h_evac, 2 * b + half)
                for m in range(M0 // 2):
                    for k in range(DC):
                        f = (half * M0 // 2 + m) * 128
                        last = mm(pC[:, T * m:T * m + T], w1T[:, k, f:f + 128], xqT[:, k, :], k == 0, k == DC - 1)
                last.then_inc(h_ps, 1)

            @batch
            def t_amcT(b):
                pe.wait_ge(amc_ready, b + 1)
                tr(pC[0:T, 0:128], amc[:, :], idf).then_inc(amcT_ps, 1)

            @batch
            def t_dg2(b):
                pe.wait_ge(dg2_ready, b + 1)
                mm(pC[:, 128:128 + T], onesf[0:T, :], dg[:, :], True, True).then_inc(dg2_ps, 1)

            @batch
            def t_down(b):
                pe.wait_ge(hq_ready, b + 1)
                for m in range(M0):
                    last = mm(pC[0:T, 0:D], hq[:, m, :], w2T[:, m, :], m == 0, m == M0 - 1)
                last.then_inc(f_ps, 1)

            @batch
            def u_xn2T(b):
                pe.wait_ge(xn2_ready, b + 1)
                if b >= 1:
                    pe.wait_ge(lg_ready, b)
                for k in range(DC):
                    last = tr(pU[:, T * k:T * k + T], xm[:, 128 * k:128 * k + 128], idf)
                last.then_inc(xn2T_ps, 1)

            @batch
            def u_t(b):
                pe.wait_ge(xn2T_sb, b + 1)
                for m in range(DC):
                    for k in range(DC):
                        last = mm(pU[:, T * m:T * m + T], Wa[:, k, 128 * m:128 * m + 128], xn2T[:, k, :], k == 0, k == DC - 1)
                last.then_inc(t_ps, 1)

            @batch
            def u_sc(b):
                pe.wait_ge(t_sb, b + 1)
                for k in range(DC):
                    last = mm(pU[0:T, 0:L], tT[:, k, :], cxT[b % 3][:, k, :], k == 0, k == DC - 1)
                last.then_inc(sc_ps, 1)

            @batch
            def u_alT(b):
                pe.wait_ge(al_ready, b + 1)
                for t in range(KT):
                    last = tr(pU[0:LT, T * t:T * t + T], al[:, LT * t:LT * t + LT], idf)
                last.then_inc(alT_ps, 1)

            @batch
            def u_c(b):
                pe.wait_ge(alT_sb, b + 1)
                pe.wait_ge(cxt_loaded, 16 * (b + 1))
                for m in range(DC):
                    for t in range(KT):
                        last = mm(pU[:, T * m:T * m + T], cx_t[:, t, 128 * m:128 * m + 128], alT[:, t, :], t == 0, t == KT - 1)
                last.then_inc(c_ps, 1)

            @batch
            def u_wc(b):
                pe.wait_ge(c_sb, b + 1)
                for k in range(2 * DC):
                    last = mm(pU[0:T, 0:D], cT[:, k, :] if k < DC else xn2T[:, k - DC, :], WcT[:, k, :],
                              k == 0, k == 2 * DC - 1)
                last.then_inc(wc_ps, 1)

            @batch
            def u_router(b):
                pe.wait_ge(xn3_ready, b + 1)
                pe.wait_ge(thx_ready, b + 1)
                for k in range(DC):
                    last = tr(pU[:, T * k:T * k + T], xm[:, 128 * k:128 * k + 128], idf)
                last.then_inc(xn3T_ps, 1)
                pe.wait_ge(xn3T_sb, b + 1)
                for k in range(DC):
                    last = mm(pU[0:T, 256:256 + NE], cT[:, k, :], Wr[:, k, :], k == 0, k == DC - 1)
                last.then_inc(r_ps, 1)

            for i in range(-1, B + 2):
                t_oT(i - 1)
                a_scores(i, 0)
                a_scores(i, 1)
                t_onT(i - 1)
                a_scores(i, 2)
                a_scores(i, 3)
                t_oproj(i - 1)
                a_scores(i, 4)
                a_scores(i, 5)
                a_scores(i, 6)
                a_scores(i, 7)
                u_xn2T(i - 2)
                a_scores(i, 8)
                a_scores(i, 9)
                t_xqT(i - 1)
                a_scores(i, 10)
                a_scores(i, 11)
                u_t(i - 2)
                t_h(i - 1, 0)
                a_scores(i, 12)
                a_scores(i, 13)
                a_scores(i, 14)
                a_scores(i, 15)
                t_h(i - 1, 1)
                p_cxT(i + 1)
                a_max(i)
                u_sc(i - 2)
                p_k(i + 1)
                t_amcT(i - 1)
                a_scoresT(i, 0)
                u_alT(i - 2)
                t_dg2(i - 1)
                a_scoresT(i, 1)
                p_vq(i + 1)
                a_pv(i, 0)
                u_c(i - 2)
                t_down(i - 1)
                a_scoresT(i, 2)
                a_pv(i, 1)
                u_wc(i - 2)
                a_scoresT(i, 3)
                a_pv(i, 2)
                u_router(i - 2)
                a_pv(i, 3)
            pe.wait_ge(tri_made, 1)
            pe.wait_ge(m_oh, 1)
            pe.wait_ge(lg_ready, B)
            mm(pC[:, 0:64], onesb[0:T, :], ohb, True, True)
            mm(pC[0:T, 64:128], tri[0:T, 0:T], ohb, True, True).then_inc(cnt_ps, 1)
            pe.wait_ge(sel_ready, 1)
            pe.wait_ge(m_slots, 1)
            pe.wait_ge(ebt_loaded, 16)

            def e_xT(j):
                pe.wait_ge(xs_loaded[j % 4], 16 * (j // 4 + 1))
                if j >= 1:
                    pe.wait_ge(xT_sb, j)
                for k in range(DC):
                    last = tr(pC[:, 128 * k:128 * k + 128], xsb[:, j % 4, 128 * k:128 * k + 128], idf)
                last.then_inc(xT_ps, 1)

            def e_up(j, e):
                pe.wait_ge(xT_sb, j + 1)
                if j >= 2:
                    pe.wait_ge(gelu_done, 2 * (j - 1))
                for n in range(F1 // 512):
                    o = ps[:, 2 * (j % 2) + n, :]
                    mm(o, selx[:, j, :], ebt[:, 512 * n:512 * n + 512], True, False)
                    for k in range(DC):
                        last = mm(o, xsT[:, j % 2, k, :], late[:, bass.ds(e * EW + k * F1 + 512 * n, 512)], False, k == DC - 1)
                    last.then_inc(h1_ps, 1)

            def e_hT(j):
                for n in range(2):
                    pe.wait_ge(gelu_done, 2 * j + n + 1)
                    if j >= 1:
                        pe.wait_ge(hT_sb, 2 * (j - 1) + n + 1)
                    for f in range(M1 // 2):
                        g = n * M1 // 2 + f
                        last = tr(pAB[:, n, 128 * f:128 * f + 128], hx[:, j % 2, 128 * g:128 * g + 128], idf)
                    last.then_inc(hT_ps, 1)

            def e_down(j, e):
                if j >= 1:
                    pe.wait_ge(y_sb, j)
                mm(pO[:, 0:D], selx[:, j, :], ebt[:, F1:FB], True, False)
                for f in range(M1):
                    if f % 4 == 0:
                        pe.wait_ge(hT_sb, 2 * j + f // 4 + 1)
                    last = mm(pO[:, 0:D], hxT[:, j % 2, f, :], late[:, bass.ds(e * EW + DC * F1 + f * D, D)], False, f == M1 - 1)
                last.then_inc(y_ps, 1)

            def expert(j):
                return pe.value_load(ebi[0:1, j:j + 1], min_val=0, max_val=NE - 1)

            pe.wait_ge(w_loaded, 16 * 2 * NE)
            e_xT(0)
            cur = expert(0)
            e_up(0, cur)
            for j in range(NB):
                if j + 1 < NB:
                    e_xT(j + 1)
                    nxt = expert(j + 1)
                    e_up(j + 1, nxt)
                e_hT(j)
                e_down(j, cur)
                cur = nxt

        @block.scalar
        def _(act):
            def copy(dst, src):
                return act.activation(dst, src, ACT.Copy)

            def load_expert(e):
                act.dma_start(W[:, e, 0:DC * F1].rearrange("p (k f) -> p k f", k=DC),
                              A["L1_ffn_W1"][e].rearrange("(k p) f -> p k f", p=128)).then_inc(w_loaded, 16)
                act.dma_start(W[:, e, DC * F1:EW].rearrange("p (m d) -> p m d", m=M1),
                              A["L1_ffn_W2"][e].rearrange("(m p) d -> p m d", p=128)).then_inc(w_loaded, 16)

            act.wait_ge(prep_made, 1)
            act.activation(prep8[:, 5, :], prep8[:, 2, :], ACT.Exp, scale=-1.0 / 128.0).then_inc(gauss_made, 1)
            act.wait_ge(tr_qkv, 1)
            for w, dst in ((0, WqT), (1, WkT)):
                for k in range(DC):
                    for m in range(DC):
                        a = (k * DC + m) * 128
                        copy(dst[:, k, m, :].rearrange("p (d h) -> p d h", h=HM),
                             ps[:, w, a:a + 128].rearrange("p (h d) -> p d h", h=HM))
            copy(WvT[:, :, :].rearrange("p k d -> p (k d)"), ps[:, 2, :]).then_inc(w_evac, 1)
            act.wait_ge(tr_c, 1)
            copy(WcT[:, :, :].rearrange("p (a k) d -> p a (k d)", a=2), ps[:, 3:5, :]).then_inc(w_evac, 1)
            act.wait_ge(tr_o, 1)
            copy(WoT[:, :, :].rearrange("p k d -> p (k d)"), ps[:, 5, :]).then_inc(w_evac, 1)
            psb = ps[:, :, :].bitcast(bf16)
            act.wait_ge(tr_f, 1)
            copy(w1T[:, :, :], psb[:, 0:2, :]).then_inc(w_evac, 1)
            act.wait_ge(tr_f, 2)
            copy(w2T[:, :, :].rearrange("p (a m) d -> p a (m d)", a=2), psb[:, 2:4, :]).then_inc(w_evac, 1)

            @batch
            def w_early(b):
                if b < 3:
                    if b == 0:
                        act.wait_ge(w_evac, 5)
                        act.wait_ge(eb_written, 16)
                    load_expert(b)

            @batch
            def w_late(b):
                if b == B - 1:
                    act.wait_ge(pv_ps, NG * B)
                    act.wait_ge(nm_loaded, 16 * B)
                    for e in range(3, NE - 1):
                        load_expert(e)

            @batch
            def p_cxT(b):
                act.wait_ge(xn0T_ps, b + 1)
                if b >= 3:
                    act.wait_ge(v_ps, b - 2)
                    act.wait_ge(sc_ps, b - 2)
                copy(cxT[b % 3][:, :, :], pAB[:, :, 0:L]).then_inc(cxT_sb, 1)
                if b >= 1:
                    act.wait_ge(q_ps, b)
                copy(xn0T[:, :, :], pAB[:, :, 384:384 + T]).then_inc(xn0T_sb, 1)

            @batch
            def p_kf(b):
                if b == 0:
                    act.wait_ge(bk4_made, 1)
                act.wait_ge(k_ps, b + 1)
                if b >= 1:
                    act.wait_ge(kr_made, b)
                for m in range(DC):
                    last = act.activation(kf[:, m, :], pAB[:, m, 0:L], ACT.Identity, bias=bk4[:, m:m + 1], scale=0.25)
                last.then_inc(k_evac, 1)
                act.wait_ge(k_evac, b + 1)
                if b >= 1:
                    act.wait_ge(k_written, 16 * b)
                copy(kt3[:, :, 0, :], kf).then_inc(kh_made, 1)

            @batch
            def p_km(b):
                act.wait_ge(kr_made, b + 1)
                copy(kt3[:, :, 1, :], kr).then_inc(km_made, 1)

            @batch
            def a_exp(b, g):
                for t in range(KT):
                    n = KT * g + t
                    act.wait_ge(st_ps, KT * NG * b + n + 1)
                    if b >= 1 or g >= 2:
                        act.wait_ge(pv_ps, NG * b + g - 1)
                    act.activation(pexp[g % 2][0:LT, t, :], pS[n % 3][0:LT, 0:HG * T], ACT.Exp).then_inc(exp_done, 1)

            @batch
            def t_osb(b):
                act.wait_ge(pv_ps, NG * (b + 1))
                if b >= 1:
                    act.wait_ge(oT_ps, b)
                copy(osb[:, :], pO[:, 0:HG * T]).then_inc(o_evac, 1)

            @batch
            def t_onT(b):
                act.wait_ge(onT_ps, b + 1)
                if b >= 1:
                    act.wait_ge(oproj_ps, b)
                copy(onT[:, :, :], pC[:, 0:DC * T].rearrange("p (k t) -> p k t", k=DC)).then_inc(onT_sb, 1)

            @batch
            def t_xqT(b):
                act.wait_ge(xqT_ps, b + 1)
                if b >= 1:
                    act.wait_ge(h_ps, 2 * b)
                if b >= 1:
                    act.wait_ge(h_evac, 2 * b)
                copy(xqT[:, :, :], pCb[:, 0:DC * T].rearrange("p (k t) -> p k t", k=DC))
                copy(stB[:, :], pC[:, 128:128 + T]).then_inc(xqT_sb, 1)

            @batch
            def t_center(b, half):
                if b == 0 and half == 0:
                    act.wait_ge(const_loaded, 16 * 7)
                act.wait_ge(h_evac, 2 * b + half + 1)
                if b >= 1:
                    act.wait_ge(g_made, 2 * b)
                for m in range(half * M0 // 2, (half + 1) * M0 // 2):
                    last = act.activation(yc[:, m, :], hs[:, m, 1:1 + T], ACT.Identity, bias=cb[:, m:m + 1], scale=cw[:, m, 1:2])
                last.then_inc(yc_done, 1)

            @batch
            def t_tanh(b, half):
                act.wait_ge(y_ready, 2 * b + half + 1)
                if b >= 1:
                    act.wait_ge(hq_ready, b)
                ms = slice(half * M0 // 2, (half + 1) * M0 // 2)
                act.activation(th[:, ms, :], yc[:, ms, :], ACT.Tanh, scale=0.5).then_inc(th_ready, 1)

            @batch
            def u_xn2T(b):
                act.wait_ge(xn2T_ps, b + 1)
                if b >= 1:
                    act.wait_ge(wc_ps, b)
                copy(xn2T[:, :, :], pU[:, 0:DC * T].rearrange("p (k t) -> p k t", k=DC)).then_inc(xn2T_sb, 1)

            @batch
            def u_t(b):
                act.wait_ge(t_ps, b + 1)
                if b >= 1:
                    act.wait_ge(sc_ps, b)
                copy(tT[:, :, :], pU[:, 0:DC * T].rearrange("p (k t) -> p k t", k=DC)).then_inc(t_sb, 1)

            @batch
            def u_e(b):
                act.wait_ge(sc_done, b + 1)
                if b >= 1:
                    act.wait_ge(al_ready, b)
                act.activation(al[:, :], scr, ACT.Exp, bias=tiny[:, 8:9], accum_out=tiny[:, 9:10]).then_inc(e_ready, 1)

            @batch
            def u_alT(b):
                act.wait_ge(alT_ps, b + 1)
                if b >= 1:
                    act.wait_ge(c_ps, b)
                copy(alT[:, :, :], pU[0:LT, 0:KT * T].rearrange("p (k t) -> p k t", k=KT)).then_inc(alT_sb, 1)

            @batch
            def u_c(b):
                act.wait_ge(c_ps, b + 1)
                if b >= 1:
                    act.wait_ge(r_ps, b)
                copy(cT[:, :, :], pU[:, 0:DC * T].rearrange("p (k t) -> p k t", k=DC)).then_inc(c_sb, 1)

            @batch
            def u_thx(b):
                act.wait_ge(wc_ps, b + 1)
                if b >= 1:
                    act.wait_ge(x3_ready, b)
                act.activation(thx[:, :], pU[0:T, 0:D], ACT.Tanh).then_inc(thx_ready, 1)

            @batch
            def u_router(b):
                act.wait_ge(xn3T_ps, b + 1)
                copy(cT[:, :, :], pU[:, 0:DC * T].rearrange("p (k t) -> p k t", k=DC)).then_inc(xn3T_sb, 1)

            for i in range(-1, B + 2):
                t_osb(i - 1)
                t_onT(i - 1)
                w_early(i - 1)
                u_xn2T(i - 2)
                t_xqT(i - 1)
                u_t(i - 2)
                t_center(i - 1, 0)
                t_center(i - 1, 1)
                p_cxT(i + 1)
                u_e(i - 2)
                p_kf(i + 1)
                t_tanh(i - 1, 0)
                t_tanh(i - 1, 1)
                a_exp(i, 0)
                u_alT(i - 2)
                p_km(i + 1)
                a_exp(i, 1)
                u_c(i - 2)
                a_exp(i, 2)
                u_thx(i - 2)
                a_exp(i, 3)
                u_router(i - 2)
                w_late(i - 1)
            act.wait_ge(lg_ready, B)
            load_expert(NE - 1)
            act.wait_ge(m_d, 1)
            act.activation(m_e3, m_d3, ACT.Exp).then_inc(m_e, 1)
            for j in range(NB):
                for n in range(2):
                    act.wait_ge(h1_ps, 2 * j + n + 1)
                    if j >= 2:
                        act.wait_ge(hT_ps, 2 * (j - 2) + n + 1)
                    act.activation(hx[:, j % 2, 512 * n:512 * n + 512], ps[:, 2 * (j % 2) + n, :], ACT.Gelu)\
                       .then_inc(gelu_done, 1)

        @block.gpsimd
        def _(pool):
            pool.memset(idf[:, :], 0.0)
            pool.memset(idb[:, :], 0.0)
            pool.memset(onesf[:, :], 1.0)
            pool.memset(onesb[:, :], 1.0)
            pool.memset(tri, 1.0)
            pool.memset(expo[:, :], -0.5).then_inc(ones_made, 1)
            pool.wait_ge(ones_made, 1)
            for m in (idf, idb):
                last = pool.affine_select(out=m[:, :], in_=m[:, :], compare_op=ALU.not_equal, fill=1.0, base=0,
                                          pattern=[[-1, 128]], channel_multiplier=1)
            last.then_inc(idents, 1)
            pool.affine_select(out=tri, in_=tri, compare_op=ALU.is_gt, fill=0.0, base=0,
                               pattern=[[1, T]], channel_multiplier=-1).then_inc(tri_made, 1)
            pool.iota(prep8[:, 1, :], [[1, L]], base=0, channel_multiplier=0, allow_small_or_imprecise_dtypes=True)\
                .then_inc(iota_made, 1)
            for n in range(2):
                last = pool.memset(vaug[n][:, :, :, :], 1.0)
            last.then_inc(vpads_made, 1)
            pool.memset(zero, 0.0).then_inc(zero_made, 1)

            @batch
            def rstd_of(b, which):
                pool.wait_ge(ln_in[which], b + 1)
                pool.tensor_tensor(rstd[:, which:which + 1], ve[:, which:which + 1], expo[0:T, :], ALU.pow)\
                    .then_inc(ln_rstd[which], 1)

            @batch
            def p_x0b(b):
                if b == 0:
                    pool.wait_ge(const_loaded, 16 * 7)
                pool.wait_ge(x_loaded, 16 * (b + 1))
                if b >= 2:
                    pool.wait_ge(x1_done, b - 1)
                pool.tensor_tensor(x0b[b % 2][:, :], x0[b % 2][:, :], bo_b[:, :], ALU.add).then_inc(x0b_ready, 1)

            @batch
            def u_x3(b):
                if b == 0:
                    pool.wait_ge(zeroed, 16 * NB)
                pool.wait_ge(thx_ready, b + 1)
                if b >= 1:
                    pool.wait_ge(x3_stored, 16 * b)
                pool.tensor_tensor(x3, x2[:, :], thx[:, :], ALU.add).then_inc(x3_ready, 1)

            for i in range(-1, B + 2):
                rstd_of(i - 2, 2)
                rstd_of(i - 1, 1)
                p_x0b(i + 1)
                rstd_of(i + 1, 0)
                u_x3(i - 2)
                rstd_of(i - 2, 3)
            pool.wait_ge(lg_ready, B)
            pool.wait_ge(x3_stored, 16 * B)
            pool.wait_ge(xn3_stored, 16 * B)
            pool.iota(w8, [[0, B], [-1, NE]], base=NE, channel_multiplier=0, allow_small_or_imprecise_dtypes=True)
            pool.iota(thr, [[0, NE], [128, NB - NE + 1]], base=0, channel_multiplier=0, allow_small_or_imprecise_dtypes=True)
            pool.iota(jix, [[1, NB], [0, NE - 1]], base=0, channel_multiplier=0, allow_small_or_imprecise_dtypes=True)
            pool.iota(ecol, [[0, 1]], base=0, channel_multiplier=1, allow_small_or_imprecise_dtypes=True)\
                .then_inc(m_iota, 1)
            pool.wait_ge(m_slots, 1)
            pool.wait_ge(mx_loaded, 32)
            pool.wait_ge(zeroed, 16 * NB)
            for b in range(B):
                pool.indirect_dma_start(d_xs, bass.IndirectOffsetOnAxis(ap=mi[:, b:b + 1], axis=0), xnall[:, b, :], None)\
                    .then_inc(scattered, 16)
            for n in range(2):
                pool.wait_ge(y_stored[n], 16 * (NB // 2))
            for b in range(B):
                pool.indirect_dma_start(yg[:, b, :], None, d_ys, bass.IndirectOffsetOnAxis(ap=mi[:, b:b + 1], axis=0))\
                    .then_inc(gathered[b], 16)

        @block.vector
        def _(dve):
            steps = [0]

            def step(ins):
                steps[0] += 1
                ins.then_inc(dve_step, 1)
                dve.wait_ge(dve_step, steps[0])

            def tt(o, a, b, op):
                return dve.tensor_tensor(o, a, b, op)

            def ts(o, a, s1, s2, op0, op1):
                return dve.tensor_scalar(o, a, s1, s2, op0, op1)

            for n in range(2):
                dve.memset(kst[n][96:128, :, :], 1.0)
                last = dve.memset(qst[n][96:128, :, :], 1.0)
            last.then_inc(pads_made, 1)
            dve.wait_ge(nat_loaded, 16 * 7)
            for i in range(2):
                step(dve.tensor_reduce(wsum[:, i:i + 1], nat_f[i], X, ALU.add, apply_absolute_value=True))
            dve.sem_inc(wsum_made, 1)
            dve.wait_ge(bias_loaded, 32)
            dve.tensor_copy(bperm[0:1, :, :].rearrange("o w (m d h) -> o (w m) d h", m=DC, h=HM),
                            brow[0:1, :, :].rearrange("o w (m h d) -> o (w m) d h", m=DC, h=HM)).then_inc(bperm_made, 1)
            dve.wait_ge(wsum_ps, 1)
            dve.tensor_copy(bq[:, :], pC[:, 0:2])
            ts(bk4[:, :], pC[:, 2:4], 0.25, None, ALU.mult, ALU.bypass).then_inc(bk4_made, 1)
            step(ts(wscl[:, 0, :], pC[:, 8:10], 1.0 / (F0 * D), 1e-5, ALU.mult, ALU.max))
            step(dve.reciprocal(wscl[:, 1, :], wscl[:, 0, :]))
            for i in range(2):
                step(ts(qw_a[i], nat_f[i], wscl[:, 1, i:i + 1], MAGIC, ALU.mult, ALU.add))
                step(ts(qw_a[i], qw_a[i], MAGIC, 1.0, ALU.subtract, ALU.min))
                ts(qw_b[i], qw_a[i], -1.0, None, ALU.max, ALU.bypass).then_inc(quant, 1)
            dve.wait_ge(prep_loaded, 48)
            dve.wait_ge(iota_made, 1)
            step(ts(prep8[:, 2, :], prep8[:, 0, :], 0.25, None, ALU.mult, ALU.bypass))
            step(dve.tensor_copy(prepb[:, 0, :], prep8[:, 2, :]))
            step(tt(prep8[:, 2, :], prep8[:, 2, :], prepb[:, 0, :], ALU.subtract))
            step(dve.tensor_copy(prepb[:, 1, :], prep8[:, 2, :]))
            step(tt(prepb[:, 2, :], prep8[:, 2, :], prepb[:, 1, :], ALU.subtract))
            step(dve.tensor_copy(prepc[:, 1:2], prepi[:, :]))
            step(ts(prepc[:, 2:3], prepc[:, 0:1], 16.0, 0.0, ALU.subtract, ALU.max))
            step(ts(prepc[:, 3:4], prepc[:, 0:1], 16.0, prepc[:, 1:2], ALU.add, ALU.min))
            step(ts(prep8[:, 3, :], prep8[:, 1, :], prepc[:, 2:3], None, ALU.is_ge, ALU.bypass))
            step(dve.scalar_tensor_tensor(prep8[:, 3, :], prep8[:, 1, :], prepc[:, 3:4], prep8[:, 3, :], ALU.is_le, ALU.mult))
            step(ts(prep8[:, 4, :], prep8[:, 3, :], 1.0, 1e9, ALU.subtract, ALU.mult))
            step(ts(prep8[:, 2, :], prep8[:, 1, :], prepc[:, 0:1], None, ALU.subtract, ALU.bypass))
            step(tt(prep8[:, 2, :], prep8[:, 2, :], prep8[:, 2, :], ALU.mult))
            dve.sem_inc(prep_made, 1)
            dve.wait_ge(eb_loaded, 32)
            step(dve.tensor_copy(eb3[:, 0, :], ebn))
            step(tt(ebr, ebn, eb3[:, 0, :], ALU.subtract))
            step(dve.tensor_copy(eb3[:, 1, :], ebr))
            step(tt(eb3[:, 2, :], ebr, eb3[:, 1, :], ALU.subtract))
            dve.sem_inc(eb_made, 1)

            def ln_stats(x, which):
                step(dve.bn_stats(bst[:, which, :], x))
                step(dve.bn_aggr(mv[:, which, :], bst[:, which, :]))
                ts(ve[:, which:which + 1], mv[:, which, 1:2], EPS, None, ALU.add, ALU.bypass).then_inc(ln_in[which], 1)

            def ln(x, which, b, o):
                dve.wait_ge(ln_rstd[which], b + 1)
                return ts(o, x, mv[:, which, 0:1], rstd[:, which:which + 1], ALU.subtract, ALU.mult)

            @batch
            def p_stats(b):
                dve.wait_ge(x_loaded, 16 * (b + 1))
                ln_stats(x0[b % 2][:, :], 0)

            @batch
            def p_ln(b):
                if b >= 1:
                    dve.wait_ge(xn0T_ps, b)
                ln(x0[b % 2][:, :], 0, b, xn0[:, :]).then_inc(xn0_ready, 1)

            @batch
            def p_kr(b):
                dve.wait_ge(kh_made, b + 1)
                if b >= 1:
                    dve.wait_ge(km_made, b)
                tt(kr, kf, kt3[:, :, 0, :], ALU.subtract).then_inc(kr_made, 1)

            @batch
            def p_kl(b):
                dve.wait_ge(km_made, b + 1)
                tt(kt3[:, :, 2, :], kr, kt3[:, :, 1, :], ALU.subtract).then_inc(kt3_ready, 1)

            @batch
            def p_v(b):
                dve.wait_ge(q_ps, b + 1)
                if b == 0:
                    dve.wait_ge(vpads_made, 1)
                if b >= 2:
                    dve.wait_ge(pv_ps, NG * (b - 1))
                for t in range(KT):
                    last = tt(vaug[b % 2][0:LT, t, :, 0:DK],
                              pAB[0:LT, t // 2, (t % 2) * D:(t % 2) * D + D].rearrange("p (h c) -> p h c", c=DK),
                              bv_b[0:LT, :].rearrange("p (h c) -> p h c", c=DK), ALU.add)
                last.then_inc(v_evac, 1)

            @batch
            def p_q(b):
                dve.wait_ge(q_ps, b + 1)
                dve.wait_ge(tau_loaded, 16 * (b + 1))
                if b >= 1:
                    dve.wait_ge(q_written, 16 * b)
                for m in range(DC):
                    last = ts(qf[:, m, :], pAB[:, 1, D + T * m:D + T * m + T], bq[:, m:m + 1], tau[b % 2][:, 0:1],
                              ALU.add, ALU.mult)
                last.then_inc(q_evac, 1)
                dve.wait_ge(q_evac, b + 1)
                step(dve.tensor_copy(qt3[:, :, 0, :], qf[:, :, :]))
                step(tt(qr[:, :, :], qf[:, :, :], qt3[:, :, 0, :], ALU.subtract))
                step(dve.tensor_copy(qt3[:, :, 1, :], qr[:, :, :]))
                tt(qt3[:, :, 2, :], qr[:, :, :], qt3[:, :, 1, :], ALU.subtract).then_inc(qt3_ready, 1)

            @batch
            def a_max(b, h):
                dve.wait_ge(s_ps, NH * b + h + 1)
                dve.tensor_reduce(mx[:, h:h + 1], pS[h % 3][0:T, 0:L], X, ALU.max).then_inc(mx_done, 1)

            @batch
            def a_neg(b):
                dve.wait_ge(mx_done, NH * (b + 1))
                if b >= 1:
                    dve.wait_ge(nmT_ps, b)
                step(ts(nm[:, 0, :], mx[:, :], -1.0, None, ALU.mult, ALU.bypass))
                step(dve.scalar_tensor_tensor(nr[:, :], mx[:, :], -1.0, nm[:, 0, :], ALU.mult, ALU.subtract))
                step(dve.tensor_copy(nm[:, 1, :], nr[:, :]))
                tt(nm[:, 2, :], nr[:, :], nm[:, 1, :], ALU.subtract).then_inc(nm_ready, 1)

            @batch
            def a_nmT(b):
                dve.wait_ge(nmT_ps, b + 1)
                if b >= 1:
                    dve.wait_ge(nm_written, 16 * b)
                dve.tensor_copy(nmT[:, :], pOb[0:3 * NH, 0:T]).then_inc(nmT_sb, 1)

            @batch
            @batch
            def t_norm(b):
                dve.wait_ge(oT_ps, b + 1)
                heads = pC[0:T, :].rearrange("t (h c) -> t h c", h=NH)
                dve.reciprocal(rs[:, :], heads[:, :, DK:DK + 1].rearrange("t h o -> t (h o)")).then_inc(recip_done, 1)
                dve.wait_ge(recip_done, b + 1)
                if b >= 1:
                    dve.wait_ge(onT_ps, b)
                tt(on[:, :].rearrange("t (h d) -> t h d", h=NH), heads[:, :, 0:DK],
                   rs[:, :].unsqueeze(2).to_broadcast([T, NH, DK]), ALU.mult).then_inc(on_ready, 1)

            def quant_scale(am, c0, half, w, b):
                step(ts(tiny[:, c0 + 2:c0 + 3], am, half, 1e-5, ALU.mult, ALU.max))
                step(dve.reciprocal(tiny[:, c0 + 3:c0 + 4], tiny[:, c0 + 2:c0 + 3]))
                ts(tiny[:, c0:c0 + 1], tiny[:, c0 + 3:c0 + 4], QMAX * half, None, ALU.mult, ALU.bypass)
                step(ts(tiny[:, c0 + 1:c0 + 2], tiny[:, c0 + 2:c0 + 3], 1.0 / QMAX, wscl[0:T, 0, w:w + 1], ALU.mult, ALU.mult))

            @batch
            def t_x1(b):
                dve.wait_ge(oproj_ps, b + 1)
                dve.wait_ge(x0b_ready, b + 1)
                tt(x1[:, :], pC[0:T, 0:D], x0b[b % 2][:, :], ALU.add).then_inc(x1_done, 1)
                dve.wait_ge(x1_done, b + 1)
                ln_stats(x1[:, :], 1)

            @batch
            def t_xq(b):
                if b == 0:
                    dve.wait_ge(w_evac, 5)
                    dve.memset(hs[:, :, 0:1], 0.0)
                    dve.memset(hs[:, :, T + 1:T + 2], 0.0)
                step(ln(x1[:, :], 1, b, xn[:, :]))
                step(dve.tensor_reduce(tiny[:, 4:5], xn[:, :], X, ALU.max, apply_absolute_value=True))
                quant_scale(tiny[:, 4:5], 0, 1.0, 0, b)
                step(ts(xn[:, :], xn[:, :], tiny[:, 0:1], MAGIC, ALU.mult, ALU.add))
                ts(xq[:, :], xn[:, :], MAGIC, QMAX, ALU.subtract, ALU.min)
                if b >= 1:
                    dve.wait_ge(dg2_ps, b)
                ts(dg[:, :], idf[0:T, 0:T], tiny[:, 1:2], None, ALU.mult, ALU.bypass).then_inc(xq_ready, 1)

            @batch
            def t_h(b, half):
                dve.wait_ge(xqT_sb, b + 1)
                dve.wait_ge(h_ps, 2 * b + half + 1)
                if b >= 1:
                    dve.wait_ge(yc_done, 2 * b)
                m0 = half * M0 // 2
                tt(hs[:, m0:m0 + M0 // 2, 1:1 + T], pC[:, 0:M0 // 2 * T].rearrange("p (m t) -> p m t", t=T),
                   stB[:, :].unsqueeze(1).to_broadcast([128, M0 // 2, T]), ALU.mult).then_inc(h_evac, 1)

            @batch
            def t_conv(b, half):
                dve.wait_ge(h_evac, 2 * b + half + 1)
                dve.wait_ge(yc_done, 2 * b + half + 1)
                ms = range(half * M0 // 2, (half + 1) * M0 // 2)
                for m in ms:
                    last = dve.scalar_tensor_tensor(yc[:, m, :], hs[:, m, 0:T], cw[:, m, 0:1], yc[:, m, :],
                                                    ALU.mult, ALU.add)
                step(last)
                for m in ms:
                    last = dve.scalar_tensor_tensor(yc[:, m, :], hs[:, m, 2:2 + T], cw[:, m, 2:3], yc[:, m, :],
                                                    ALU.mult, ALU.add)
                last.then_inc(y_ready, 1)

            @batch
            def t_silu(b, half):
                dve.wait_ge(th_ready, 2 * b + half + 1)
                ms = slice(half * M0 // 2, (half + 1) * M0 // 2)
                dve.scalar_tensor_tensor(th[:, ms, :], th[:, ms, :], 1.0, yc[:, ms, :], ALU.add, ALU.mult).then_inc(g_made, 1)

            @batch
            def t_amax(b):
                dve.wait_ge(g_made, 2 * b + 2)
                if b >= 1:
                    dve.wait_ge(amcT_ps, b)
                dve.tensor_reduce(amc[:, :], th.rearrange("p m t -> p t m"), X, ALU.max, apply_absolute_value=True)\
                   .then_inc(amc_ready, 1)

            @batch
            def t_q2(b):
                dve.wait_ge(amcT_ps, b + 1)
                step(dve.tensor_reduce(tiny[:, 5:6], pC[0:T, 0:128], X, ALU.max))
                quant_scale(tiny[:, 5:6], 10, 0.5, 1, b)
                ts(dg[:, :], idf[0:T, 0:T], tiny[:, 10:11], None, ALU.mult, ALU.bypass).then_inc(dg2_ready, 1)

            @batch
            def t_hq(b):
                dve.wait_ge(dg2_ps, b + 1)
                if b >= 1:
                    dve.wait_ge(f_ps, b)
                step(tt(th, th, pC[:, 128:128 + T].unsqueeze(1).to_broadcast([128, M0, T]), ALU.mult))
                ts(hq, th, MAGIC, MAGIC, ALU.add, ALU.subtract).then_inc(hq_ready, 1)

            @batch
            def t_x2(b):
                dve.wait_ge(f_ps, b + 1)
                if b >= 1:
                    dve.wait_ge(x3_ready, b)
                dve.scalar_tensor_tensor(x2[:, :], pC[0:T, 0:D], tiny[:, 11:12], x1[:, :], ALU.mult, ALU.add)\
                   .then_inc(x2_ready, 1)

            @batch
            def u_stats(b):
                dve.wait_ge(x2_ready, b + 1)
                ln_stats(x2[:, :], 2)

            @batch
            def u_ln(b):
                if b >= 1:
                    dve.wait_ge(xn3T_ps, b)
                    dve.wait_ge(xn3_stored, 16 * b)
                ln(x2[:, :], 2, b, xm[:, :]).then_inc(xn2_ready, 1)

            @batch
            def u_sc(b):
                dve.wait_ge(sc_ps, b + 1)
                dve.wait_ge(msk_loaded, 16 * (b + 1))
                if b >= 1:
                    dve.wait_ge(e_ready, b)
                step(tt(scr, pU[0:T, 0:L], msk[:, 0, :], ALU.mult))
                step(tt(scr, scr, msk[:, 1, :], ALU.add))
                step(dve.tensor_reduce(tiny[:, 6:7], scr, X, ALU.max))
                ts(tiny[:, 8:9], tiny[:, 6:7], -1.0, None, ALU.mult, ALU.bypass).then_inc(sc_done, 1)

            @batch
            def u_al(b):
                dve.wait_ge(e_ready, b + 1)
                step(dve.reciprocal(tiny[:, 7:8], tiny[:, 9:10]))
                if b >= 1:
                    dve.wait_ge(alT_ps, b)
                dve.scalar_tensor_tensor(al[:, :], al[:, :], tiny[:, 7:8], msk[:, 2, :], ALU.mult, ALU.mult)\
                   .then_inc(al_ready, 1)

            @batch
            def u_stats3(b):
                dve.wait_ge(x3_ready, b + 1)
                ln_stats(x3, 3)

            @batch
            def u_ln3(b):
                ln(x3, 3, b, xm[:, :]).then_inc(xn3_ready, 1)

            @batch
            def u_lg(b):
                dve.wait_ge(r_ps, b + 1)
                if b >= 1:
                    dve.wait_ge(lg_stored, 16 * b)
                tt(lg[:, :], pU[0:T, 256:256 + NE], br_b[:, :], ALU.add).then_inc(lg_ready, 1)

            for i in range(-1, B + 2):
                t_norm(i - 1)
                a_max(i, 0)
                a_max(i, 1)
                a_max(i, 2)
                a_max(i, 3)
                u_ln(i - 2)
                t_x1(i - 1)
                a_max(i, 4)
                a_max(i, 5)
                a_max(i, 6)
                a_max(i, 7)
                p_stats(i + 1)
                t_xq(i - 1)
                a_max(i, 8)
                a_max(i, 9)
                a_max(i, 10)
                a_max(i, 11)
                p_ln(i + 1)
                t_h(i - 1, 0)
                a_max(i, 12)
                a_max(i, 13)
                a_max(i, 14)
                a_max(i, 15)
                a_neg(i)
                t_h(i - 1, 1)
                u_sc(i - 2)
                t_conv(i - 1, 0)
                a_nmT(i)
                t_conv(i - 1, 1)
                u_al(i - 2)
                t_silu(i - 1, 0)
                t_silu(i - 1, 1)
                t_amax(i - 1)
                p_kr(i + 1)
                t_q2(i - 1)
                t_hq(i - 1)
                p_kl(i + 1)
                p_v(i + 1)
                p_q(i + 1)
                t_x2(i - 1)
                u_stats3(i - 2)
                u_ln3(i - 2)
                u_lg(i - 2)
                u_stats(i - 1)
            dve.wait_ge(m_loaded, 16)
            dve.wait_ge(m_iota, 1)

            def bc(x):
                return x.unsqueeze(2).to_broadcast([T, B, NE])

            step(dve.tensor_reduce(m_g[:, 0, :], lgall, X, ALU.max))
            tt(m_d3, lgall, bc(m_g[:, 0, :]), ALU.subtract).then_inc(m_d, 1)
            step(tt(oh, lgall, bc(m_g[:, 0, :]), ALU.is_equal))
            step(tt(oh, oh, w8, ALU.mult))
            step(dve.tensor_reduce(m_g[:, 1, :], oh, X, ALU.max))
            step(tt(oh, oh, bc(m_g[:, 1, :]), ALU.is_equal))
            dve.tensor_copy(ohb, oh.rearrange("p b e -> p (b e)")).then_inc(m_oh, 1)
            dve.wait_ge(m_e, 1)
            step(dve.tensor_reduce(m_g[:, 2, :], m_e3, X, ALU.add))
            step(dve.reciprocal(m_g[:, 3, :], m_g[:, 2, :]))
            dve.wait_ge(cnt_ps, 1)
            step(dve.tensor_copy(cnt, pC[:, 0:64].rearrange("p (b e) -> p b e", e=NE)))
            step(dve.memset(pre[:, 0, :], 0.0))
            for b in range(B):
                step(tt(pre[:, b + 1, :], pre[:, b, :], cnt[:, b, :], ALU.add))
            step(tt(cmp1, pre[:, B, :].unsqueeze(2).to_broadcast([128, NE, NB - NE + 1]), thr, ALU.is_gt))
            step(dve.tensor_reduce(nblk, cmp1, X, ALU.add))
            step(dve.memset(bs[:, 0:1], 0.0))
            for e in range(NE - 1):
                step(tt(bs[:, e + 1:e + 2], bs[:, e:e + 1], nblk[:, e:e + 1], ALU.add))
            step(tt(cmp2, jix, bs[:, 1:NE].unsqueeze(1).to_broadcast([128, NB, NE - 1]), ALU.is_ge))
            step(dve.tensor_reduce(ebj, cmp2, X, ALU.add))
            dve.tensor_copy(ebi[:, :], ebj[0:1, :])
            step(ts(ecol2, ecol, float(NE), float(NE), ALU.is_ge, ALU.mult))
            step(ts(ecol3, ecol, 2.0 * NE, float(NE), ALU.is_ge, ALU.mult))
            step(tt(ecol2, ecol2, ecol3, ALU.add))
            step(tt(ecol2, ecol, ecol2, ALU.subtract))
            step(ts(sel, ebj[0:3 * NE, :], ecol2, None, ALU.is_equal, ALU.bypass))
            dve.tensor_copy(selx[:, :, :], sel.unsqueeze(2).to_broadcast([3 * NE, NB, 128])).then_inc(sel_ready, 1)
            step(dve.scalar_tensor_tensor(base, bs[0:T, :].unsqueeze(1).to_broadcast([T, B, NE]), 128.0, pre[0:T, 0:B, :],
                                          ALU.mult, ALU.add))
            step(tt(base, pC[0:T, 64:128].rearrange("p (b e) -> p b e", e=NE), base, ALU.add))
            step(tt(base, base, oh, ALU.mult))
            step(dve.tensor_reduce(m_g[:, 4, :], base, X, ALU.add))
            dve.tensor_copy(mi[:, :], m_g[:, 4, :]).then_inc(m_slots, 1)

            for j in range(NB):
                if j == 0:
                    dve.wait_ge(xT_ps, 1)
                    dve.tensor_copy(xsT[:, 0], pC[:, 0:D].rearrange("p (k t) -> p k t", k=DC)).then_inc(xT_sb, 1)
                if j + 1 < NB:
                    dve.wait_ge(xT_ps, j + 2)
                    if j >= 1:
                        dve.wait_ge(h1_ps, 2 * j)
                    dve.tensor_copy(xsT[:, (j + 1) % 2], pC[:, 0:D].rearrange("p (k t) -> p k t", k=DC))\
                       .then_inc(xT_sb, 1)
                for n in range(2):
                    dve.wait_ge(hT_ps, 2 * j + n + 1)
                    if j >= 2:
                        dve.wait_ge(y_ps, j - 1)
                    dve.tensor_copy(hxT[:, j % 2, 4 * n:4 * n + 4, :].rearrange("p f t -> p (f t)"), pAB[:, n, :])\
                       .then_inc(hT_sb, 1)
                dve.wait_ge(y_ps, j + 1)
                if j >= 2:
                    dve.wait_ge(y_stored[j % 2], 16 * (j // 2))
                dve.tensor_copy(ysb[:, j % 2, :], pO[:, 0:D]).then_inc(y_sb, 1)
            for b in range(B):
                dve.wait_ge(gathered[b], 16)
                dve.scalar_tensor_tensor(yg[:, b, :], yg[:, b, :], m_g[:, 3, b:b + 1], x3all[:, b, :], ALU.mult, ALU.add)\
                   .then_inc(out_ready, 1)


_INS = ['x', 'ctx_1024', 'condB_tau', 'fside_BxS2_0', 'condB_pt', '_lenS2', 'L0_xcond_Wq', 'L0_xcond_bq', 'L0_xcond_Wk',
        'L0_xcond_bk', 'L0_xcond_Wv', 'L0_xcond_bv', 'L0_xcond_Wo', 'L0_xcond_bo', 'L0_ffn_w1', 'L0_ffn_conv_w',
        'L0_ffn_conv_b', 'L0_ffn_w2', 'L1_xcond_W_a', 'L1_xcond_W_c', 'L1_ffn_W1', 'L1_ffn_b1', 'L1_ffn_W2', 'L1_ffn_b2',
        'L1_ffn_Wr', 'L1_ffn_br']


def kernel(**inputs):
    import numpy as _np
    import concourse.bacc as _bacc
    from concourse import mybir as _mybir
    from concourse.bass_utils import run_bass_kernel_spmd as _run

    nc = _bacc.Bacc("TRN2", target_bir_lowering=False, num_devices=1)
    arrays, aps = {}, {}
    for name in _INS:
        a = _np.ascontiguousarray(inputs[name])
        arrays[f"in_{name}"] = a
        aps[name] = nc.dram_tensor(f"in_{name}", a.shape, _mybir.dt.from_np(a.dtype), kind="ExternalInput").ap()
    out = nc.dram_tensor("out_x", inputs["x"].shape, _mybir.dt.float32, kind="ExternalOutput").ap()
    pixart_block(nc, aps, out)
    r = _run(nc, [arrays], core_ids=[0])
    return r.results[0]["out_x"]
```

```python
import concourse.bass as bass
from concourse import mybir
from contextlib import ExitStack, nullcontext


def pixart_block(nc, A, out):
    fp32 = mybir.dt.float32
    bf16 = mybir.dt.bfloat16
    i32 = mybir.dt.int32
    ALU = mybir.AluOpType
    ACT = mybir.ActivationFunctionType
    X = mybir.AxisListType.X

    B, T, D = A["x"].shape
    L = A["ctx_1024"].shape[1]
    NH, DK = 16, 16
    KT = 3
    LT = L // KT
    DC = D // 128
    HM = NH // DC
    HG = 4
    NG = NH // HG
    F0 = A["L0_ffn_w1"].shape[0]
    M0 = F0 // 128
    NE, _, F1 = A["L1_ffn_W1"].shape
    M1 = F1 // 128
    FB = F1 + D
    NT = B * T
    NB = NT // 128 + NE - 1
    SURE = -(-NT // 128)
    TERMS = [(0, 0), (0, 1), (0, 2), (1, 0), (1, 1), (2, 0)]
    KS = 16 * len(TERMS)
    KD = KS + 3
    KX = KD + 3
    MAGIC = 12582912.0
    EPS = 1e-5
    QMAX = 127.0

    ctx = ExitStack()
    with ctx:
        def sb(name, shape, dt=fp32):
            return ctx.enter_context(nc.sbuf_tensor(name, shape, dt))

        def sem(name):
            return ctx.enter_context(nc.semaphore(name))

        def dram(name, shape, dt=fp32):
            return nc.dram_tensor(name, shape, dt).ap()

        d_k = [dram(f"d_k{i}", [DC, 3, 128, L], bf16) for i in range(2)]
        d_q = [dram(f"d_q{i}", [DC, 3, 128, T], bf16) for i in range(2)]
        d_nm = [dram(f"d_nm{i}", [3 * NH, T], bf16) for i in range(2)]
        d_delta = dram("d_delta", [B, 3, L], bf16)
        d_mask = dram("d_mask", [B, 3 * L])
        d_x3 = dram("d_x3", [B, T, D])
        d_xn3 = dram("d_xn3", [B, T, D])
        d_eb = dram("d_eb", [3, NE, FB], bf16)
        XW = 2 * D + 2
        d_xs = dram("d_xs", [NB * 128, XW])

        EW = DC * F1 + M1 * D
        W = sb("W", [128, NE, EW])
        late = W[:, :, :].rearrange("p e n -> p (e n)")
        LATE0 = 3 * EW
        taken = [LATE0]

        def carve(words):
            a = taken[0]
            taken[0] += words
            assert taken[0] <= (NE - 1) * EW
            return late[:, a:a + words]

        kst = [carve(NH * L // 2).bitcast(bf16).rearrange("p (h l) -> p h l", h=NH) for _ in range(2)]
        qst = [carve(NH * T // 2).bitcast(bf16).rearrange("p (h t) -> p h t", h=NH) for _ in range(2)]
        pexp = [carve(KT * HG * T).rearrange("p (k n) -> p k n", k=KT) for _ in range(2)]
        vaug = [carve(KT * NH * 32).rearrange("p (k h c) -> p k h c", k=KT, h=NH) for _ in range(2)]
        kf = carve(DC * L).rearrange("p (m l) -> p m l", m=DC)
        kr = carve(DC * L).rearrange("p (m l) -> p m l", m=DC)
        kt3 = carve(3 * DC * L // 2).bitcast(bf16).rearrange("p (m t l) -> p m t l", t=3, m=DC)

        st3 = W[:, NE - 1, :]
        nat_qkv = st3[:, 0:3 * 512].rearrange("p (w m d) -> p w m d", w=3, m=DC)
        nat_o = st3[:, 1536:2048].rearrange("p (m d) -> p m d", m=DC)
        nat_c = st3[:, 2048:3072].rearrange("p (m d) -> p m d", m=DC)
        nat_f = [W[:, 2, i * 2048:(i + 1) * 2048] for i in range(2)]
        qw_a = [W[:, 1, i * 2048:(i + 1) * 2048] for i in range(2)]
        qw_b = [W[:, 0, i * 1024:(i + 1) * 1024].bitcast(bf16) for i in range(2)]
        eb3 = W[0:NE, 0, 2048:2048 + 3 * FB // 2].bitcast(bf16).rearrange("e (t f) -> e t f", t=3)

        WqT = sb("WqT", [128, DC, DC, 128])
        WkT = sb("WkT", [128, DC, DC, 128])
        WvT = sb("WvT", [128, DC, D])
        WoT = sb("WoT", [128, DC, D])
        WcT = sb("WcT", [128, 2 * DC, D])
        Wa = sb("Wa", [128, DC, D])
        Wr = sb("Wr", [128, DC, NE])
        w1T = sb("w1T", [128, DC, F0], bf16)
        w2T = sb("w2T", [128, M0, D], bf16)
        bq = sb("bq", [128, DC])
        bk4 = sb("bk4", [128, DC])
        bv = sb("bv", [128, DC])
        bo_b = sb("bo_b", [T, D])
        br_b = sb("br_b", [T, NE])
        cw = sb("cw", [128, M0, 3])
        cb = sb("cb", [128, M0])
        idf = sb("idf", [128, 128])
        idb = sb("idb", [128, 128], bf16)
        onesf = sb("onesf", [128, 128])
        onesb = sb("onesb", [128, 128], bf16)
        expo = sb("expo", [128, 1])
        wsum = sb("wsum", [128, 2])
        wscl = sb("wscl", [128, 2, 2])
        spare = kst[1][0:B].rearrange("p h l -> p (h l)")
        prep8 = spare[:, 0:12 * L].bitcast(fp32).rearrange("p (k l) -> p k l", k=6)
        prepb = spare[:, 12 * L:15 * L].rearrange("p (k l) -> p k l", k=3)
        prepi = sb("prepi", [B, 1], i32)
        prepc = sb("prepc", [B, 5])

        HOLD = 12752
        hold = sb("hold", [128, HOLD])
        used = [0]

        def hb(rows, *dims, dt=fp32):
            n = 1
            for d in dims:
                n *= d
            words = n if dt == fp32 else (n + 1) // 2
            a = used[0]
            used[0] += words
            assert used[0] <= HOLD, used[0]
            v = hold[0:rows, a:a + words]
            if dt != fp32:
                v = v.bitcast(dt)
            if len(dims) == 2:
                v = v.rearrange("p (a b) -> p a b", a=dims[0])
            if len(dims) == 3:
                v = v.rearrange("p (a b c) -> p a b c", a=dims[0], b=dims[1])
            return v

        cx = hb(LT, KT, D)
        xn0 = hb(T, D)
        xn0T = hb(128, DC, T)
        qf = hb(128, DC, T)
        qr = hb(128, DC, T)
        qt3 = hb(128, DC, 3, T, dt=bf16)
        x0 = [hb(T, D) for i in range(2)]
        x0b = [hb(T, D) for i in range(2)]
        osb = hb(128, HG * T)
        on = hb(T, D)
        onT = hb(128, DC, T)
        x1 = hb(T, D)
        xn = hb(T, D)
        xq = hb(T, D, dt=bf16)
        xqT = hb(128, DC, T, dt=bf16)
        amc = hb(128, T)
        cxT = [None] * 3
        for n in range(3):
            cxT[(B + n) % 3] = hb(128, DC, L)
        FREE = used[0] - DC * L
        cx_t = hb(LT, KT, D)
        x2 = hb(T, D)
        zero = hb(128, D + 1)
        x3 = zero[0:T, 0:D]
        xm = hb(T, D)
        ebn = hold[0:NE, used[0]:used[0] + FB]
        msk = hb(T, 3, L)
        al = hb(T, L)
        alT = hb(LT, KT, T)
        xn2T = hb(128, DC, T)
        tT = hb(128, DC, T)
        cT = hb(128, DC, T)
        thx = hb(T, D)
        scr = hb(T, L)
        big = W[:, NE - 1, :]
        hs = big[:, 0:M0 * (T + 2)].rearrange("p (m t) -> p m t", m=M0)
        yc = big[:, 1024:1024 + M0 * T].rearrange("p (m t) -> p m t", m=M0)
        th = big[:, 2048:2048 + M0 * T].rearrange("p (m t) -> p m t", m=M0)
        hq = big[:, 3072:3072 + M0 * T // 2].bitcast(bf16).rearrange("p (m t) -> p m t", m=M0)
        stB = big[:, 1920:1920 + T]
        dg = big[0:T, 2944:2944 + T]
        used[0] = 0
        xall = hb(T, B, XW)
        w8 = hb(T, B, NE)
        thr, cmp1 = (hb(128, NE, NB - NE + 1) for _ in range(2))
        jix = hb(128, NB, NE - 1)
        earlier = hb(128, NE, NE)
        ecol = hb(3 * NE, 1)
        erow = hb(3 * NE, 1)
        assert used[0] <= FREE
        hx = hb(128, 2, F1)
        hxT = hb(128, 2, M1, 128)
        xsb = hb(128, 4, XW)
        xsT = hb(128, 2, DC, 128)
        ysb = hb(128, 2, D)
        oh, m_d3, m_e3, base = (hb(T, B, NE) for _ in range(4))
        ohb = hb(T, B, NE, dt=bf16)
        cmp2 = hb(128, NB, NE - 1)
        cmp3 = hb(128, NE, NE)
        nblk, bs = (hb(128, NE) for _ in range(2))
        ebj = hb(128, NB + 1)
        ebi = hb(1, NB + 1).bitcast(i32)
        sel = hb(3 * NE, NB)
        rid = hb(128, 4)
        tid = hb(128, 4).bitcast(i32)
        selx = w1T[0:3 * NE, :, :].rearrange("p k f -> p (k f)")[:, 0:NB * 128].rearrange("p (j c) -> p j c", j=NB)
        ebt = w2T[0:3 * NE, :, :].rearrange("p m d -> p (m d)")[:, 0:FB]
        lgall = sb("lgall", [T, B, NE])
        tau = sb("tau", [128, B])
        mx = sb("mx", [T, NH])
        rs = sb("rs", [T, NH])
        nr = sb("nr", [T, NH])
        nm = sb("nm", [T, 3, NH], bf16)
        nmT = sb("nmT", [3 * NH, T], bf16)
        bst = sb("bst", [T, 4, 6])
        mv = sb("mv", [T, 4, 2])
        ve = sb("ve", [T, 4])
        rstd = sb("rstd", [T, 4])
        tiny = sb("tiny", [T, 16])
        brow = kf[0:1].rearrange("o m l -> o (m l)")[:, 0:2 * D].rearrange("o (w d) -> o w d", w=2)
        bperm = kr[0:1].rearrange("o m l -> o (m l)")[:, 0:2 * D].rearrange("o (w d) -> o w d", w=2)
        mi = sb("mi", [T, B], i32)
        m_g = sb("m_g", [T, 8, B])

        tri = sb("tri", [T, T], bf16)[:, :]

        ps = ctx.enter_context(nc.psum_tensor("ps", [128, 8, 512], fp32))
        pS = [ps[:, i, :] for i in range(3)]
        pU = ps[:, 3, :]
        pO = ps[:, 4, :]
        pAB = ps[:, 5:7, :]
        pC = ps[:, 7, :]
        pCb = pC.bitcast(bf16)
        pOb = pO.bitcast(bf16)

        alT_ps = sem("alT_ps")
        alT_sb = sem("alT_sb")
        al_ready = sem("al_ready")
        amcT_ps = sem("amcT_ps")
        amc_ready = sem("amc_ready")
        bias_loaded = sem("bias_loaded")
        qr_made = sem("qr_made")
        qm_made = sem("qm_made")
        qh_made = sem("qh_made")
        bo_made = sem("bo_made")
        wscl_made = sem("wscl_made")
        win_loaded = sem("win_loaded")
        tr_w = sem("tr_w")
        qkvT_sb = sem("qkvT_sb")
        qkv_loaded = sem("qkv_loaded")
        mask_written = sem("mask_written")
        mask_made = sem("mask_made")
        f_loaded = sem("f_loaded")
        eb_step = sem("eb_step")
        delta_written = sem("delta_written")
        delta_made = sem("delta_made")
        co_loaded = sem("co_loaded")
        bk4_made = sem("bk4_made")
        bperm_made = sem("bperm_made")
        c_ps = sem("c_ps")
        c_sb = sem("c_sb")
        cnt_ps = sem("cnt_ps")
        const_loaded = sem("const_loaded")
        cxT_ps = sem("cxT_ps")
        cxT_sb = sem("cxT_sb")
        cx_loaded = sem("cx_loaded")
        cxt_loaded = sem("cxt_loaded")
        dg2_ps = sem("dg2_ps")
        dg2_ready = sem("dg2_ready")
        dve_step = sem("dve_step")
        e_ready = sem("e_ready")
        eb_loaded = sem("eb_loaded")
        eb_made = sem("eb_made")
        eb_written = sem("eb_written")
        ebt_loaded = sem("ebt_loaded")
        exp_done = sem("exp_done")
        f_ps = sem("f_ps")
        g_made = sem("g_made")
        gauss_made = sem("gauss_made")
        gelu_done = sem("gelu_done")
        h1_ps = sem("h1_ps")
        hT_ps = sem("hT_ps")
        hT_sb = sem("hT_sb")
        h_evac = sem("h_evac")
        h_ps = sem("h_ps")
        hq_ready = sem("hq_ready")
        idents = sem("idents")
        iota_made = sem("iota_made")
        k_evac = sem("k_evac")
        k_ps = sem("k_ps")
        k_written = sem("k_written")
        kh_made = sem("kh_made")
        km_made = sem("km_made")
        kr_made = sem("kr_made")
        kst_loaded = sem("kst_loaded")
        kt3_ready = sem("kt3_ready")
        lg_ready = sem("lg_ready")
        m_d = sem("m_d")
        m_e = sem("m_e")
        m_iota = sem("m_iota")
        m_oh = sem("m_oh")
        m_slots = sem("m_slots")
        msk_loaded = sem("msk_loaded")
        mx_done = sem("mx_done")
        mx_loaded = sem("mx_loaded")
        nmT_ps = sem("nmT_ps")
        nmT_sb = sem("nmT_sb")
        nm_loaded = sem("nm_loaded")
        nm_ready = sem("nm_ready")
        nm_written = sem("nm_written")
        o_evac = sem("o_evac")
        on_ready = sem("on_ready")
        ones_made = sem("ones_made")
        oT_ps = sem("oT_ps")
        onT_ps = sem("onT_ps")
        onT_sb = sem("onT_sb")
        oproj_ps = sem("oproj_ps")
        recip_done = sem("recip_done")
        prep_loaded = sem("prep_loaded")
        pv_ps = sem("pv_ps")
        q_evac = sem("q_evac")
        q_ps = sem("q_ps")
        q_written = sem("q_written")
        qst_loaded = sem("qst_loaded")
        qt3_ready = sem("qt3_ready")
        quant = sem("quant")
        r_ps = sem("r_ps")
        s_ps = sem("s_ps")
        sc_done = sem("sc_done")
        sc_ps = sem("sc_ps")
        scattered = sem("scattered")
        sel_ready = sem("sel_ready")
        st_ps = sem("st_ps")
        t_ps = sem("t_ps")
        t_sb = sem("t_sb")
        th_ready = sem("th_ready")
        thx_ready = sem("thx_ready")
        tr_qkv = sem("tr_qkv")
        filled = sem("filled")
        v_evac = sem("v_evac")
        v_ps = sem("v_ps")
        w_evac = sem("w_evac")
        w_loaded = sem("w_loaded")
        wc_ps = sem("wc_ps")
        wsum_made = sem("wsum_made")
        prep_ps = sem("prep_ps")
        x0b_ready = sem("x0b_ready")
        x1_done = sem("x1_done")
        x2_ready = sem("x2_ready")
        x3_ready = sem("x3_ready")
        x3_stored = sem("x3_stored")
        xT_ps = sem("xT_ps")
        xT_sb = sem("xT_sb")
        x_loaded = sem("x_loaded")
        xn0T_ps = sem("xn0T_ps")
        xn0T_sb = sem("xn0T_sb")
        xn0_ready = sem("xn0_ready")
        xn2T_ps = sem("xn2T_ps")
        xn2T_sb = sem("xn2T_sb")
        xn2_ready = sem("xn2_ready")
        xn3T_ps = sem("xn3T_ps")
        xn3T_sb = sem("xn3T_sb")
        xn3_ready = sem("xn3_ready")
        xn3_stored = sem("xn3_stored")
        xqT_ps = sem("xqT_ps")
        xqT_sb = sem("xqT_sb")
        xq_ready = sem("xq_ready")
        y_ps = sem("y_ps")
        y_ready = sem("y_ready")
        y_sb = sem("y_sb")
        y_stored = sem("y_stored")
        yc_done = sem("yc_done")
        zeroed = sem("zeroed")
        xs_loaded = [sem(f"xs_loaded{i}") for i in range(4)]
        gathered = [sem(f"gathered{i}") for i in range(B // 2)]
        ln_in = [sem(f"ln_in{i}") for i in range(4)]
        ln_rstd = [sem(f"ln_rstd{i}") for i in range(4)]

        block = ctx.enter_context(nc.Block())

        def blocks(eng):
            return eng.value_load(ebi[0:1, NB:NB + 1], min_val=SURE, max_val=NB)

        def filled_block(eng, total, j):
            return eng.If(total > j) if j >= SURE else nullcontext()

        def batch(f):
            def stage(b, *part):
                if 0 <= b < B:
                    f(b, *part)
            return stage


        @block.sync
        def _(sp):
            def rows(b):
                if b >= 1:
                    sp.wait_ge(cxT_ps, b)
                sp.dma_start(cx[:, :, :], A["ctx_1024"][b].rearrange("(k p) d -> p k d", p=LT)).then_inc(cx_loaded, 16)
                if b >= 2:
                    sp.wait_ge(x0b_ready, b - 1)
                if b >= 1:
                    sp.wait_ge(xn0_ready, b)
                sp.dma_start(x0[b % 2][:, :], A["x"][b]).then_inc(x_loaded, 16)

            @batch
            def p_rows(b):
                if b > 0:
                    rows(b)

            @batch
            def p_stackk(b):
                sp.wait_ge(kt3_ready, b + 1)
                sp.dma_start(d_k[b % 2].rearrange("m t p l -> p (m t) l"), kt3.rearrange("p m t l -> p (m t) l")).then_inc(k_written, 16)
                sp.wait_ge(k_written, 16 * (b + 1))
                if b == 1:
                    sp.wait_ge(mask_written, 16)
                if b >= 2:
                    sp.wait_ge(st_ps, 12 * (b - 1))
                src = d_k[b % 2].rearrange("m t (d h) l -> (t d) m (h l)", h=HM)
                for lo, n in ((0, 3), (48, 2), (80, 1)):
                    sp.dma_start(kst[b % 2][lo:lo + 16 * n].rearrange("p (m h) l -> p m (h l)", m=DC), src[0:16 * n]).then_inc(kst_loaded, 16)
                sp.dma_start(kst[b % 2][KS:KD], d_delta[b].unsqueeze(1).to_broadcast([3, NH, L])).then_inc(kst_loaded, 16)

            @batch
            def p_stackq(b):
                sp.wait_ge(qt3_ready, b + 1)
                sp.dma_start(d_q[b % 2].rearrange("m t p l -> p (m t) l"), qt3.rearrange("p m t l -> p (m t) l")).then_inc(q_written, 16)
                sp.wait_ge(q_written, 16 * (b + 1))
                src = d_q[b % 2].rearrange("m t (d h) l -> (t d) m (h l)", h=HM)
                for r, (tq, _) in enumerate(TERMS):
                    sp.dma_start(qst[b % 2][16 * r:16 * r + 16].rearrange("p (m h) l -> p m (h l)", m=DC),
                         src[16 * tq:16 * tq + 16]).then_inc(qst_loaded, 16)

            @batch
            def a_stack(b):
                sp.wait_ge(nmT_sb, b + 1)
                sp.dma_start(d_nm[b % 2], nmT[:, :]).then_inc(nm_written, 16)
                sp.wait_ge(nm_written, 16 * (b + 1))
                sp.dma_start(qst[b % 2][KD:KX].rearrange("p h t -> p (h t)"), d_nm[b % 2].rearrange("(t h) n -> t (h n)", t=3)).then_inc(nm_loaded, 16)

            @batch
            def u_cx(b):
                if b >= 1:
                    sp.wait_ge(c_ps, b)
                sp.dma_start(cx_t[:, :, :], A["ctx_1024"][b].rearrange("(k p) d -> p k d", p=LT)).then_inc(cxt_loaded, 16)

            @batch
            def u_mask(b):
                if b == 0:
                    sp.wait_ge(mask_written, 16)
                    sp.wait_ge(eb_made, 1)
                if b >= 1:
                    sp.wait_ge(al_ready, b)
                sp.dma_start(msk[:, :, :], d_mask[b].partition_broadcast(T).rearrange("t (k l) -> t k l", k=3)).then_inc(msk_loaded, 16)

            def store(b):
                sp.wait_ge(x3_ready, b + 1)
                sp.dma_start(d_x3[b], x3).then_inc(x3_stored, 16)
                sp.wait_ge(xn3_ready, b + 1)
                sp.dma_start(d_xn3[b], xm[:, :]).then_inc(xn3_stored, 16)

            @batch
            def u_store(b):
                if b < B - 1:
                    store(b)

            @batch
            def w_mask(b):
                if b == 0:
                    sp.wait_ge(gauss_made, 1)
                    sp.dma_start(d_mask, prep8[:, 3:6, :].rearrange("b k l -> b (k l)")).then_inc(mask_written, 16)

            @batch
            def w_eb(b):
                if b == 0:
                    sp.wait_ge(eb_made, 1)
                    sp.dma_start(d_eb.rearrange("t e f -> e t f"), eb3).then_inc(eb_written, 16)
                    sp.wait_ge(eb_written, 16)
                    sp.wait_ge(filled, 4)
                    n = NB * XW // (D + 1)
                    sp.dma_start(d_xs.rearrange("(p j) w -> p (j w)", p=128).rearrange("p (n w) -> p n w", n=n),
                                 zero.unsqueeze(1).to_broadcast([128, n, D + 1])).then_inc(zeroed, 16)

            sp.dma_start(prep8[:, 0, :], A["fside_BxS2_0"]).then_inc(prep_loaded, 16)
            for i, n in ((1, "Wk"), (0, "Wq"), (2, "Wv")):
                sp.dma_start(nat_qkv[:, i], A[f"L0_xcond_{n}"].rearrange("(m p) d -> p m d", p=128)).then_inc(qkv_loaded, 16)
            rows(0)
            sp.dma_start(prepc[:, 0:1], A["condB_pt"].unsqueeze(1)).then_inc(win_loaded, 16)
            sp.dma_start(prepi[:, :], A["_lenS2"].unsqueeze(1)).then_inc(win_loaded, 16)
            sp.dma_start(nat_f[0].rearrange("p (m d) -> p m d", m=M0), A["L0_ffn_w1"].rearrange("(m p) d -> p m d", p=128)).then_inc(f_loaded, 16)
            sp.dma_start(nat_f[1].rearrange("p (m d) -> p m d", m=DC), A["L0_ffn_w2"].rearrange("(m p) d -> p m d", p=128)).then_inc(f_loaded, 16)
            sp.dma_start(nat_o, A["L0_xcond_Wo"].rearrange("(m p) d -> p m d", p=128)).then_inc(co_loaded, 16)
            sp.dma_start(nat_c, A["L1_xcond_W_c"].rearrange("(m p) d -> p m d", p=128)).then_inc(co_loaded, 16)
            sp.wait_ge(delta_made, 1)
            sp.dma_start(d_delta, prepb[:, :, :]).then_inc(delta_written, 16)
            sp.wait_ge(delta_written, 16)
            sp.wait_ge(filled, 2)
            for i in range(-1, B + 3):
                w_eb(i)
                p_rows(i + 2)
                u_mask(i - 1)
                a_stack(i)
                p_stackk(i + 1)
                u_store(i - 2)
                w_mask(i + 1)
                p_stackq(i + 1)
                u_cx(i - 1)
            sp.wait_ge(x2_ready, B)
            sp.wait_ge(eb_written, 16)
            sp.dma_start(ebt, d_eb.rearrange("t e f -> (t e) f")).then_inc(ebt_loaded, 16)
            sp.wait_ge(x3_stored, 16 * (B - 1))
            sp.wait_ge(xn3_stored, 16 * (B - 1))
            sp.dma_start(xall[:, 0:B - 1, 0:D], d_xn3[0:B - 1].rearrange("b t d -> t b d")).then_inc(mx_loaded, 16)
            sp.dma_start(xall[:, 0:B - 1, D:2 * D], d_x3[0:B - 1].rearrange("b t d -> t b d")).then_inc(mx_loaded, 16)
            store(B - 1)
            sp.wait_ge(x3_stored, 16 * B)
            sp.dma_start(xall[:, B - 1, D:2 * D], d_x3[B - 1]).then_inc(mx_loaded, 16)
            sp.wait_ge(xn3_stored, 16 * B)
            sp.dma_start(xall[:, B - 1, 0:D], d_xn3[B - 1]).then_inc(mx_loaded, 16)
            sp.wait_ge(scattered, 16 * B)
            sp.wait_ge(sel_ready, 1)
            total = blocks(sp)
            for j in range(NB):
                with filled_block(sp, total, j - 1):
                    if j >= 4:
                        sp.wait_ge(y_sb, j - 3)
                    sp.dma_start(xsb[:, j % 4, :], d_xs[128 * j:128 * j + 128, :]).then_inc(xs_loaded[j % 4], 16)

        @block.tensor
        def _(pe):
            def mm(o, l, r, start, stop):
                return pe.matmul(o, lhsT=l, rhs=r, start=start, stop=stop, skip_group_check=True)

            def tr(o, i, ident):
                n = i.shape[0]
                return pe.transpose(o, i, ident[0:n, 0:n])

            pe.wait_ge(idents, 1)
            pe.wait_ge(qkv_loaded, 16 * 3)
            for w in (1, 0, 2):
                for m in range(DC):
                    for k in range(DC):
                        a = (k * DC + m) * 128
                        last = tr(ps[:, w, a:a + 128], nat_qkv[:, w, m, k * 128:k * 128 + 128], idf)
                last.then_inc(tr_qkv, 1)
            pe.wait_ge(bperm_made, 1)
            for w in range(2):
                for m in range(DC):
                    last = mm(pO[:, 2 * w + m:2 * w + m + 1], bperm[0:1, w, 128 * m:128 * m + 128], onesf[0:1, 0:1],
                              True, True)
            last.then_inc(prep_ps, 1)

            @batch
            def w_sum(b):
                if b == 0:
                    pe.wait_ge(wsum_made, 2)
                    mm(pU[:, 0:2], onesf[:, :], wsum[:, :], True, True).then_inc(prep_ps, 1)

            @batch
            def w_bo(b):
                if b == 0:
                    pe.wait_ge(const_loaded, 16 * 8)
                    pe.wait_ge(w_evac, 7)
                    for k in range(DC):
                        last = mm(pU[0:T, 0:D], bv[:, k:k + 1].to_broadcast([128, T]), WoT[:, k, :], k == 0, k == DC - 1)
                    last.then_inc(prep_ps, 1)

            @batch
            def w_tr(b, n):
                if b == 0:
                    bank = (pC, pU)[n % 2]
                    bankb = bank.bitcast(bf16)
                    if n == 0:
                        pe.wait_ge(co_loaded, 32)
                    if n == 1:
                        pe.wait_ge(wscl_made, 1)
                    if n >= 2:
                        pe.wait_ge(w_evac, n - 1)
                    if n == 3:
                        pe.wait_ge(quant, 1)
                    if n == 5:
                        pe.wait_ge(quant, 2)
                    for m in range(DC):
                        if n < 2:
                            for k in range(2):
                                last = tr(bank[:, k * D + m * 128:k * D + m * 128 + 128],
                                          nat_c[:, m, (2 * n + k) * 128:(2 * n + k) * 128 + 128], idf)
                        elif n == 2:
                            for k in range(DC):
                                last = tr(bank[:, k * D + m * 128:k * D + m * 128 + 128], nat_o[:, m, k * 128:k * 128 + 128], idf)
                        elif n < 5:
                            for t in range(m * M0 // 2, (m + 1) * M0 // 2):
                                a = t * D + (n - 3) * 128
                                last = tr(bankb[:, t * 128:t * 128 + 128], qw_b[0][:, a:a + 128], idb)
                        else:
                            for t in range(4):
                                a = m * F0 + (4 * (n - 5) + t) * 128
                                last = tr(bankb[:, t * D + m * 128:t * D + m * 128 + 128], qw_b[1][:, a:a + 128], idb)
                    last.then_inc(tr_w, 1)

            @batch
            def p_cxT(b):
                if b == 0:
                    pe.wait_ge(qkvT_sb, 3)
                    pe.wait_ge(bk4_made, 1)
                pe.wait_ge(cx_loaded, 16 * (b + 1))
                if b >= 1:
                    pe.wait_ge(q_evac, b)
                if b >= 1:
                    pe.wait_ge(v_evac, b)
                for k in range(DC):
                    for t in range(KT):
                        last = tr(pAB[:, k, LT * t:LT * t + LT], cx[:, t, 128 * k:128 * k + 128], idf)
                last.then_inc(cxT_ps, 1)
                pe.wait_ge(xn0_ready, b + 1)
                for k in range(DC):
                    last = tr(pAB[:, k, 384:384 + T], xn0[:, 128 * k:128 * k + 128], idf)
                last.then_inc(xn0T_ps, 1)

            @batch
            def p_k(b):
                pe.wait_ge(cxT_sb, b + 1)
                pe.wait_ge(xn0T_sb, b + 1)
                for m in range(DC):
                    for k in range(DC):
                        last = mm(pAB[:, m, 0:L], WkT[:, k, m, :], cxT[b % 3][:, k, :], k == 0, k == DC - 1)
                last.then_inc(k_ps, 1)

            @batch
            def p_vq(b):
                pe.wait_ge(k_evac, b + 1)
                for t in range(KT):
                    for k in range(DC):
                        last = mm(pAB[0:LT, t // 2, (t % 2) * D:(t % 2) * D + D], cxT[b % 3][:, k, LT * t:LT * t + LT],
                                  WvT[:, k, :], k == 0, k == DC - 1)
                last.then_inc(v_ps, 1)
                for m in range(DC):
                    for k in range(DC):
                        last = mm(pAB[:, 1, D + T * m:D + T * m + T], WqT[:, k, m, :], xn0T[:, k, :], k == 0, k == DC - 1)
                last.then_inc(q_ps, 1)

            @batch
            def a_scores(b, h):
                if h == 0:
                    pe.wait_ge(kst_loaded, 64 * (b + 1))
                    pe.wait_ge(qst_loaded, 96 * (b + 1))
                if b >= 1 and h < 3:
                    pe.wait_ge(exp_done, KT * NG * b - 2 + h)
                if h >= 3:
                    pe.wait_ge(mx_done, NH * b + h - 2)
                mm(pS[h % 3][0:T, 0:L], qst[b % 2][0:KD, h, :], kst[b % 2][0:KD, h, :], True, True).then_inc(s_ps, 1)

            @batch
            def a_max(b):
                pe.wait_ge(nm_ready, b + 1)
                if b >= 1:
                    pe.wait_ge(o_evac, b)
                tr(pOb[0:3 * NH, 0:T], nm[:, :, :].rearrange("p t h -> p (t h)"), idb).then_inc(nmT_ps, 1)

            @batch
            def a_scoresT(b, g):
                if g == 0:
                    pe.wait_ge(nm_loaded, 16 * (b + 1))
                for t in range(KT):
                    n = KT * g + t
                    if n >= 3:
                        pe.wait_ge(exp_done, KT * NG * b + n - 2)
                    for j in range(HG):
                        last = mm(pS[n % 3][0:LT, T * j:T * j + T], kst[b % 2][0:KX, HG * g + j, LT * t:LT * t + LT],
                                  qst[b % 2][0:KX, HG * g + j, :], True, True)
                    last.then_inc(st_ps, 1)

            @batch
            def a_pv(b, g):
                if g == 0:
                    pe.wait_ge(v_evac, b + 1)
                    pe.wait_ge(nmT_sb, b + 1)
                pe.wait_ge(exp_done, KT * NG * b + KT * (g + 1))
                for t in range(KT):
                    for j in range(HG):
                        last = mm(pO[32 * j:32 * j + 32, T * g:T * g + T], vaug[b % 2][0:LT, t, HG * g + j, :],
                                  pexp[g % 2][0:LT, t, T * j:T * j + T], t == 0, t == KT - 1)
                last.then_inc(pv_ps, 1)

            @batch
            def t_oT(b):
                pe.wait_ge(o_evac, b + 1)
                if b == 0:
                    pe.wait_ge(w_evac, 7)
                if b >= 1:
                    pe.wait_ge(x2_ready, b)
                for g in range(NG):
                    last = tr(pC[0:T, 128 * g:128 * g + 128], osb[:, T * g:T * g + T], idf)
                last.then_inc(oT_ps, 1)

            @batch
            def t_onT(b):
                pe.wait_ge(on_ready, b + 1)
                for k in range(DC):
                    last = tr(pC[:, T * k:T * k + T], on[:, 128 * k:128 * k + 128], idf)
                last.then_inc(onT_ps, 1)

            @batch
            def t_oproj(b):
                pe.wait_ge(onT_sb, b + 1)
                for k in range(DC):
                    last = mm(pC[0:T, 0:D], onT[:, k, :], WoT[:, k, :], k == 0, k == DC - 1)
                last.then_inc(oproj_ps, 1)

            @batch
            def t_xqT(b):
                pe.wait_ge(xq_ready, b + 1)
                for k in range(DC):
                    tr(pCb[:, T * k:T * k + T], xq[:, 128 * k:128 * k + 128], idb)
                mm(pC[:, 128:128 + T], onesf[0:T, :], dg[:, :], True, True).then_inc(xqT_ps, 1)

            @batch
            def t_h(b, half):
                pe.wait_ge(xqT_sb, b + 1)
                if b >= 1 or half:
                    pe.wait_ge(h_evac, 2 * b + half)
                for m in range(M0 // 2):
                    for k in range(DC):
                        f = (half * M0 // 2 + m) * 128
                        last = mm(pC[:, T * m:T * m + T], w1T[:, k, f:f + 128], xqT[:, k, :], k == 0, k == DC - 1)
                last.then_inc(h_ps, 1)

            @batch
            def t_amcT(b):
                pe.wait_ge(amc_ready, b + 1)
                tr(pC[0:T, 0:128], amc[:, :], idf).then_inc(amcT_ps, 1)

            @batch
            def t_dg2(b):
                pe.wait_ge(dg2_ready, b + 1)
                mm(pC[:, 128:128 + T], onesf[0:T, :], dg[:, :], True, True).then_inc(dg2_ps, 1)

            @batch
            def t_down(b):
                pe.wait_ge(hq_ready, b + 1)
                for m in range(M0):
                    last = mm(pC[0:T, 0:D], hq[:, m, :], w2T[:, m, :], m == 0, m == M0 - 1)
                last.then_inc(f_ps, 1)

            @batch
            def u_xn2T(b):
                pe.wait_ge(xn2_ready, b + 1)
                if b == 0:
                    pe.wait_ge(bo_made, 1)
                if b >= 1:
                    pe.wait_ge(lg_ready, b)
                for k in range(DC):
                    last = tr(pU[:, T * k:T * k + T], xm[:, 128 * k:128 * k + 128], idf)
                last.then_inc(xn2T_ps, 1)

            @batch
            def u_t(b):
                if b == 0:
                    pe.wait_ge(const_loaded, 16 * 8)
                pe.wait_ge(xn2T_sb, b + 1)
                for m in range(DC):
                    for k in range(DC):
                        last = mm(pU[:, T * m:T * m + T], Wa[:, k, 128 * m:128 * m + 128], xn2T[:, k, :], k == 0, k == DC - 1)
                last.then_inc(t_ps, 1)

            @batch
            def u_sc(b):
                pe.wait_ge(t_sb, b + 1)
                for k in range(DC):
                    last = mm(pU[0:T, 0:L], tT[:, k, :], cxT[b % 3][:, k, :], k == 0, k == DC - 1)
                last.then_inc(sc_ps, 1)

            @batch
            def u_alT(b):
                pe.wait_ge(al_ready, b + 1)
                for t in range(KT):
                    last = tr(pU[0:LT, T * t:T * t + T], al[:, LT * t:LT * t + LT], idf)
                last.then_inc(alT_ps, 1)

            @batch
            def u_c(b):
                pe.wait_ge(alT_sb, b + 1)
                pe.wait_ge(cxt_loaded, 16 * (b + 1))
                for m in range(DC):
                    for t in range(KT):
                        last = mm(pU[:, T * m:T * m + T], cx_t[:, t, 128 * m:128 * m + 128], alT[:, t, :], t == 0, t == KT - 1)
                last.then_inc(c_ps, 1)

            @batch
            def u_wc(b):
                pe.wait_ge(c_sb, b + 1)
                for k in range(2 * DC):
                    last = mm(pU[0:T, 0:D], cT[:, k, :] if k < DC else xn2T[:, k - DC, :], WcT[:, k, :],
                              k == 0, k == 2 * DC - 1)
                last.then_inc(wc_ps, 1)

            @batch
            def u_router(b):
                pe.wait_ge(xn3_ready, b + 1)
                pe.wait_ge(thx_ready, b + 1)
                for k in range(DC):
                    last = tr(pU[:, T * k:T * k + T], xm[:, 128 * k:128 * k + 128], idf)
                last.then_inc(xn3T_ps, 1)
                pe.wait_ge(xn3T_sb, b + 1)
                for k in range(DC):
                    last = mm(pU[0:T, 256:256 + NE], cT[:, k, :], Wr[:, k, :], k == 0, k == DC - 1)
                last.then_inc(r_ps, 1)

            for i in range(-1, B + 3):
                t_down(i - 3)
                w_tr(i - 1, 5)
                a_scoresT(i - 2, 3)
                w_tr(i - 1, 6)
                p_cxT(i)
                a_pv(i - 2, 2)
                u_xn2T(i - 3)
                a_pv(i - 2, 3)
                u_t(i - 3)
                t_oT(i - 2)
                u_sc(i - 3)
                a_scores(i - 1, 0)
                t_onT(i - 2)
                a_scores(i - 1, 1)
                a_scores(i - 1, 2)
                t_oproj(i - 2)
                p_k(i)
                a_scores(i - 1, 3)
                w_bo(i - 1)
                w_sum(i)
                for n in range(4, 8):
                    a_scores(i - 1, n)
                w_tr(i, 0)
                p_vq(i)
                a_scores(i - 1, 8)
                t_xqT(i - 2)
                u_alT(i - 3)
                a_scores(i - 1, 9)
                a_scores(i - 1, 10)
                t_h(i - 2, 0)
                w_tr(i, 1)
                for n in range(11, 14):
                    a_scores(i - 1, n)
                t_h(i - 2, 1)
                a_scores(i - 1, 14)
                a_scores(i - 1, 15)
                a_max(i - 1)
                u_c(i - 3)
                u_wc(i - 3)
                a_scoresT(i - 1, 0)
                t_amcT(i - 2)
                a_scoresT(i - 1, 1)
                a_pv(i - 1, 0)
                a_scoresT(i - 1, 2)
                t_dg2(i - 2)
                a_pv(i - 1, 1)
                w_tr(i, 2)
                u_router(i - 3)
                w_tr(i, 3)
                w_tr(i, 4)
            pe.wait_ge(filled, 1)
            pe.wait_ge(m_oh, 1)
            pe.wait_ge(x2_ready, B)
            mm(pC[0:T, 0:B * NE], tri[0:T, 0:T], ohb.rearrange("t b e -> t (b e)"), True, False)
            for b in range(B - 1):
                n = B - 1 - b
                mm(pC[0:T, (b + 1) * NE:B * NE], onesb[0:T, 0:T], ohb[:, b:b + 1, :].to_broadcast([T, n, NE]), False, n == 1)
            for b in range(B):
                last = mm(pC[:, B * NE:B * NE + NE], onesb[0:T, :], ohb[:, b, :], b == 0, b == B - 1)
            last.then_inc(cnt_ps, 1)
            pe.wait_ge(m_slots, 1)

            def e_xT(j):
                pe.wait_ge(xs_loaded[j % 4], 16 * (j // 4 + 1))
                if j >= 1:
                    pe.wait_ge(xT_sb, j)
                for k in range(DC):
                    last = tr(pC[:, 128 * k:128 * k + 128], xsb[:, j % 4, 128 * k:128 * k + 128], idf)
                last.then_inc(xT_ps, 1)

            def e_up(j):
                e = expert(j)
                pe.wait_ge(xT_sb, j + 1)
                if j >= 2:
                    pe.wait_ge(gelu_done, 2 * (j - 1))
                for n in range(F1 // 512):
                    o = ps[:, 2 * (j % 2) + n, :]
                    mm(o, selx[:, j, :], ebt[:, 512 * n:512 * n + 512], True, False)
                    for k in range(DC):
                        last = mm(o, xsT[:, j % 2, k, :], late[:, bass.ds(e * EW + k * F1 + 512 * n, 512)], False, k == DC - 1)
                    last.then_inc(h1_ps, 1)

            def e_hT(j):
                for n in range(2):
                    pe.wait_ge(gelu_done, 2 * j + n + 1)
                    if j >= 1:
                        pe.wait_ge(hT_sb, 2 * (j - 1) + n + 1)
                    for f in range(M1 // 2):
                        g = n * M1 // 2 + f
                        last = tr(pAB[:, n, 128 * f:128 * f + 128], hx[:, j % 2, 128 * g:128 * g + 128], idf)
                    last.then_inc(hT_ps, 1)

            def e_down(j):
                e = expert(j)
                if j >= 1:
                    pe.wait_ge(y_sb, j)
                mm(pO[:, 0:D], selx[:, j, :], ebt[:, F1:FB], True, False)
                for f in range(M1):
                    if f % 4 == 0:
                        pe.wait_ge(hT_sb, 2 * j + f // 4 + 1)
                    last = mm(pO[:, 0:D], hxT[:, j % 2, f, :], late[:, bass.ds(e * EW + DC * F1 + f * D, D)], False, f == M1 - 1)
                last.then_inc(y_ps, 1)

            def expert(j):
                return pe.value_load(ebi[0:1, j:j + 1], min_val=0, max_val=NE - 1)

            e_xT(0)
            pe.wait_ge(sel_ready, 1)
            pe.wait_ge(ebt_loaded, 16)
            pe.wait_ge(w_loaded, 16 * 2 * NE)
            total = blocks(pe)
            e_up(0)
            e_xT(1)
            for j in range(NB):
                if j + 1 < NB:
                    with filled_block(pe, total, j + 1):
                        e_up(j + 1)
                        if j + 2 < NB:
                            e_xT(j + 2)
                with filled_block(pe, total, j):
                    e_hT(j)
                    e_down(j)

        @block.scalar
        def _(act):
            def copy(dst, src):
                return act.activation(dst, src, ACT.Copy)

            def load_expert(e):
                act.dma_start(W[:, e, 0:DC * F1].rearrange("p (k f) -> p k f", k=DC),
                              A["L1_ffn_W1"][e].rearrange("(k p) f -> p k f", p=128)).then_inc(w_loaded, 16)
                act.dma_start(W[:, e, DC * F1:EW].rearrange("p (m d) -> p m d", m=M1),
                              A["L1_ffn_W2"][e].rearrange("(m p) d -> p m d", p=128)).then_inc(w_loaded, 16)

            for i, (n, cols) in enumerate((("L1_ffn_b1", slice(0, F1)), ("L1_ffn_b2", slice(F1, FB)))):
                act.dma_start(ebn[:, cols], A[n]).then_inc(eb_loaded, 16)
            act.dma_start(brow[0:1, 0], A["L0_xcond_bq"].unsqueeze(0)).then_inc(bias_loaded, 16)
            act.dma_start(brow[0:1, 1], A["L0_xcond_bk"].unsqueeze(0)).then_inc(bias_loaded, 16)
            for n, (w, dst) in enumerate(((1, WkT), (0, WqT))):
                act.wait_ge(tr_qkv, n + 1)
                for k in range(DC):
                    last = copy(dst[:, k, :, :].rearrange("p m (d h) -> p m d h", h=HM),
                                ps[:, w, k * D:k * D + D].rearrange("p (m h d) -> p m d h", m=DC, h=HM))
                last.then_inc(qkvT_sb, 1)
            act.wait_ge(tr_qkv, 3)
            copy(WvT[:, :, :].rearrange("p k d -> p (k d)"), ps[:, 2, :]).then_inc(qkvT_sb, 1)
            act.dma_start(tau[:, :], A["condB_tau"].partition_broadcast(128)).then_inc(const_loaded, 16)
            act.dma_start(bv[:, :], A["L0_xcond_bv"].rearrange("(k p) -> p k", p=128),
                          allow_slow_non_contiguous=True).then_inc(const_loaded, 16)
            act.dma_start(bo_b[:, :], A["L0_xcond_bo"].partition_broadcast(T)).then_inc(const_loaded, 16)
            act.dma_start(br_b[:, :], A["L1_ffn_br"].partition_broadcast(T)).then_inc(const_loaded, 16)
            act.dma_start(cw[:, :, :], A["L0_ffn_conv_w"].rearrange("(m p) o j -> p m (o j)", p=128)).then_inc(const_loaded, 16)
            act.dma_start(cb[:, :], A["L0_ffn_conv_b"].rearrange("(m p) -> p m", p=128),
                          allow_slow_non_contiguous=True).then_inc(const_loaded, 16)
            act.dma_start(Wa[:, :, :], A["L1_xcond_W_a"].rearrange("(m p) d -> p m d", p=128)).then_inc(const_loaded, 16)
            act.dma_start(Wr[:, :, :], A["L1_ffn_Wr"].rearrange("(m p) d -> p m d", p=128)).then_inc(const_loaded, 16)

            @batch
            def w_gauss(b):
                if b == 0:
                    act.wait_ge(mask_made, 1)
                    act.activation(prep8[:, 5, :], prep8[:, 2, :], ACT.Exp, scale=-1.0 / 128.0).then_inc(gauss_made, 1)

            @batch
            def w_sb(b, n):
                if b == 0:
                    act.wait_ge(tr_w, n + 1)
                    bank = (pC, pU)[n % 2]
                    if n < 2:
                        dst = WcT[:, 2 * n:2 * n + 2, :].rearrange("p k d -> p (k d)")
                    elif n == 2:
                        dst = WoT[:, :, :].rearrange("p k d -> p (k d)")
                    elif n < 5:
                        dst = w1T[:, n - 3, :]
                    else:
                        dst = w2T[:, 4 * (n - 5):4 * (n - 5) + 4, :].rearrange("p m d -> p (m d)")
                    copy(dst, bank if n < 3 else bank.bitcast(bf16)).then_inc(w_evac, 1)

            @batch
            def w_early(b):
                if b < 3:
                    if b == 0:
                        act.wait_ge(w_evac, 7)
                        act.wait_ge(eb_written, 16)
                    load_expert(b)

            @batch
            def w_late(b):
                if b == B - 1:
                    act.wait_ge(pv_ps, NG * B)
                    act.wait_ge(nm_loaded, 16 * B)
                    for e in range(3, NE - 1):
                        load_expert(e)

            @batch
            def w_last(b):
                if b == B - 1:
                    act.wait_ge(x2_ready, B)
                    load_expert(NE - 1)

            @batch
            def p_cxT(b):
                act.wait_ge(xn0T_ps, b + 1)
                if b >= 3:
                    act.wait_ge(v_ps, b - 2)
                    act.wait_ge(sc_ps, b - 2)
                copy(cxT[b % 3][:, :, :], pAB[:, :, 0:L]).then_inc(cxT_sb, 1)
                if b >= 1:
                    act.wait_ge(q_ps, b)
                copy(xn0T[:, :, :], pAB[:, :, 384:384 + T]).then_inc(xn0T_sb, 1)

            @batch
            def p_kf(b):
                if b == 0:
                    act.wait_ge(bk4_made, 1)
                act.wait_ge(k_ps, b + 1)
                if b >= 1:
                    act.wait_ge(kr_made, b)
                for m in range(DC):
                    last = act.activation(kf[:, m, :], pAB[:, m, 0:L], ACT.Identity, bias=bk4[:, m:m + 1], scale=0.25)
                last.then_inc(k_evac, 1)
                act.wait_ge(k_evac, b + 1)
                if b >= 1:
                    act.wait_ge(k_written, 16 * b)
                copy(kt3[:, :, 0, :], kf).then_inc(kh_made, 1)

            @batch
            def p_km(b):
                act.wait_ge(kr_made, b + 1)
                copy(kt3[:, :, 1, :], kr).then_inc(km_made, 1)

            @batch
            def p_v(b):
                act.wait_ge(q_ps, b + 1)
                act.wait_ge(q_evac, b + 1)
                if b == 0:
                    act.wait_ge(filled, 3)
                if b >= 2:
                    act.wait_ge(pv_ps, NG * (b - 1))
                for t in range(KT):
                    last = copy(vaug[b % 2][0:LT, t, :, 0:DK],
                                pAB[0:LT, t // 2, (t % 2) * D:(t % 2) * D + D].rearrange("p (h c) -> p h c", c=DK))
                last.then_inc(v_evac, 1)

            @batch
            def p_qh(b):
                act.wait_ge(q_evac, b + 1)
                if b >= 1:
                    act.wait_ge(q_written, 16 * b)
                copy(qt3[:, :, 0, :], qf[:, :, :]).then_inc(qh_made, 1)

            @batch
            def p_qm(b):
                act.wait_ge(qr_made, b + 1)
                copy(qt3[:, :, 1, :], qr[:, :, :]).then_inc(qm_made, 1)

            @batch
            def a_exp(b, g):
                for t in range(KT):
                    n = KT * g + t
                    act.wait_ge(st_ps, KT * NG * b + n + 1)
                    if b >= 1 or g >= 2:
                        act.wait_ge(pv_ps, NG * b + g - 1)
                    act.activation(pexp[g % 2][0:LT, t, :], pS[n % 3][0:LT, 0:HG * T], ACT.Exp).then_inc(exp_done, 1)

            @batch
            def t_osb(b):
                act.wait_ge(pv_ps, NG * (b + 1))
                if b >= 1:
                    act.wait_ge(oT_ps, b)
                copy(osb[:, :], pO[:, 0:HG * T]).then_inc(o_evac, 1)

            @batch
            def t_onT(b):
                act.wait_ge(onT_ps, b + 1)
                if b >= 1:
                    act.wait_ge(oproj_ps, b)
                copy(onT[:, :, :], pC[:, 0:DC * T].rearrange("p (k t) -> p k t", k=DC)).then_inc(onT_sb, 1)

            @batch
            def t_xqT(b):
                act.wait_ge(xqT_ps, b + 1)
                if b >= 1:
                    act.wait_ge(h_ps, 2 * b)
                if b >= 1:
                    act.wait_ge(h_evac, 2 * b)
                copy(xqT[:, :, :], pCb[:, 0:DC * T].rearrange("p (k t) -> p k t", k=DC))
                copy(stB[:, :], pC[:, 128:128 + T]).then_inc(xqT_sb, 1)

            @batch
            def t_center(b, half):
                if b == 0 and half == 0:
                    act.wait_ge(const_loaded, 16 * 8)
                act.wait_ge(h_evac, 2 * b + half + 1)
                if b >= 1:
                    act.wait_ge(g_made, 2 * b)
                for m in range(half * M0 // 2, (half + 1) * M0 // 2):
                    last = act.activation(yc[:, m, :], hs[:, m, 1:1 + T], ACT.Identity, bias=cb[:, m:m + 1], scale=cw[:, m, 1:2])
                last.then_inc(yc_done, 1)

            @batch
            def t_tanh(b, half):
                act.wait_ge(y_ready, 2 * b + half + 1)
                if b >= 1:
                    act.wait_ge(hq_ready, b)
                ms = slice(half * M0 // 2, (half + 1) * M0 // 2)
                act.activation(th[:, ms, :], yc[:, ms, :], ACT.Tanh, scale=0.5).then_inc(th_ready, 1)

            @batch
            def u_xn2T(b):
                act.wait_ge(xn2T_ps, b + 1)
                if b >= 1:
                    act.wait_ge(wc_ps, b)
                copy(xn2T[:, :, :], pU[:, 0:DC * T].rearrange("p (k t) -> p k t", k=DC)).then_inc(xn2T_sb, 1)

            @batch
            def u_t(b):
                act.wait_ge(t_ps, b + 1)
                if b >= 1:
                    act.wait_ge(sc_ps, b)
                copy(tT[:, :, :], pU[:, 0:DC * T].rearrange("p (k t) -> p k t", k=DC)).then_inc(t_sb, 1)

            @batch
            def u_e(b):
                act.wait_ge(sc_done, b + 1)
                if b >= 1:
                    act.wait_ge(al_ready, b)
                act.activation(al[:, :], scr, ACT.Exp, bias=tiny[:, 8:9], accum_out=tiny[:, 9:10]).then_inc(e_ready, 1)

            @batch
            def u_alT(b):
                act.wait_ge(alT_ps, b + 1)
                if b >= 1:
                    act.wait_ge(c_ps, b)
                copy(alT[:, :, :], pU[0:LT, 0:KT * T].rearrange("p (k t) -> p k t", k=KT)).then_inc(alT_sb, 1)

            @batch
            def u_c(b):
                act.wait_ge(c_ps, b + 1)
                if b >= 1:
                    act.wait_ge(r_ps, b)
                copy(cT[:, :, :], pU[:, 0:DC * T].rearrange("p (k t) -> p k t", k=DC)).then_inc(c_sb, 1)

            @batch
            def u_thx(b):
                act.wait_ge(wc_ps, b + 1)
                if b >= 1:
                    act.wait_ge(x3_ready, b)
                act.activation(thx[:, :], pU[0:T, 0:D], ACT.Tanh).then_inc(thx_ready, 1)

            @batch
            def u_router(b):
                act.wait_ge(xn3T_ps, b + 1)
                copy(cT[:, :, :], pU[:, 0:DC * T].rearrange("p (k t) -> p k t", k=DC)).then_inc(xn3T_sb, 1)

            for i in range(-1, B + 3):
                t_osb(i - 2)
                w_sb(i - 1, 2)
                u_t(i - 3)
                t_onT(i - 2)
                for n in range(3, 6):
                    w_sb(i - 1, n)
                w_last(i - 3)
                w_sb(i - 1, 6)
                w_early(i - 2)
                w_late(i - 2)
                p_cxT(i)
                u_e(i - 3)
                p_kf(i)
                p_km(i)
                t_xqT(i - 2)
                u_alT(i - 3)
                w_gauss(i)
                t_center(i - 2, 0)
                t_center(i - 2, 1)
                u_c(i - 3)
                t_tanh(i - 2, 0)
                t_tanh(i - 2, 1)
                u_thx(i - 3)
                a_exp(i - 1, 0)
                a_exp(i - 1, 1)
                p_v(i)
                p_qh(i)
                w_sb(i, 0)
                u_router(i - 3)
                p_qm(i)
                a_exp(i - 1, 2)
                a_exp(i - 1, 3)
                w_sb(i, 1)
                u_xn2T(i - 2)
            act.wait_ge(m_d, 1)
            act.activation(m_e3, m_d3, ACT.Exp).then_inc(m_e, 1)
            act.wait_ge(sel_ready, 1)
            total = blocks(act)
            for j in range(NB):
                with filled_block(act, total, j):
                    for n in range(2):
                        act.wait_ge(h1_ps, 2 * j + n + 1)
                        if j >= 2:
                            act.wait_ge(hT_ps, 2 * (j - 2) + n + 1)
                        act.activation(hx[:, j % 2, 512 * n:512 * n + 512], ps[:, 2 * (j % 2) + n, :], ACT.Gelu)\
                           .then_inc(gelu_done, 1)

        @block.gpsimd
        def _(pool):
            pool.memset(idf[:, :], 0.0)
            pool.memset(idb[:, :], 0.0)
            pool.memset(onesf[:, :], 1.0)
            pool.memset(onesb[:, :], 1.0)
            pool.memset(tri, 1.0)
            pool.memset(expo[:, :], -0.5).then_inc(ones_made, 1)
            pool.iota(prep8[:, 1, :], [[1, L]], base=0, channel_multiplier=0, allow_small_or_imprecise_dtypes=True)\
                .then_inc(iota_made, 1)
            pool.wait_ge(ones_made, 1)
            for m in (idf, idb):
                last = pool.affine_select(out=m[:, :], in_=m[:, :], compare_op=ALU.not_equal, fill=1.0, base=0,
                                          pattern=[[-1, 128]], channel_multiplier=1)
            last.then_inc(idents, 1)
            pool.affine_select(out=tri, in_=tri, compare_op=ALU.is_gt, fill=0.0, base=0,
                               pattern=[[1, T]], channel_multiplier=-1).then_inc(filled, 1)
            @batch
            def w_fill(b, n):
                if b == 0:
                    pool.wait_ge(filled, n)
                    if n == 1:
                        pool.wait_ge(ln_rstd[0], 1)
                        for i in range(2):
                            pool.memset(kst[i][96:128, :, :], 1.0)
                            last = pool.memset(qst[i][96:128, :, :], 1.0)
                    if n == 2:
                        for i in range(2):
                            last = pool.memset(vaug[i][:, :, :, :], 1.0)
                    if n == 3:
                        last = pool.memset(zero, 0.0)
                    last.then_inc(filled, 1)
                    pool.wait_ge(filled, n + 1)

            @batch
            def w_eb(b, n):
                if b == 0:
                    if n == 0:
                        pool.wait_ge(eb_loaded, 32)
                        pool.tensor_copy(eb3[:, 0, :], ebn).then_inc(eb_step, 1)
                    if n == 1:
                        pool.wait_ge(eb_step, 1)
                        pool.tensor_tensor(ebn, ebn, eb3[:, 0, :], ALU.subtract).then_inc(eb_step, 1)
                    if n == 2:
                        pool.wait_ge(eb_step, 2)
                        pool.tensor_copy(eb3[:, 1, :], ebn).then_inc(eb_step, 1)
                    if n == 3:
                        pool.wait_ge(eb_step, 3)
                        pool.tensor_tensor(eb3[:, 2, :], ebn, eb3[:, 1, :], ALU.subtract).then_inc(eb_made, 1)

            @batch
            def rstd_of(b, which):
                pool.wait_ge(ln_in[which], b + 1)
                pool.tensor_tensor(rstd[:, which:which + 1], ve[:, which:which + 1], expo[0:T, :], ALU.pow)\
                    .then_inc(ln_rstd[which], 1)

            @batch
            def p_kr(b):
                pool.wait_ge(kh_made, b + 1)
                if b >= 1:
                    pool.wait_ge(km_made, b)
                pool.tensor_tensor(kr, kf, kt3[:, :, 0, :], ALU.subtract).then_inc(kr_made, 1)

            @batch
            def p_kl(b):
                pool.wait_ge(km_made, b + 1)
                pool.tensor_tensor(kt3[:, :, 2, :], kr, kt3[:, :, 1, :], ALU.subtract).then_inc(kt3_ready, 1)

            @batch
            def p_qr(b):
                pool.wait_ge(qh_made, b + 1)
                if b >= 1:
                    pool.wait_ge(qm_made, b)
                pool.tensor_tensor(qr[:, :, :], qf[:, :, :], qt3[:, :, 0, :], ALU.subtract).then_inc(qr_made, 1)

            @batch
            def p_ql(b):
                pool.wait_ge(qm_made, b + 1)
                pool.tensor_tensor(qt3[:, :, 2, :], qr[:, :, :], qt3[:, :, 1, :], ALU.subtract).then_inc(qt3_ready, 1)

            @batch
            def p_x0b(b):
                if b == 0:
                    pool.wait_ge(bo_made, 1)
                pool.wait_ge(xn0_ready, b + 1)
                if b >= 2:
                    pool.wait_ge(x1_done, b - 1)
                pool.tensor_tensor(x0b[b % 2][:, :], x0[b % 2][:, :], bo_b[:, :], ALU.add).then_inc(x0b_ready, 1)

            @batch
            def u_x3(b):
                if b == 0:
                    pool.wait_ge(zeroed, 16)
                pool.wait_ge(thx_ready, b + 1)
                if b >= 1:
                    pool.wait_ge(x3_stored, 16 * b)
                pool.tensor_tensor(x3, x2[:, :], thx[:, :], ALU.add).then_inc(x3_ready, 1)

            for i in range(-1, B + 3):
                u_x3(i - 3)
                w_fill(i, 2)
                w_fill(i, 3)
                rstd_of(i - 3, 3)
                p_qr(i)
                rstd_of(i + 1, 0)
                p_ql(i)
                rstd_of(i - 2, 2)
                rstd_of(i - 1, 1)
                for n in range(0, 4):
                    w_eb(i, n)
                w_fill(i + 1, 1)
                p_kr(i + 1)
                p_kl(i + 1)
                p_x0b(i)
            pool.wait_ge(x2_ready, B)
            pool.iota(w8, [[0, B], [-1, NE]], base=NE, channel_multiplier=0, allow_small_or_imprecise_dtypes=True)
            pool.iota(thr, [[0, NE], [128, NB - NE + 1]], base=0, channel_multiplier=0, allow_small_or_imprecise_dtypes=True)
            pool.iota(jix, [[1, NB], [0, NE - 1]], base=0, channel_multiplier=0, allow_small_or_imprecise_dtypes=True)
            pool.iota(earlier, [[1, NE], [-1, NE]], base=0, channel_multiplier=0, allow_small_or_imprecise_dtypes=True)
            pool.iota(ecol, [[0, 1]], base=0, channel_multiplier=1, allow_small_or_imprecise_dtypes=True)
            pool.iota(xall[:, :, XW - 1], [[-T, B]], base=NT, channel_multiplier=-1, allow_small_or_imprecise_dtypes=True)\
                .then_inc(m_iota, 1)
            pool.wait_ge(m_slots, 1)
            pool.wait_ge(mx_loaded, 64)
            pool.wait_ge(zeroed, 16)
            for b in range(B):
                pool.indirect_dma_start(d_xs, bass.IndirectOffsetOnAxis(ap=mi[:, b:b + 1], axis=0), xall[:, b, :], None)\
                    .then_inc(scattered, 16)
            pool.wait_ge(sel_ready, 1)
            total = blocks(pool)
            for j in range(NB):
                with filled_block(pool, total, j):
                    pool.wait_ge(y_sb, j + 1)
                    pool.indirect_dma_start(out.rearrange("b t d -> (b t) d"),
                                            bass.IndirectOffsetOnAxis(ap=tid[:, j % 4:j % 4 + 1], axis=0),
                                            ysb[:, j % 2, :], None, bounds_check=NT - 1, oob_is_err=False)\
                        .then_inc(y_stored, 16)
                    pool.wait_ge(y_stored, 16 * (j + 1))

        @block.vector
        def _(dve):
            steps = [0]

            def step(ins):
                steps[0] += 1
                ins.then_inc(dve_step, 1)
                dve.wait_ge(dve_step, steps[0])

            def tt(o, a, b, op):
                return dve.tensor_tensor(o, a, b, op)

            def ts(o, a, s1, s2, op0, op1):
                return dve.tensor_scalar(o, a, s1, s2, op0, op1)

            dve.wait_ge(prep_loaded, 16)
            step(ts(prep8[:, 2, :], prep8[:, 0, :], 0.25, None, ALU.mult, ALU.bypass))
            step(dve.tensor_copy(prepb[:, 0, :], prep8[:, 2, :]))
            step(tt(prep8[:, 2, :], prep8[:, 2, :], prepb[:, 0, :], ALU.subtract))
            step(dve.tensor_copy(prepb[:, 1, :], prep8[:, 2, :]))
            tt(prepb[:, 2, :], prep8[:, 2, :], prepb[:, 1, :], ALU.subtract).then_inc(delta_made, 1)
            dve.wait_ge(bias_loaded, 32)
            dve.tensor_copy(bperm[0:1, :, :].rearrange("o w (m d h) -> o (w m) d h", m=DC, h=HM),
                            brow[0:1, :, :].rearrange("o w (m h d) -> o (w m) d h", m=DC, h=HM)).then_inc(bperm_made, 1)
            dve.wait_ge(prep_ps, 1)
            dve.tensor_copy(bq[:, :], pO[:, 0:2])
            ts(bk4[:, :], pO[:, 2:4], 0.25, None, ALU.mult, ALU.bypass).then_inc(bk4_made, 1)

            @batch
            def w_mask(b):
                if b == 0:
                    dve.wait_ge(win_loaded, 32)
                    dve.wait_ge(iota_made, 1)
                    dve.wait_ge(delta_made, 1)
                    step(dve.tensor_copy(prepc[:, 1:2], prepi[:, :]))
                    step(ts(prepc[:, 2:3], prepc[:, 0:1], 16.0, 0.0, ALU.subtract, ALU.max))
                    step(ts(prepc[:, 3:4], prepc[:, 0:1], 16.0, prepc[:, 1:2], ALU.add, ALU.min))
                    step(ts(prep8[:, 3, :], prep8[:, 1, :], prepc[:, 2:3], None, ALU.is_ge, ALU.bypass))
                    step(dve.scalar_tensor_tensor(prep8[:, 3, :], prep8[:, 1, :], prepc[:, 3:4], prep8[:, 3, :], ALU.is_le, ALU.mult))
                    step(ts(prep8[:, 4, :], prep8[:, 3, :], 1.0, 1e9, ALU.subtract, ALU.mult))
                    step(ts(prep8[:, 2, :], prep8[:, 1, :], prepc[:, 0:1], None, ALU.subtract, ALU.bypass))
                    tt(prep8[:, 2, :], prep8[:, 2, :], prep8[:, 2, :], ALU.mult).then_inc(mask_made, 1)

            @batch
            def w_sum(b, i):
                if b == 0 and i < 2:
                    dve.wait_ge(f_loaded, 32)
                    dve.tensor_reduce(wsum[:, i:i + 1], nat_f[i], X, ALU.add, apply_absolute_value=True).then_inc(wsum_made, 1)
                if b == 0 and i == 2:
                    dve.wait_ge(prep_ps, 2)
                    step(ts(wscl[:, 0, :], pU[:, 0:2], 1.0 / (F0 * D), 1e-5, ALU.mult, ALU.max))
                    dve.reciprocal(wscl[:, 1, :], wscl[:, 0, :]).then_inc(wscl_made, 1)

            @batch
            def w_bo(b):
                if b == 0:
                    dve.wait_ge(const_loaded, 16 * 8)
                    dve.wait_ge(prep_ps, 3)
                    tt(bo_b[:, :], bo_b[:, :], pU[0:T, 0:D], ALU.add).then_inc(bo_made, 1)

            @batch
            def w_quant(b, i, part):
                if b == 0:
                    if part == 0:
                        dve.wait_ge(wscl_made, 1)
                        step(ts(qw_a[i], nat_f[i], wscl[:, 1, i:i + 1], MAGIC, ALU.mult, ALU.add))
                    if part == 1:
                        step(ts(qw_a[i], qw_a[i], MAGIC, 1.0, ALU.subtract, ALU.min))
                    if part == 2:
                        ts(qw_b[i], qw_a[i], -1.0, None, ALU.max, ALU.bypass).then_inc(quant, 1)

            def ln_stats(x, which):
                step(dve.bn_stats(bst[:, which, :], x))
                step(dve.bn_aggr(mv[:, which, :], bst[:, which, :]))
                ts(ve[:, which:which + 1], mv[:, which, 1:2], EPS, None, ALU.add, ALU.bypass).then_inc(ln_in[which], 1)

            def ln(x, which, b, o):
                dve.wait_ge(ln_rstd[which], b + 1)
                return ts(o, x, mv[:, which, 0:1], rstd[:, which:which + 1], ALU.subtract, ALU.mult)

            @batch
            def p_stats(b):
                dve.wait_ge(x_loaded, 16 * (b + 1))
                ln_stats(x0[b % 2][:, :], 0)

            @batch
            def p_ln(b):
                if b >= 1:
                    dve.wait_ge(xn0T_ps, b)
                ln(x0[b % 2][:, :], 0, b, xn0[:, :]).then_inc(xn0_ready, 1)

            @batch
            def p_q(b):
                dve.wait_ge(q_ps, b + 1)
                if b == 0:
                    dve.wait_ge(const_loaded, 16 * 8)
                if b >= 1:
                    dve.wait_ge(qr_made, b)
                for m in range(DC):
                    last = ts(qf[:, m, :], pAB[:, 1, D + T * m:D + T * m + T], bq[:, m:m + 1], tau[:, b:b + 1],
                              ALU.add, ALU.mult)
                last.then_inc(q_evac, 1)

            @batch
            def a_max(b, h):
                dve.wait_ge(s_ps, NH * b + h + 1)
                dve.tensor_reduce(mx[:, h:h + 1], pS[h % 3][0:T, 0:L], X, ALU.max).then_inc(mx_done, 1)

            @batch
            def a_neg(b):
                dve.wait_ge(mx_done, NH * (b + 1))
                if b >= 1:
                    dve.wait_ge(nmT_ps, b)
                step(ts(nm[:, 0, :], mx[:, :], -1.0, None, ALU.mult, ALU.bypass))
                step(dve.scalar_tensor_tensor(nr[:, :], mx[:, :], -1.0, nm[:, 0, :], ALU.mult, ALU.subtract))
                step(dve.tensor_copy(nm[:, 1, :], nr[:, :]))
                tt(nm[:, 2, :], nr[:, :], nm[:, 1, :], ALU.subtract).then_inc(nm_ready, 1)

            @batch
            def a_nmT(b):
                dve.wait_ge(nmT_ps, b + 1)
                if b >= 1:
                    dve.wait_ge(nm_written, 16 * b)
                dve.tensor_copy(nmT[:, :], pOb[0:3 * NH, 0:T]).then_inc(nmT_sb, 1)

            @batch
            @batch
            def t_norm(b):
                dve.wait_ge(oT_ps, b + 1)
                heads = pC[0:T, :].rearrange("t (h c) -> t h c", h=NH)
                dve.reciprocal(rs[:, :], heads[:, :, DK:DK + 1].rearrange("t h o -> t (h o)")).then_inc(recip_done, 1)
                dve.wait_ge(recip_done, b + 1)
                if b >= 1:
                    dve.wait_ge(onT_ps, b)
                tt(on[:, :].rearrange("t (h d) -> t h d", h=NH), heads[:, :, 0:DK],
                   rs[:, :].unsqueeze(2).to_broadcast([T, NH, DK]), ALU.mult).then_inc(on_ready, 1)

            def quant_scale(am, c0, half, w, b):
                step(ts(tiny[:, c0 + 2:c0 + 3], am, half, 1e-5, ALU.mult, ALU.max))
                step(dve.reciprocal(tiny[:, c0 + 3:c0 + 4], tiny[:, c0 + 2:c0 + 3]))
                ts(tiny[:, c0:c0 + 1], tiny[:, c0 + 3:c0 + 4], QMAX * half, None, ALU.mult, ALU.bypass)
                step(ts(tiny[:, c0 + 1:c0 + 2], tiny[:, c0 + 2:c0 + 3], 1.0 / QMAX, wscl[0:T, 0, w:w + 1], ALU.mult, ALU.mult))

            @batch
            def t_x1(b):
                dve.wait_ge(oproj_ps, b + 1)
                dve.wait_ge(x0b_ready, b + 1)
                tt(x1[:, :], pC[0:T, 0:D], x0b[b % 2][:, :], ALU.add).then_inc(x1_done, 1)
                dve.wait_ge(x1_done, b + 1)
                ln_stats(x1[:, :], 1)

            @batch
            def t_xq(b):
                if b == 0:
                    dve.wait_ge(w_evac, 7)
                    dve.memset(hs[:, :, 0:1], 0.0)
                    dve.memset(hs[:, :, T + 1:T + 2], 0.0)
                step(ln(x1[:, :], 1, b, xn[:, :]))
                step(dve.tensor_reduce(tiny[:, 4:5], xn[:, :], X, ALU.max, apply_absolute_value=True))
                quant_scale(tiny[:, 4:5], 0, 1.0, 0, b)
                step(ts(xn[:, :], xn[:, :], tiny[:, 0:1], MAGIC, ALU.mult, ALU.add))
                ts(xq[:, :], xn[:, :], MAGIC, QMAX, ALU.subtract, ALU.min)
                if b >= 1:
                    dve.wait_ge(dg2_ps, b)
                ts(dg[:, :], idf[0:T, 0:T], tiny[:, 1:2], None, ALU.mult, ALU.bypass).then_inc(xq_ready, 1)

            @batch
            def t_h(b, half):
                dve.wait_ge(xqT_sb, b + 1)
                dve.wait_ge(h_ps, 2 * b + half + 1)
                if b >= 1:
                    dve.wait_ge(yc_done, 2 * b)
                m0 = half * M0 // 2
                tt(hs[:, m0:m0 + M0 // 2, 1:1 + T], pC[:, 0:M0 // 2 * T].rearrange("p (m t) -> p m t", t=T),
                   stB[:, :].unsqueeze(1).to_broadcast([128, M0 // 2, T]), ALU.mult).then_inc(h_evac, 1)

            @batch
            def t_conv(b, half):
                dve.wait_ge(h_evac, 2 * b + half + 1)
                dve.wait_ge(yc_done, 2 * b + half + 1)
                ms = range(half * M0 // 2, (half + 1) * M0 // 2)
                for m in ms:
                    last = dve.scalar_tensor_tensor(yc[:, m, :], hs[:, m, 0:T], cw[:, m, 0:1], yc[:, m, :],
                                                    ALU.mult, ALU.add)
                step(last)
                for m in ms:
                    last = dve.scalar_tensor_tensor(yc[:, m, :], hs[:, m, 2:2 + T], cw[:, m, 2:3], yc[:, m, :],
                                                    ALU.mult, ALU.add)
                last.then_inc(y_ready, 1)

            @batch
            def t_silu(b, half):
                dve.wait_ge(th_ready, 2 * b + half + 1)
                ms = slice(half * M0 // 2, (half + 1) * M0 // 2)
                dve.scalar_tensor_tensor(th[:, ms, :], th[:, ms, :], 1.0, yc[:, ms, :], ALU.add, ALU.mult).then_inc(g_made, 1)

            @batch
            def t_amax(b):
                dve.wait_ge(g_made, 2 * b + 2)
                if b >= 1:
                    dve.wait_ge(amcT_ps, b)
                dve.tensor_reduce(amc[:, :], th.rearrange("p m t -> p t m"), X, ALU.max, apply_absolute_value=True)\
                   .then_inc(amc_ready, 1)

            @batch
            def t_q2(b):
                dve.wait_ge(amcT_ps, b + 1)
                step(dve.tensor_reduce(tiny[:, 5:6], pC[0:T, 0:128], X, ALU.max))
                quant_scale(tiny[:, 5:6], 10, 0.5, 1, b)
                ts(dg[:, :], idf[0:T, 0:T], tiny[:, 10:11], None, ALU.mult, ALU.bypass).then_inc(dg2_ready, 1)

            @batch
            def t_hq(b):
                dve.wait_ge(dg2_ps, b + 1)
                if b >= 1:
                    dve.wait_ge(f_ps, b)
                step(tt(th, th, pC[:, 128:128 + T].unsqueeze(1).to_broadcast([128, M0, T]), ALU.mult))
                ts(hq, th, MAGIC, MAGIC, ALU.add, ALU.subtract).then_inc(hq_ready, 1)

            @batch
            def t_x2(b):
                dve.wait_ge(f_ps, b + 1)
                if b >= 1:
                    dve.wait_ge(x3_ready, b)
                dve.scalar_tensor_tensor(x2[:, :], pC[0:T, 0:D], tiny[:, 11:12], x1[:, :], ALU.mult, ALU.add)\
                   .then_inc(x2_ready, 1)

            @batch
            def u_stats(b):
                dve.wait_ge(x2_ready, b + 1)
                ln_stats(x2[:, :], 2)

            @batch
            def u_ln(b):
                if b >= 1:
                    dve.wait_ge(xn3T_ps, b)
                    dve.wait_ge(xn3_stored, 16 * b)
                ln(x2[:, :], 2, b, xm[:, :]).then_inc(xn2_ready, 1)

            @batch
            def u_sc(b):
                dve.wait_ge(sc_ps, b + 1)
                dve.wait_ge(msk_loaded, 16 * (b + 1))
                if b >= 1:
                    dve.wait_ge(e_ready, b)
                step(tt(scr, pU[0:T, 0:L], msk[:, 0, :], ALU.mult))
                step(tt(scr, scr, msk[:, 1, :], ALU.add))
                step(dve.tensor_reduce(tiny[:, 6:7], scr, X, ALU.max))
                ts(tiny[:, 8:9], tiny[:, 6:7], -1.0, None, ALU.mult, ALU.bypass).then_inc(sc_done, 1)

            @batch
            def u_al(b):
                dve.wait_ge(e_ready, b + 1)
                step(dve.reciprocal(tiny[:, 7:8], tiny[:, 9:10]))
                if b >= 1:
                    dve.wait_ge(alT_ps, b)
                dve.scalar_tensor_tensor(al[:, :], al[:, :], tiny[:, 7:8], msk[:, 2, :], ALU.mult, ALU.mult)\
                   .then_inc(al_ready, 1)

            @batch
            def u_stats3(b):
                dve.wait_ge(x3_ready, b + 1)
                ln_stats(x3, 3)

            @batch
            def u_ln3(b):
                ln(x3, 3, b, xm[:, :]).then_inc(xn3_ready, 1)

            @batch
            def u_lg(b):
                dve.wait_ge(r_ps, b + 1)
                tt(lgall[:, b, :], pU[0:T, 256:256 + NE], br_b[:, :], ALU.add).then_inc(lg_ready, 1)

            for i in range(-1, B + 3):
                t_x2(i - 3)
                u_stats(i - 3)
                u_ln(i - 3)
                t_norm(i - 2)
                w_quant(i - 1, 1, 2)
                u_sc(i - 3)
                for n in range(0, 3):
                    a_max(i - 1, n)
                t_x1(i - 2)
                for n in range(3, 6):
                    a_max(i - 1, n)
                for n in range(0, 3):
                    w_sum(i, n)
                w_mask(i)
                t_xq(i - 2)
                w_bo(i - 1)
                w_quant(i, 0, 0)
                u_al(i - 3)
                for n in range(6, 10):
                    a_max(i - 1, n)
                w_quant(i, 0, 1)
                w_quant(i, 0, 2)
                a_max(i - 1, 10)
                t_h(i - 2, 0)
                for n in range(11, 14):
                    a_max(i - 1, n)
                w_quant(i, 1, 0)
                a_max(i - 1, 14)
                a_max(i - 1, 15)
                a_neg(i - 1)
                t_h(i - 2, 1)
                a_nmT(i - 1)
                t_conv(i - 2, 0)
                t_conv(i - 2, 1)
                t_silu(i - 2, 0)
                p_q(i)
                t_silu(i - 2, 1)
                t_amax(i - 2)
                u_stats3(i - 3)
                t_q2(i - 2)
                p_stats(i + 1)
                u_ln3(i - 3)
                t_hq(i - 2)
                p_ln(i + 1)
                w_quant(i, 1, 1)
                u_lg(i - 3)
            dve.wait_ge(m_iota, 1)
            step(ts(earlier, earlier, 0.0, None, ALU.is_gt, ALU.bypass))
            step(ts(erow, ecol, float(NE), -float(NE), ALU.is_ge, ALU.mult))
            step(tt(erow, ecol, erow, ALU.add))
            step(ts(ecol, ecol, 2.0 * NE, -float(NE), ALU.is_ge, ALU.mult))
            step(tt(erow, ecol, erow, ALU.add))
            dve.wait_ge(lg_ready, B)

            def bc(x):
                return x.unsqueeze(2).to_broadcast([T, B, NE])

            step(dve.tensor_reduce(m_g[:, 0, :], lgall[:, :, :], X, ALU.max))
            step(tt(oh, lgall[:, :, :], bc(m_g[:, 0, :]), ALU.is_equal))
            step(tt(oh, oh, w8, ALU.mult))
            step(dve.tensor_reduce(m_g[:, 1, :], oh, X, ALU.max))
            step(tt(oh, oh, bc(m_g[:, 1, :]), ALU.is_equal))
            dve.tensor_copy(ohb, oh).then_inc(m_oh, 1)
            tt(m_d3, lgall[:, :, :], bc(m_g[:, 0, :]), ALU.subtract).then_inc(m_d, 1)
            dve.wait_ge(cnt_ps, 1)
            step(tt(cmp1, pC[:, B * NE:B * NE + NE].unsqueeze(2).to_broadcast([128, NE, NB - NE + 1]), thr, ALU.is_gt))
            step(dve.tensor_reduce(nblk, cmp1, X, ALU.add))
            step(tt(cmp3, earlier, nblk.unsqueeze(1).to_broadcast([128, NE, NE]), ALU.mult))
            step(dve.tensor_reduce(bs, cmp3, X, ALU.add))
            step(dve.scalar_tensor_tensor(base, bs[0:T, :].unsqueeze(1).to_broadcast([T, B, NE]), 128.0,
                                          pC[0:T, 0:B * NE].rearrange("p (b e) -> p b e", e=NE), ALU.mult, ALU.add))
            step(tt(base, base, oh, ALU.mult))
            step(dve.tensor_reduce(m_g[:, 4, :], base, X, ALU.add))
            step(dve.tensor_copy(mi[:, :], m_g[:, 4, :]))
            dve.wait_ge(m_e, 1)
            step(dve.tensor_reduce(m_g[:, 2, :], m_e3, X, ALU.add))
            dve.reciprocal(xall[:, :, XW - 2], m_g[:, 2, :]).then_inc(m_slots, 1)
            step(tt(cmp2, jix, bs[:, 1:NE].unsqueeze(1).to_broadcast([128, NB, NE - 1]), ALU.is_ge))
            tt(ebj[:, NB:NB + 1], bs[:, NE - 1:NE], nblk[:, NE - 1:NE], ALU.add)
            step(dve.tensor_reduce(ebj[:, 0:NB], cmp2, X, ALU.add))
            dve.tensor_copy(ebi[:, :], ebj[0:1, :])
            step(ts(sel, ebj[0:3 * NE, 0:NB], erow, None, ALU.is_equal, ALU.bypass))
            dve.tensor_copy(selx, sel.unsqueeze(2).to_broadcast([3 * NE, NB, 128])).then_inc(sel_ready, 1)

            def e_xT(j):
                dve.wait_ge(xT_ps, j + 1)
                if j >= 2:
                    dve.wait_ge(h1_ps, 2 * (j - 1))
                dve.tensor_copy(xsT[:, j % 2], pC[:, 0:D].rearrange("p (k t) -> p k t", k=DC)).then_inc(xT_sb, 1)

            def e_tokens(j):
                dve.wait_ge(xs_loaded[j % 4], 16 * (j // 4 + 1))
                step(ts(rid[:, j % 4:j % 4 + 1], xsb[:, j % 4, XW - 1:XW], -1.0, float(NT), ALU.mult, ALU.add))
                dve.tensor_copy(tid[:, j % 4:j % 4 + 1], rid[:, j % 4:j % 4 + 1])

            def e_hT(j):
                for n in range(2):
                    dve.wait_ge(hT_ps, 2 * j + n + 1)
                    if j >= 2:
                        dve.wait_ge(y_ps, j - 1)
                    dve.tensor_copy(hxT[:, j % 2, 4 * n:4 * n + 4, :].rearrange("p f t -> p (f t)"), pAB[:, n, :])\
                       .then_inc(hT_sb, 1)

            def e_y(j):
                dve.wait_ge(y_ps, j + 1)
                if j >= 2:
                    dve.wait_ge(y_stored, 16 * (j - 1))
                dve.scalar_tensor_tensor(ysb[:, j % 2, :], pO[:, 0:D], xsb[:, j % 4, XW - 2:XW - 1], xsb[:, j % 4, D:2 * D],
                                         ALU.mult, ALU.add).then_inc(y_sb, 1)

            dve.wait_ge(sel_ready, 1)
            e_xT(0)
            e_xT(1)
            total = blocks(dve)
            for j in range(NB):
                if j + 2 < NB:
                    with filled_block(dve, total, j + 1):
                        e_xT(j + 2)
                with filled_block(dve, total, j):
                    e_tokens(j)
                    e_hT(j)
                    e_y(j)


_INS = ['x', 'ctx_1024', 'condB_tau', 'fside_BxS2_0', 'condB_pt', '_lenS2', 'L0_xcond_Wq', 'L0_xcond_bq', 'L0_xcond_Wk',
        'L0_xcond_bk', 'L0_xcond_Wv', 'L0_xcond_bv', 'L0_xcond_Wo', 'L0_xcond_bo', 'L0_ffn_w1', 'L0_ffn_conv_w',
        'L0_ffn_conv_b', 'L0_ffn_w2', 'L1_xcond_W_a', 'L1_xcond_W_c', 'L1_ffn_W1', 'L1_ffn_b1', 'L1_ffn_W2', 'L1_ffn_b2',
        'L1_ffn_Wr', 'L1_ffn_br']


def kernel(**inputs):
    import numpy as _np
    import concourse.bacc as _bacc
    from concourse import mybir as _mybir
    from concourse.bass_utils import run_bass_kernel_spmd as _run

    nc = _bacc.Bacc("TRN2", target_bir_lowering=False, num_devices=1)
    arrays, aps = {}, {}
    for name in _INS:
        a = _np.ascontiguousarray(inputs[name])
        arrays[f"in_{name}"] = a
        aps[name] = nc.dram_tensor(f"in_{name}", a.shape, _mybir.dt.from_np(a.dtype), kind="ExternalInput").ap()
    out = nc.dram_tensor("out_x", inputs["x"].shape, _mybir.dt.float32, kind="ExternalOutput").ap()
    pixart_block(nc, aps, out)
    r = _run(nc, [arrays], core_ids=[0])
    return r.results[0]["out_x"]
```
